# Optimizing a Trainium2 kernel written in Bass

```python
import numpy as np
import jax
import jax.numpy as jnp

def _softmax(x, axis=-1):
    return jax.nn.softmax(x, axis=axis)

def _gelu(x):
    return jax.nn.gelu(x, approximate=True)

def _silu(x):
    return jax.nn.silu(x)

def _sigmoid(x):
    return jax.nn.sigmoid(x)

def _layernorm(x, axis=-1, eps=1e-05):
    m = jnp.mean(x, axis=axis, keepdims=True)
    v = jnp.var(x, axis=axis, keepdims=True)
    return (x - m) / jnp.sqrt(v + eps)

def _scatter_add(tgt, idx, src, axis=0):
    return tgt.at[idx].add(src)

def _segment_sum(src, seg, n):
    return jax.ops.segment_sum(src, seg, n)
kernel_name = 'mk_perceiver_d1_seqx_r4_c3108f'

def setup_inputs(seed: int=0):
    np.random.seed(seed)
    _w = jnp.asarray

    def _rec_inputs():
        import jax
        import jax.numpy as jnp
        _rk = jax.random.key(seed)
        x = -0.0005146 + 1 * jax.random.normal(jax.random.fold_in(_rk, 1), (1, 256, 256), jnp.float32)
        _lenS = 256 - jax.random.randint(jax.random.fold_in(_rk, 7), (1,), 0, max(1, 256 // 4) + 1, jnp.int32)
        _lenS2 = 4096 - jax.random.randint(jax.random.fold_in(_rk, 8), (1,), 0, max(1, 4096 // 4) + 1, jnp.int32)
        _ctx_768P = jax.random.normal(jax.random.fold_in(_rk, 11), (1, 16, 192), jnp.float32)
        _ctx_768c = jax.random.dirichlet(jax.random.fold_in(_rk, 511), 0.3 * jnp.ones((16,), jnp.float32), (1, 4096))
        _ctx_768t = jnp.einsum('bsk,bkd->bsd', _ctx_768c, _ctx_768P)
        _ctx_768t = _ctx_768t * jax.lax.rsqrt(jnp.mean(jnp.square(_ctx_768t)) + 1e-12) * 0.953939
        ctx_768 = -0.00040386 + 0.999972 * (_ctx_768t + 0.3 * jax.random.normal(jax.random.fold_in(_rk, 611), (1, 4096, 192), jnp.float32))
        _validS = jnp.arange(256)[None, :] < _lenS[:, None]
        _validS2 = jnp.arange(4096)[None, :] < _lenS2[:, None]
        _causal = jnp.tril(jnp.ones((256, 256), dtype=bool))
        mask_BxS2_bk0 = jnp.logical_not(jnp.broadcast_to(_validS2[:, :], (1, 4096)))
        return (x, ctx_768, mask_BxS2_bk0)
    x, ctx_768, mask_BxS2_bk0 = _rec_inputs()

    def _L0_xattn_setup():
        import jax, jax.numpy as jnp
        import numpy as np
        DIM_IN, DIM_LAT, DIM_HEAD = (192, 256, 64)
        INNER = max(DIM_LAT, DIM_IN)
        HEADS = INNER // DIM_HEAD
        SCALE = DIM_HEAD ** (-0.5)
        RMS_EPS = 1e-08
        LN_EPS = 1e-05

        def layernorm(x, g, b):
            mu = jnp.mean(x, axis=-1, keepdims=True)
            var = jnp.mean((x - mu) ** 2, axis=-1, keepdims=True)
            return (x - mu) * jax.lax.rsqrt(var + LN_EPS) * g + b

        def rmsnorm(x, gamma):
            norm = jnp.sqrt(jnp.sum(x * x, axis=-1, keepdims=True)) * x.shape[-1] ** (-0.5)
            return x / jnp.maximum(norm, RMS_EPS) * gamma
        key = jax.random.key(seed)
        ks = jax.random.split(key, 12)
        b, n, m = (4, 1024, 128)
        x = jax.random.normal(ks[0], (b, n, DIM_IN), jnp.float32)
        latents = jax.random.normal(ks[1], (b, m, DIM_LAT), jnp.float32)
        mask = jax.random.randint(ks[2], (b, n), 0, 2).astype(bool)
        s = lambda k, sh, fan: jax.random.normal(k, sh, jnp.float32) * fan ** (-0.5)
        return {'x': x, 'latents': latents, 'mask': mask, 'ln_x_g': jnp.ones((DIM_IN,), jnp.float32), 'ln_x_b': jnp.zeros((DIM_IN,), jnp.float32), 'ln_l_g': jnp.ones((DIM_LAT,), jnp.float32), 'ln_l_b': jnp.zeros((DIM_LAT,), jnp.float32), 'qn_g': jnp.ones((DIM_HEAD,), jnp.float32), 'kn_g': jnp.ones((DIM_HEAD,), jnp.float32), 'Wq': s(ks[3], (INNER, DIM_LAT), DIM_LAT), 'Wkv': s(ks[4], (2 * INNER, DIM_IN), DIM_IN), 'Wlkv': s(ks[5], (2 * INNER, DIM_LAT), DIM_LAT), 'Wo': s(ks[6], (DIM_LAT, INNER), INNER), 'bo': jnp.zeros((DIM_LAT,), jnp.float32)}
    _L0_xattn_all = _L0_xattn_setup()
    _L0_xattn_in = {k: v for k, v in _L0_xattn_all.items() if k in ('ln_x_g', 'ln_x_b', 'ln_l_g', 'ln_l_b', 'qn_g', 'kn_g', 'Wq', 'Wkv', 'Wlkv', 'Wo', 'bo')}
    del _L0_xattn_all

    def _L0_attn_setup():
        import jax, jax.numpy as jnp
        import numpy as np
        EPS = 1e-05

        def layernorm(x, g, b):
            m = jnp.mean(x, axis=-1, keepdims=True)
            v = jnp.mean(jnp.square(x - m), axis=-1, keepdims=True)
            return (x - m) * jax.lax.rsqrt(v + EPS) * g + b

        def delta(x, gates_w, gates_b, lr_w, lr_b, out_w, out_b):
            N, T, C = x.shape
            qkv = x @ gates_w + gates_b
            q, k, v = jnp.split(qkv, 3, axis=-1)
            lr = x @ lr_w + lr_b
            k = k / jnp.linalg.norm(k, axis=-1, keepdims=True)
            K = jnp.tril(jnp.einsum('ntc,nsc->nts', k, k), k=-1)
            A = K + jnp.eye(T, dtype=x.dtype)
            u = jax.scipy.linalg.solve_triangular(A, v, lower=True)
            score = jnp.einsum('nsk,ntk->nst', q, k)
            y = jnp.einsum('nst,ntv->nsv', score, lr * u)
            return y @ out_w + out_b

        def mlp(x, w1, b1, w2, b2):
            return jax.nn.relu(x @ w1 + b1) @ w2 + b2
        N, T, C = (8, 512, 256)
        key = jax.random.key(seed)
        ks = jax.random.split(key, 16)
        s = 0.02
        return {'x': jax.random.normal(ks[0], (N, T, C), jnp.float32), 'dn_g': jnp.ones((C,), jnp.float32), 'dn_b': jnp.zeros((C,), jnp.float32), 'gates_w': jax.random.normal(ks[1], (C, 3 * C), jnp.float32) * s, 'gates_b': jnp.zeros((3 * C,), jnp.float32), 'lr_w': jax.random.normal(ks[2], (C, 1), jnp.float32) * s, 'lr_b': jnp.zeros((1,), jnp.float32), 'out_w': jax.random.normal(ks[3], (C, C), jnp.float32) * s, 'out_b': jnp.zeros((C,), jnp.float32), 'mn_g': jnp.ones((C,), jnp.float32), 'mn_b': jnp.zeros((C,), jnp.float32), 'w1': jax.random.normal(ks[4], (C, C), jnp.float32) * s, 'b1': jnp.zeros((C,), jnp.float32), 'w2': jax.random.normal(ks[5], (C, C), jnp.float32) * s, 'b2': jnp.zeros((C,), jnp.float32)}
    _L0_attn_all = _L0_attn_setup()
    _L0_attn_in = {k: v for k, v in _L0_attn_all.items() if k in ('dn_g', 'dn_b', 'gates_w', 'gates_b', 'lr_w', 'lr_b', 'out_w', 'out_b', 'mn_g', 'mn_b', 'w1', 'b1', 'w2', 'b2')}
    del _L0_attn_all

    def _L0_ffn_setup():
        import jax, jax.numpy as jnp
        import numpy as np
        B, L, H, E, I = (4, 512, 256, 8, 1024)
        S = B * L
        CAP_FACTOR_EVAL = 2.0
        MIN_CAP = 4
        _cap = int(np.floor(CAP_FACTOR_EVAL * S / E))
        _cap += _cap % 2
        CAPACITY = max(_cap, MIN_CAP)

        def _layer_norm(x, g, b, eps=1e-05):
            mu = x.mean(-1, keepdims=True)
            var = ((x - mu) ** 2).mean(-1, keepdims=True)
            return (x - mu) * jax.lax.rsqrt(var + eps) * g + b
        key = jax.random.key(seed)
        ks = jax.random.split(key, 8)
        gate_std = float(np.sqrt(0.1 / H))
        return {'inputs': jax.random.normal(ks[0], (B, L, H), jnp.float32), 'gate_weight': jax.random.normal(ks[1], (E, H), jnp.float32) * gate_std, 'ln_gamma': jnp.ones((H,), jnp.float32), 'ln_beta': jnp.zeros((H,), jnp.float32), 'wi': jax.random.normal(ks[2], (E, H, I), jnp.float32) * float(1.0 / np.sqrt(H)), 'wo': jax.random.normal(ks[3], (E, I, H), jnp.float32) * float(1.0 / np.sqrt(I)), 'conf_w1': jax.random.normal(ks[4], (H // 2, H), jnp.float32) * float(np.sqrt(2.0 / (H + H // 2))), 'conf_b1': -jnp.ones((H // 2,), jnp.float32), 'conf_w2': jax.random.normal(ks[5], (1, H // 2), jnp.float32) * float(np.sqrt(2.0 / (1 + H // 2))), 'conf_b2': -jnp.ones((1,), jnp.float32), 'comp_w': jax.random.normal(ks[6], (1, H), jnp.float32) * float(1.0 / np.sqrt(H)), 'comp_b': jnp.zeros((1,), jnp.float32)}
    _L0_ffn_all = _L0_ffn_setup()
    _L0_ffn_in = {k: v for k, v in _L0_ffn_all.items() if k in ('gate_weight', 'ln_gamma', 'ln_beta', 'wi', 'wo', 'conf_w1', 'conf_b1', 'conf_w2', 'conf_b2', 'comp_w', 'comp_b')}
    del _L0_ffn_all
    return {'x': x, 'ctx_768': ctx_768, 'mask_BxS2_bk0': mask_BxS2_bk0, 'L0_xattn_ln_x_g': _L0_xattn_in['ln_x_g'], 'L0_xattn_ln_x_b': _L0_xattn_in['ln_x_b'], 'L0_xattn_ln_l_g': _L0_xattn_in['ln_l_g'], 'L0_xattn_ln_l_b': _L0_xattn_in['ln_l_b'], 'L0_xattn_qn_g': _L0_xattn_in['qn_g'], 'L0_xattn_kn_g': _L0_xattn_in['kn_g'], 'L0_xattn_Wq': _L0_xattn_in['Wq'], 'L0_xattn_Wkv': _L0_xattn_in['Wkv'], 'L0_xattn_Wlkv': _L0_xattn_in['Wlkv'], 'L0_xattn_Wo': _L0_xattn_in['Wo'], 'L0_xattn_bo': _L0_xattn_in['bo'], 'L0_attn_dn_g': _L0_attn_in['dn_g'], 'L0_attn_dn_b': _L0_attn_in['dn_b'], 'L0_attn_gates_w': _L0_attn_in['gates_w'], 'L0_attn_gates_b': _L0_attn_in['gates_b'], 'L0_attn_lr_w': _L0_attn_in['lr_w'], 'L0_attn_lr_b': _L0_attn_in['lr_b'], 'L0_attn_out_w': _L0_attn_in['out_w'], 'L0_attn_out_b': _L0_attn_in['out_b'], 'L0_attn_mn_g': _L0_attn_in['mn_g'], 'L0_attn_mn_b': _L0_attn_in['mn_b'], 'L0_attn_w1': _L0_attn_in['w1'], 'L0_attn_b1': _L0_attn_in['b1'], 'L0_attn_w2': _L0_attn_in['w2'], 'L0_attn_b2': _L0_attn_in['b2'], 'L0_ffn_gate_weight': _L0_ffn_in['gate_weight'], 'L0_ffn_ln_gamma': _L0_ffn_in['ln_gamma'], 'L0_ffn_ln_beta': _L0_ffn_in['ln_beta'], 'L0_ffn_wi': _L0_ffn_in['wi'], 'L0_ffn_wo': _L0_ffn_in['wo'], 'L0_ffn_conf_w1': _L0_ffn_in['conf_w1'], 'L0_ffn_conf_b1': _L0_ffn_in['conf_b1'], 'L0_ffn_conf_w2': _L0_ffn_in['conf_w2'], 'L0_ffn_conf_b2': _L0_ffn_in['conf_b2'], 'L0_ffn_comp_w': _L0_ffn_in['comp_w'], 'L0_ffn_comp_b': _L0_ffn_in['comp_b']}

def reference(x, ctx_768, mask_BxS2_bk0, L0_xattn_ln_x_g, L0_xattn_ln_x_b, L0_xattn_ln_l_g, L0_xattn_ln_l_b, L0_xattn_qn_g, L0_xattn_kn_g, L0_xattn_Wq, L0_xattn_Wkv, L0_xattn_Wlkv, L0_xattn_Wo, L0_xattn_bo, L0_attn_dn_g, L0_attn_dn_b, L0_attn_gates_w, L0_attn_gates_b, L0_attn_lr_w, L0_attn_lr_b, L0_attn_out_w, L0_attn_out_b, L0_attn_mn_g, L0_attn_mn_b, L0_attn_w1, L0_attn_b1, L0_attn_w2, L0_attn_b2, L0_ffn_gate_weight, L0_ffn_ln_gamma, L0_ffn_ln_beta, L0_ffn_wi, L0_ffn_wo, L0_ffn_conf_w1, L0_ffn_conf_b1, L0_ffn_conf_w2, L0_ffn_conf_b2, L0_ffn_comp_w, L0_ffn_comp_b):
    import jax
    import jax.numpy as jnp

    def _L0_xattn_ref(x, latents, mask, ln_x_g, ln_x_b, ln_l_g, ln_l_b, qn_g, kn_g, Wq, Wkv, Wlkv, Wo, bo):
        import jax, jax.numpy as jnp
        import numpy as np
        DIM_IN, DIM_LAT, DIM_HEAD = (192, 256, 64)
        INNER = max(DIM_LAT, DIM_IN)
        HEADS = INNER // DIM_HEAD
        SCALE = DIM_HEAD ** (-0.5)
        RMS_EPS = 1e-08
        LN_EPS = 1e-05

        def layernorm(x, g, b):
            mu = jnp.mean(x, axis=-1, keepdims=True)
            var = jnp.mean((x - mu) ** 2, axis=-1, keepdims=True)
            return (x - mu) * jax.lax.rsqrt(var + LN_EPS) * g + b

        def rmsnorm(x, gamma):
            norm = jnp.sqrt(jnp.sum(x * x, axis=-1, keepdims=True)) * x.shape[-1] ** (-0.5)
            return x / jnp.maximum(norm, RMS_EPS) * gamma
        b, n, _ = x.shape
        m = latents.shape[1]
        xn = layernorm(x, ln_x_g, ln_x_b)
        ln = layernorm(latents, ln_l_g, ln_l_b)
        q = ln @ Wq.T
        kv = jnp.concatenate([xn @ Wkv.T, ln @ Wlkv.T], axis=1)
        k, v = (kv[..., :INNER], kv[..., INNER:])
        split_heads = lambda t: t.reshape(t.shape[0], t.shape[1], HEADS, DIM_HEAD).transpose(0, 2, 1, 3)
        q, k, v = (split_heads(q), split_heads(k), split_heads(v))
        qn = rmsnorm(q, qn_g) * SCALE
        kn = rmsnorm(k, kn_g)
        attn = jnp.einsum('bhid,bhjd->bhij', qn, kn)
        full_mask = jnp.pad(mask, ((0, 0), (0, m)), constant_values=True)
        attn = jnp.where(full_mask[:, None, None, :], attn, -jnp.finfo(attn.dtype).max)
        attn = jax.nn.softmax(attn, axis=-1)
        out = jnp.einsum('bhij,bhjd->bhid', attn, v)
        out = out.transpose(0, 2, 1, 3).reshape(b, m, INNER)
        return out @ Wo.T + bo

    def _L0_attn_ref(x, dn_g, dn_b, gates_w, gates_b, lr_w, lr_b, out_w, out_b, mn_g, mn_b, w1, b1, w2, b2):
        import jax, jax.numpy as jnp
        import numpy as np
        EPS = 1e-05

        def layernorm(x, g, b):
            m = jnp.mean(x, axis=-1, keepdims=True)
            v = jnp.mean(jnp.square(x - m), axis=-1, keepdims=True)
            return (x - m) * jax.lax.rsqrt(v + EPS) * g + b

        def delta(x, gates_w, gates_b, lr_w, lr_b, out_w, out_b):
            N, T, C = x.shape
            qkv = x @ gates_w + gates_b
            q, k, v = jnp.split(qkv, 3, axis=-1)
            lr = x @ lr_w + lr_b
            k = k / jnp.linalg.norm(k, axis=-1, keepdims=True)
            K = jnp.tril(jnp.einsum('ntc,nsc->nts', k, k), k=-1)
            A = K + jnp.eye(T, dtype=x.dtype)
            u = jax.scipy.linalg.solve_triangular(A, v, lower=True)
            score = jnp.einsum('nsk,ntk->nst', q, k)
            y = jnp.einsum('nst,ntv->nsv', score, lr * u)
            return y @ out_w + out_b

        def mlp(x, w1, b1, w2, b2):
            return jax.nn.relu(x @ w1 + b1) @ w2 + b2
        x = x + delta(layernorm(x, dn_g, dn_b), gates_w, gates_b, lr_w, lr_b, out_w, out_b)
        x = x + mlp(layernorm(x, mn_g, mn_b), w1, b1, w2, b2)
        return x

    def _L0_ffn_ref(inputs, gate_weight, ln_gamma, ln_beta, wi, wo, conf_w1, conf_b1, conf_w2, conf_b2, comp_w, comp_b):
        import jax, jax.numpy as jnp
        import numpy as np
        B, L, H, E, I = (4, 512, 256, 8, 1024)
        S = B * L
        CAP_FACTOR_EVAL = 2.0
        MIN_CAP = 4
        _cap = int(np.floor(CAP_FACTOR_EVAL * S / E))
        _cap += _cap % 2
        CAPACITY = max(_cap, MIN_CAP)

        def _layer_norm(x, g, b, eps=1e-05):
            mu = x.mean(-1, keepdims=True)
            var = ((x - mu) ** 2).mean(-1, keepdims=True)
            return (x - mu) * jax.lax.rsqrt(var + eps) * g + b
        tokens = inputs.reshape(-1, H)
        residual = tokens
        tokens = _layer_norm(tokens, ln_gamma, ln_beta)
        complexity_score = jax.nn.sigmoid(tokens @ comp_w.T + comp_b).mean()
        hdn = jax.nn.relu(tokens @ conf_w1.T + conf_b1)
        confidence_score = jax.nn.sigmoid(hdn @ conf_w2.T + conf_b2).mean()
        logits = tokens.astype(jnp.float32) @ gate_weight.astype(jnp.float32).T
        probs = jax.nn.softmax(logits, axis=-1)
        top1 = jnp.argmax(logits, axis=-1)
        onehot = jax.nn.one_hot(top1, E, dtype=jnp.int32)
        rank_e = jnp.cumsum(onehot, axis=0) - onehot
        rank = jnp.sum(rank_e * onehot, axis=-1)
        keep = rank < CAPACITY
        weight = jnp.take_along_axis(probs, top1[:, None], axis=-1)[:, 0]
        weight = (weight * keep).astype(tokens.dtype)
        slot = jnp.where(keep, rank, 0)
        dispatch = jnp.zeros((E, CAPACITY, H), tokens.dtype)
        dispatch = dispatch.at[top1, slot].add(tokens * keep[:, None])
        h = jax.nn.gelu(jnp.einsum('ech,ehi->eci', dispatch, wi), approximate=False)
        expert_out = jnp.einsum('eci,eih->ech', h, wo)
        combined = weight[:, None] * expert_out[top1, slot]
        out = (residual + combined).reshape(inputs.shape)
        return out
    x = x + _L0_xattn_ref(ctx_768, _layernorm(x, axis=-1), mask_BxS2_bk0, L0_xattn_ln_x_g, L0_xattn_ln_x_b, L0_xattn_ln_l_g, L0_xattn_ln_l_b, L0_xattn_qn_g, L0_xattn_kn_g, L0_xattn_Wq, L0_xattn_Wkv, L0_xattn_Wlkv, L0_xattn_Wo, L0_xattn_bo)
    x = x + _L0_attn_ref(_layernorm(x, axis=-1), L0_attn_dn_g, L0_attn_dn_b, L0_attn_gates_w, L0_attn_gates_b, L0_attn_lr_w, L0_attn_lr_b, L0_attn_out_w, L0_attn_out_b, L0_attn_mn_g, L0_attn_mn_b, L0_attn_w1, L0_attn_b1, L0_attn_w2, L0_attn_b2)
    x = x + _L0_ffn_ref(_layernorm(x, axis=-1), L0_ffn_gate_weight, L0_ffn_ln_gamma, L0_ffn_ln_beta, L0_ffn_wi, L0_ffn_wo, L0_ffn_conf_w1, L0_ffn_conf_b1, L0_ffn_conf_w2, L0_ffn_conf_b2, L0_ffn_comp_w, L0_ffn_comp_b)
    return x

_drawn_inputs = setup_inputs


def setup_inputs(seed=0):
    import zlib

    import numpy as np

    out = dict(_drawn_inputs(seed))
    spreads = {'L0_xattn_ln_x_g': (1.0, 0.2),
     'L0_xattn_ln_x_b': (0.0, 0.1),
     'L0_xattn_ln_l_g': (1.0, 0.2),
     'L0_xattn_ln_l_b': (0.0, 0.1),
     'L0_xattn_qn_g': (1.0, 0.599),
     'L0_xattn_kn_g': (1.0, 0.6),
     'L0_xattn_bo': (0.0, 0.1),
     'L0_attn_dn_g': (1.0, 0.2),
     'L0_attn_dn_b': (0.0, 0.603),
     'L0_attn_gates_b': (0.0, 0.1),
     'L0_attn_out_b': (0.0, 0.1),
     'L0_attn_mn_g': (1.0, 0.6),
     'L0_attn_mn_b': (0.0, 2.0),
     'L0_attn_b1': (0.0, 0.788),
     'L0_attn_b2': (0.0, 0.1),
     'L0_ffn_ln_gamma': (1.0, 0.6),
     'L0_ffn_ln_beta': (0.0, 0.61),
     'L0_ffn_conf_b1': (-1.0, 0.2)}
    factors = {}
    for name, (base, spread) in spreads.items():
        noise = np.random.default_rng([zlib.crc32(name.encode()), seed]).standard_normal(out[name].shape)
        drawn = base * np.exp(spread * noise) if base else spread * noise
        out[name] = jnp.asarray(drawn.astype(out[name].dtype))
    for name, factor in factors.items():
        out[name] = (out[name] * factor).astype(out[name].dtype)
    return out
```

```python
from contextlib import ExitStack

import concourse.bass as bass
from concourse import mybir

F32 = mybir.dt.float32
F16 = mybir.dt.float16
I32 = mybir.dt.int32
U8 = mybir.dt.uint8
ALU = mybir.AluOpType
ACT = mybir.ActivationFunctionType
AX = mybir.AxisListType

P = 128
T = 256
C = 256
H2 = T // P
NCTX = 4096
DC = 192
CT = DC // 2
HEADS = 4
DH = 64
NKEY = NCTX + T
PAIR = 2 * P
NCP = NCTX // PAIR
NPAIR = NKEY // PAIR
KR = DH + 2
LN_EPS = 1e-5
RMS_EPS = 1e-8
RANGE = 8.0
BIG = 30000.0
E = 8
I = 1024
IT = I // P
W = 64
NX = (T - 1) // W
NW = E + NX
SLOTS = NW * W
NSG = (SLOTS + P - 1) // P
NRES = 3
assert NX <= NRES

ROW = {}
_at = 0
for _n, _w in (("ln_l_g", C), ("ln_l_b", C), ("qn_g", DH), ("kn_g", DH), ("bo", C), ("dn_g", C), ("dn_b", C),
               ("gates_bk", C), ("gates_bv", C), ("lr_b", 1), ("out_b", C), ("mn_g", C), ("mn_b", C), ("b2", C),
               ("ffn_g", C), ("ffn_b", C)):
    ROW[_n] = (_at, _at + _w)
    _at += _w
NROW = _at
NLEV = 7
C_ID = (NLEV + 1) * P
C_TRI = C_ID + P
C_IOTA = C_TRI + P
NCONST = C_IOTA + SLOTS


def perceiver_layer(nc, x, ctx, ctxT, mask, wkvT, wqT, wlkvT, woT, gates, lrw, outw, w1, w2, gateT, wi, wo,
                    rows, cols, cols_ctx, consts, key_ones, out):
    with ExitStack() as stack:
        def sb(name, shape, dt=F32):
            return stack.enter_context(nc.sbuf_tensor(name, shape, dt))

        sems = {}

        def sem(name):
            if name not in sems:
                sems[name] = stack.enter_context(nc.semaphore(name))
            return sems[name]

        bank = [stack.enter_context(nc.psum_tensor(f"bank{i}", [P, 512], F32))[:] for i in range(8)]

        def region(tensor, at=0):
            pos = [at]

            def take(cols, dt=F32, parts=P, **dims):
                n = cols if dt in (F32, I32) else cols // 2
                a = tensor[0:parts, pos[0]:pos[0] + n]
                pos[0] += n
                assert pos[0] <= tensor.shape[1], (pos, tensor.shape)
                return a if dt == F32 else a.bitcast(dt)
            return take, pos

        def v(ap, spec, /, **dims):
            return ap.rearrange(spec, **dims)

        def two(a):
            return a.rearrange("p (a b) -> p a b", a=2)

        rowv = sb("rowv", [P, NROW])
        colv = sb("colv", [P, 4])
        cst = sb("cst", [P, NCONST])
        ident = cst[:, C_ID:C_ID + P]
        tri = cst[:, C_TRI:C_TRI + P]
        iota = cst[:, C_IOTA:C_IOTA + SLOTS]
        lower1 = cst[:, 0:P]

        def upper(n):
            return cst[:, (1 + n) * P:(2 + n) * P]

        id16 = sb("id16", [P, P], F16)
        ones = sb("ones", [P, P])
        xbuf = sb("xbuf", [P, H2, C])
        var_eps = sb("var_eps", [P, 16])
        rstd = sb("rstd", [P, 16])
        mhalf = sb("mhalf", [P, 2])
        stats = sb("stats", [P, H2, 6])
        mv = sb("mv", [P, H2, 2])
        eps_c = sb("eps_c", [P, 1])
        gt_sb = sb("gt_sb", [P, 2, E])
        lrw_sb = sb("lrw_sb", [P, 2])
        small = sb("small", [P, 140])
        rt = sb("rt", [P, 232])
        wi_res = sb("wi_res", [P, NRES, H2, I])

        R = sb("R", [P, E * IT * C + (E - NRES) * H2 * I])
        take, _ = region(R)
        keyB = v(take(HEADS * NKEY, F16), "p (h k) -> p h k", h=HEADS)
        keyA = v(take(HEADS * NKEY, F16), "p (h k) -> p h k", h=HEADS)
        val = v(take(2 * NPAIR * HEADS * (DH + 1)), "p (j h d) -> p j h d", h=HEADS, d=DH + 1)
        take, _ = region(R)
        wo_sb = v(take(E * IT * C), "p (e i c) -> p e i c", e=E, i=IT)
        wi_late = v(take((E - NRES) * H2 * I), "p (e k n) -> p e k n", e=E - NRES, k=H2)

        def wi_of(e):
            return wi_res[:, e] if e < NRES else wi_late[:, e - NRES]

        S = sb("S", [P, 13300])
        take, pos = region(S)
        ctxn = v(take(2 * 2 * DC), "p (s t c) -> p s t c", s=2, t=2)
        ctxt = v(take(2 * 2 * PAIR, parts=CT), "p (s k n) -> p s k n", s=2, k=2)
        wc = two(take(2 * 512, parts=CT))
        wq = two(take(2 * C))
        wl = two(take(2 * 512))
        bw = take(512)
        kf = v(take(2 * 512), "p (s t n) -> p s t n", s=2, t=2)
        ksq = take(512)
        kh = v(take(2 * 512), "p (s t n) -> p s t n", s=2, t=2)
        k16 = v(take(2 * 2 * HEADS * P, F16), "p (s t h d) -> p s t h d", s=2, t=2, h=HEADS)
        qT_max = v(take(HEADS * T, F16, parts=KR), "p (h t) -> p h t", h=HEADS)
        qT_exp = v(take(HEADS * T, F16, parts=KR), "p (h t) -> p h t", h=HEADS)
        qT_hh = v(take(HEADS * T, F16), "p (h t) -> p h t", h=HEADS)
        q_exp = v(take(H2 * HEADS * KR, F16), "p (a h d) -> p a h d", a=H2, h=HEADS)
        gqk = take(DH)
        mask8 = take(P // 4)[0:NCTX // P].bitcast(U8)
        mask16 = take(P, F16, parts=NKEY // P)
        pmax = v(take(H2 * NPAIR), "p (a n) -> p a n", a=H2)
        prob = v(take(2 * 512), "p (s n) -> p s n", s=2)
        o_sb = two(take(H2 * C))
        oT = two(take(H2 * T))
        wo_at = two(take(2 * C))
        lat = two(prob[:, 0, :])
        q_hh = v(prob[:, 1, :].bitcast(F16), "p (a h d) -> p a h d", a=H2, h=HEADS)
        q_max = v(v(o_sb, "p a b -> p (a b)")[:, 0:H2 * HEADS * KR // 2].bitcast(F16),
                  "p (a h d) -> p a h d", a=H2, h=HEADS)
        lnT = oT
        cmean = v(kh[0:CT, 0], "p t n -> p (t n)")[:, 0:CT]
        bfree = two(v(kh[0:CT, 1], "p t n -> p (t n)")[:, 0:2 * P])
        take, pos = region(S)
        gw = two(take(2 * 3 * C))
        ow = two(take(2 * C))
        w1_sb = two(take(2 * C))
        w2_sb = two(take(2 * C))
        DELTA_W = pos[0]
        assert DELTA_W <= 8448
        x1 = two(take(H2 * C))
        xx = two(take(H2 * C))
        nrm = two(take(H2 * C))
        nT = two(take(H2 * T))
        knT = two(take(H2 * T))
        qT = two(take(H2 * T))
        kd = two(take(H2 * C))
        vd = two(take(H2 * C))
        score = two(take(H2 * T))
        yT = two(take(H2 * T))
        u = two(take(H2 * C))
        xm = two(take(H2 * C))
        res2 = two(take(H2 * C))
        hm = two(take(H2 * T))
        gram = v(take(3 * P), "p (b n) -> p b n", b=3)
        bT = v(take((NLEV - 1) * 2 * P), "p (l b n) -> p l b n", l=NLEV - 1, b=2)
        X = two(take(2 * P))
        XT = two(take(2 * P))
        T1 = two(take(2 * P))
        lv = two(take(2 * P))
        x2 = xbuf
        xn, tok, tokT, fin, x2xn = xx, nrm, nT, kd, vd
        sel = two(S[:, 0:H2 * SLOTS])
        xs = two(v(bT, "p l b n -> p (l b n)")[:, 0:H2 * SLOTS])

        def span(a, n):
            off = DELTA_W + 512 * a
            return S[:, off:off + n]
        selT = v(span(8, NSG * T), "p (g t) -> p g t", g=NSG)
        hT = v(S[:, pos[0] - 1024:pos[0]], "p (s i w) -> p s i w", s=2, i=IT)
        yT_e = v(span(5, 512), "p (s c w) -> p s c w", s=2, c=2)
        ys = two(span(4, 512))

        colc = small[0:CT, 0:4]
        c_st = v(small[:, 8:32], "p (s t n) -> p s t n", s=2, t=2)
        c_mv = v(small[:, 32:40], "p (s t n) -> p s t n", s=2, t=2)
        sd = two(small[:, 40:44])
        rs = two(small[:, 44:48])
        ss = two(small[:, 48:64])
        ksd = two(small[:, 64:80])
        krm = small[:, 80:88]
        kr = two(small[:, 96:112])
        shift = small[:, 128:130]
        rden = small[:, 130:132]
        var2 = small[:, 132:134]
        lr = small[:, 134:136]

        def row(name):
            return rowv[:, ROW[name][0]:ROW[name][1]]

        def row2(name):
            return row(name).unsqueeze(1).to_broadcast([P, 2, C])

        def per_head(a, n=2 * HEADS):
            return a.unsqueeze(2).to_broadcast([P, n, DH])

        def heads8(a):
            if len(a.shape) == 3:
                a = v(a, "p t n -> p (t n)")
            return v(a, "p (g d) -> p g d", g=2 * HEADS)

        rtake, _ = region(rt)
        logits = two(rtake(2 * E))
        lexp = two(rtake(2 * E))
        cand = two(rtake(2 * E))
        hot = two(rtake(2 * E))
        rk = rtake(3 * E)
        prod = two(rtake(2 * E))
        n_gt = rtake(E)
        over2 = rtake(E)
        over = rtake(E)
        incl = rtake(E)
        offs = rtake(E)
        osel = two(rtake(2 * E))
        xcmp = v(rtake(NX * E), "p (k e) -> p k e", k=NX)
        xid = rtake(NX)
        exid = rtake(NX, I32)
        lmax, nlmax, lsum, wtop, top, rank, win1, win2, win, isx, offt, dtile, dtop, dx, tile_, inpos, slot = (
            rtake(2) for _ in range(17))

        block = stack.enter_context(nc.Block())

        cn = v(ctx[0], "(g t p) c -> g p t c", t=2, p=P)
        cT = v(ctxT, "(k p) (g n) -> g p k n", k=2, g=NCP)

        @block.sync
        def _(sp):
            def load_ctx(g, s):
                sp.dma_start(ctxn[:, s], cn[bass.ds(g, 1)].rearrange("g p t c -> p (g t) c")
                             ).then_inc(sem(f"ctx_in{s}"), 16)
                sp.dma_start(ctxt[:, s], cT[bass.ds(g, 1)].rearrange("g p k n -> p (g k) n")
                             ).then_inc(sem(f"ctx_in{s}"), 16)

            def reload(g, s):
                sp.wait_ge(sem("ctx_stats"), g + 1)
                sp.wait_ge(sem("kv_mm"), g + 1)
                load_ctx(g + 2, s)

            def copy_high(g):
                sp.wait_ge(sem("keyB_done"), g + 1)
                sp.dma_start(keyA[0:DH, :, bass.ds(g * PAIR, PAIR)], keyB[0:DH, :, bass.ds(g * PAIR, PAIR)]
                             ).then_inc(sem("keyA_in"), 16)

            sp.dma_start(xbuf[:], v(x[0], "(h p) c -> p h c", p=P)).then_inc(sem("x_in"), 16)
            sp.dma_start(wc, v(wkvT, "(k p) n -> p k n", k=2)).then_inc(sem("wc_in"), 16)
            sp.dma_start(colc, cols_ctx).then_inc(sem("wc_in"), 16)
            load_ctx(0, 0)
            load_ctx(1, 1)
            sp.dma_start(wq, v(wqT, "(k p) n -> p k n", k=2)).then_inc(sem("wq_in"), 16)
            sp.dma_start(wl, v(wlkvT, "(k p) n -> p k n", k=2)).then_inc(sem("wl_in"), 16)
            sp.dma_start(wo_at, v(woT, "(k p) n -> p k n", k=2)).then_inc(sem("woa_in"), 16)
            for g in range(2):
                reload(g, g)
            with sp.Fori(1, NCP // 2 - 1) as it:
                for s in range(2):
                    reload(2 * it + s, s)
                    copy_high(2 * it + s - 2)
            for g in range(NCP - 4, NPAIR):
                copy_high(g)
            sp.dma_start(gw, v(gates, "(k p) n -> p k n", p=P)).then_inc(sem("gw_in"), 16)
            sp.dma_start(ow, v(outw, "(k p) n -> p k n", p=P)).then_inc(sem("ow_in"), 16)
            sp.dma_start(w1_sb, v(w1, "(k p) n -> p k n", p=P)).then_inc(sem("w1_in"), 16)
            sp.dma_start(w2_sb, v(w2, "(k p) n -> p k n", p=P)).then_inc(sem("w2_in"), 16)
            for e in range(NRES):
                sp.dma_start(wi_of(e), v(wi[e], "(k p) n -> p k n", p=P)).then_inc(sem(f"wi_in{e}"), 16)
            sp.wait_ge(sem("pv_done"), HEADS * NPAIR)
            for e in range(E):
                if e >= NRES:
                    sp.dma_start(wi_of(e), v(wi[e], "(k p) n -> p k n", p=P)).then_inc(sem(f"wi_in{e}"), 16)
                sp.dma_start(wo_sb[:, e], v(wo[e], "(i p) c -> p i c", p=P)).then_inc(sem(f"wo_in{e}"), 16)
            sp.wait_ge(sem("extra_ids"), 1)
            for k in range(NX):
                ex = sp.value_load(exid[0:1, k:k + 1], min_val=0, max_val=E - 1)
                sp.wait_ge(sem("window_mm"), k + 1)
                sp.dma_start(wi_of(k), v(wi[bass.ds(ex, 1)], "e (k p) n -> p (e k) n", p=P)
                             ).then_inc(sem(f"wi_in{k}"), 16)
                sp.dma_start(wo_sb[:, k], v(wo[bass.ds(ex, 1)], "e (i p) c -> p (e i) c", p=P)
                             ).then_inc(sem(f"wo_in{k}"), 16)
            for h in range(H2):
                sp.wait_ge(sem("y_out"), h + 1)
                sp.dma_start(v(out[0], "(h p) c -> p h c", p=P)[:, h], fin[:, h]).then_inc(sem("stored"), 16)
            sp.wait_ge(sem("stored"), 16 * H2)

        @block.gpsimd
        def _(pool):
            pool.memset(mhalf[:], -0.5)
            pool.memset(eps_c[:], LN_EPS)
            pool.memset(ones[:], 1.0)
            pool.memset(cmean, 1.0 / DC)
            pool.memset(q_max[:, :, :, DH:DH + 1], 0.0)
            pool.memset(q_max[:, :, :, DH + 1:KR], BIG)
            pool.memset(q_exp[:, :, :, DH + 1:KR], BIG)
            pool.memset(mask16, 0.0)
            pool.memset(val[:, :, :, DH:DH + 1], 1.0).then_inc(sem("pool_consts"), 1)

            def power(job):
                pool.wait_ge(sem("var_ready"), job + 1)
                pool.tensor_tensor(rstd[:, 2 * job:2 * job + 2], var_eps[:, 2 * job:2 * job + 2], mhalf[:], ALU.pow
                                   ).then_inc(sem("rstd_ready"), 1)

            pool.wait_ge(sem("pool_consts"), 1)
            power(0)
            power(1)

            def square(g, s):
                pool.wait_ge(sem("kraw"), g + 1)
                if not (isinstance(g, int) and g == 0):
                    pool.wait_ge(sem("ss_ready"), g)
                a = v(kf[:, s], "p t n -> p (t n)")
                pool.tensor_tensor(ksq, a, a, ALU.mult).then_inc(sem("sq_ready"), 1)

            def low(g, s):
                pool.wait_ge(sem("hi_done"), g + 1)
                for t in range(2):
                    a = v(kh[:, s, t], "p (h d) -> p h d", h=HEADS)
                    ins = pool.tensor_tensor(k16[:, s, t, :, DH:2 * DH], a, k16[:, s, t, :, 0:DH], ALU.subtract)
                ins.then_inc(sem("lo_done"), 1)

            def scale_keys(g, s):
                pool.wait_ge(sem("kr_ready"), g + 1)
                pool.tensor_tensor(heads8(kh[:, s]), heads8(kf[:, s]), per_head(kr[:, s]), ALU.mult
                                   ).then_inc(sem("khat"), 1)

            def pool_step(g, s, first=False, last=False):
                if not last:
                    square(g, s)
                if not first:
                    low(g - 1, 1 - s)
                if not last:
                    scale_keys(g, s)

            pool.wait_ge(sem("wprep_done"), 1)
            for g in range(4):
                pool_step(g, g % 2, first=g == 0)
            with pool.Fori(2, 7) as it:
                for s in range(2):
                    pool_step(2 * it + s, s)
            for g in range(14, NPAIR + 1):
                pool_step(g, g % 2, last=g == NPAIR)

            power(2)
            power(3)
            pool.wait_ge(sem("xx_ready"), 2)
            pool.tensor_tensor(res2, xx, row2("out_b"), ALU.add).then_inc(sem("xxb"), 1)
            power(4)
            pool.wait_ge(sem("gram_sb"), 1)
            for n in range(1, NLEV - 1):
                pool.tensor_tensor(bT[:, n], gram[:, 0:3:2, :], upper(n + 1).unsqueeze(1).to_broadcast([P, 2, P]),
                                   ALU.mult).then_inc(sem("bT_ready"), 1)
            pool.tensor_tensor(x1, x1, row2("b2"), ALU.add).then_inc(sem("pool_link"), 1)
            pool.wait_ge(sem("xm_ready"), 1)
            pool.wait_ge(sem("pool_link"), 1)
            pool.tensor_tensor(x1, x1, xm, ALU.add).then_inc(sem("res_ready"), 1)
            power(5)
            power(6)
            power(7)
            pool.wait_ge(sem("xn_ready"), 2)
            pool.tensor_tensor(x2xn, x2[:], xn, ALU.add).then_inc(sem("x2xn_ready"), 1)

        @block.scalar
        def _(act):
            act.dma_start(rowv[:], rows.partition_broadcast(P)).then_inc(sem("rows_in"), 16)
            act.dma_start(cst[:], consts).then_inc(sem("cst_in"), 16)
            act.dma_start(mask8, v(mask, "o (p n) -> (o p) n", n=P)).then_inc(sem("mask_in"), 16)
            act.dma_start(keyA[DH:DH + 1], key_ones).then_inc(sem("ones_in"), 16)
            act.dma_start(colv[:], cols).then_inc(sem("cols_in"), 16)
            act.dma_start(gt_sb[:], v(gateT, "(k p) n -> p k n", p=P)).then_inc(sem("gt_in"), 16)
            act.dma_start(lrw_sb[:], lrw).then_inc(sem("gt_in"), 16)
            nc.scalar.preload_act_table(ACT.Sqrt)
            act.wait_ge(sem("mask16_done"), 1)
            for h in range(HEADS):
                act.dma_start(keyA[DH + 1:KR, h, :], mask16).then_inc(sem("mrow_in"), 16)
            act.wait_ge(sem("cst_in"), 16)
            act.activation(id16[:], ident, ACT.Copy).then_inc(sem("id16_done"), 1)

            def evac(dst, src, need, n, done):
                act.wait_ge(sem(need), n)
                act.activation(dst, src, ACT.Copy).then_inc(sem(done), 1)

            evac(bw, bank[6][:, 0:512], "bw_mm", 1, "bw_done")
            evac(v(lnT, "p a b -> p (a b)"), bank[5], "lnT_mm", 1, "lnT_done")

            act.wait_ge(sem("q_ss"), 1)
            act.activation(ksd[:, 1], ss[:, 1], ACT.Sqrt, scale=1.0 / DH).then_inc(sem("q_sd"), 1)

            def values(g, s):
                act.wait_ge(sem("kv_mm"), g + 1)
                act.wait_ge(sem("rs_ready"), g + 1)
                for t in range(2):
                    ins = act.activation(val[:, bass.ds(2 * g + t, 1), :, 0:DH].rearrange("p j h d -> p (j h) d"),
                                         v(bank[2 + s][:, t * C:(t + 1) * C], "p (h d) -> p h d", h=HEADS),
                                         ACT.Copy, scale=rs[:, s, t:t + 1])
                ins.then_inc(sem("v_done"), 1)

            def deviation(g, s):
                act.wait_ge(sem("ctx_stats"), g + 1)
                act.activation(sd[:, s], c_mv[:, s, :, 1], ACT.Sqrt, bias=eps_c[:]).then_inc(sem("sd_ready"), 1)

            def high(g, s, drained=True):
                act.wait_ge(sem("khat"), g + 1)
                if drained:
                    act.wait_ge(sem("key_tr"), g - 1)
                for t in range(2):
                    ins = act.activation(k16[:, s, t, :, 0:DH], v(kh[:, s, t], "p (h d) -> p h d", h=HEADS), ACT.Copy)
                ins.then_inc(sem("hi_done"), 1)

            def key_norm(g, s):
                act.wait_ge(sem("ss_ready"), g + 1)
                act.activation(ksd[:, s], ss[:, s], ACT.Sqrt, scale=1.0 / (DH * RANGE * RANGE)
                               ).then_inc(sem("ksd_ready"), 1)

            def store_keys(g, s):
                act.wait_ge(sem("key_tr"), g + 1)
                act.activation(keyB[:, :, bass.ds(g * PAIR, PAIR)],
                               v(bank[4 + s].bitcast(F16), "p (h k) -> p h k", h=HEADS), ACT.Copy
                               ).then_inc(sem("keyB_done"), 1)

            def act_step(g, s):
                static = isinstance(g, int)
                if not static or g < NCP:
                    values(g, s)
                if not static or g + 1 < NCP:
                    deviation(g + 1, 1 - s)
                if not static or 1 <= g <= NPAIR:
                    high(g - 1, 1 - s, drained=not static or g >= 3)
                if not static or g < NPAIR:
                    key_norm(g, s)
                if not static or g >= 2:
                    store_keys(g - 2, s)

            deviation(0, 0)
            for g in range(4):
                act_step(g, g % 2)
            with act.Fori(2, 7) as it:
                for s in range(2):
                    act_step(2 * it + s, s)
            for g in range(14, NPAIR + 2):
                act_step(g, g % 2)

            nc.scalar.preload_act_table(ACT.Exp)

            def exp_group(n, s):
                act.wait_ge(sem("s_done"), n + 1)
                if not (isinstance(n, int) and n < 2):
                    act.wait_ge(sem("pv_done"), n - 1)
                act.activation(prob[:, s], bank[s], ACT.Exp, scale=1.0 / (RANGE * RANGE)
                               ).then_inc(sem("exp_done"), 1)

            exp_group(0, 0)
            exp_group(1, 1)
            with act.Fori(1, HEADS * NPAIR // 2) as it:
                for s in range(2):
                    exp_group(2 * it + s, s)

            evac(v(oT, "p a b -> p (a b)"), bank[6], "oT_mm", 1, "oT_done")
            evac(v(nT, "p a b -> p (a b)"), bank[0], "nT_mm", 1, "nT_done")
            act.wait_ge(sem("cols_in"), 16)
            act.wait_ge(sem("q_mm"), 1)
            for a in range(2):
                act.activation(qT[:, a], bank[3][:, a * T:(a + 1) * T], ACT.Identity, bias=colv[:, a:a + 1]
                               ).then_inc(sem("qT_done"), 1)
            evac(v(knT, "p a b -> p (a b)"), bank[5], "knT_mm", 1, "knT_done")
            act.wait_ge(sem("score_mm"), 1)
            act.wait_ge(sem("lr_ready"), 1)
            for a in range(2):
                act.activation(score[:, a], bank[7][:, a * T:(a + 1) * T], ACT.Copy, scale=lr[:, a:a + 1]
                               ).then_inc(sem("score_done"), 1)
            evac(v(yT, "p a b -> p (a b)"), bank[5], "yT_mm", 1, "yT_done")
            evac(v(nT, "p a b -> p (a b)"), bank[7], "nT_mm", 2, "nT_done")
            evac(v(tokT, "p a b -> p (a b)"), bank[2], "nT_mm", 3, "nT_done")
            act.wait_ge(sem("nlmax_ready"), 1)
            for a in range(2):
                act.activation(lexp[:, a], logits[:, a], ACT.Exp, bias=nlmax[:, a:a + 1],
                               accum_out=lsum[:, a:a + 1]).then_inc(sem("lsum_ready"), 1)
            nc.scalar.preload_act_table(ACT.Gelu)
            evac(xs[:, 1, 0:512], bank[1], "xs_mm", 2, "xs1_done")
            evac(xs[:, 1, 512:SLOTS], bank[3][:, 0:SLOTS - 512], "xs_mm", 4, "xs1_done")
            for n in range(NW):
                act.wait_ge(sem("h_mm"), n + 1)
                if n >= 2:
                    act.wait_ge(sem("window_mm"), n - 1)
                act.activation(v(hT[:, n % 2], "p i w -> p (i w)"), bank[n % 2], ACT.Gelu).then_inc(sem("gelu_done"), 1)

        @block.vector
        def _(dve):
            done = {}

            def link(ins, name="dve_link"):
                done[name] = done.get(name, 0) + 1
                ins.then_inc(sem(name), 1)
                dve.wait_ge(sem(name), done[name])

            def norm_stats(src, job):
                for a in range(2):
                    ins = dve.bn_stats(stats[:, a], src[:, a])
                link(ins)
                for a in range(2):
                    ins = dve.bn_aggr(mv[:, a], stats[:, a])
                link(ins)
                link(dve.tensor_scalar(var_eps[:, 2 * job:2 * job + 2], mv[:, :, 1], LN_EPS, None, ALU.add), "var_ready")

            def second_norm(job):
                r = rstd[:, 2 * job - 2:2 * job]
                link(dve.tensor_tensor(var2, mv[:, :, 1], r, ALU.mult))
                link(dve.tensor_tensor(var2, var2, r, ALU.mult))
                link(dve.tensor_scalar(var_eps[:, 2 * job:2 * job + 2], var2, LN_EPS, None, ALU.add), "var_ready")

            def twice_normed(src, once, twice, job, gamma, beta, once_done, twice_done):
                norm_stats(src, job)
                dve.wait_ge(sem("rstd_ready"), job + 1)
                for a in range(2):
                    ins = dve.tensor_scalar(once[:, a], src[:, a], mv[:, a, 0:1], rstd[:, 2 * job + a:2 * job + a + 1],
                                            ALU.subtract, ALU.mult)
                    link(ins, once_done)
                second_norm(job + 1)
                dve.wait_ge(sem("rstd_ready"), job + 2)
                for a in range(2):
                    r = rstd[:, 2 * job + 2 + a:2 * job + 3 + a]
                    ins = dve.scalar_tensor_tensor(twice[:, a], once[:, a], r, row(gamma), ALU.mult, ALU.mult)
                link(ins)
                link(dve.tensor_tensor(twice, twice, row2(beta), ALU.add), twice_done)

            dve.wait_ge(sem("pool_consts"), 1)
            dve.wait_ge(sem("wc_in"), 32)
            for k in range(2):
                ins = dve.tensor_scalar(bfree[:, k], ones[0:CT], colc[:, 2 + k:3 + k], None, ALU.mult)
            link(ins, "bfree_done")
            dve.wait_ge(sem("bw_mm"), 1)
            for k in range(2):
                ins = dve.tensor_scalar(wc[:, k], wc[:, k], colc[:, k:k + 1], None, ALU.mult)
            link(ins, "wg_done")
            dve.wait_ge(sem("cmean_mm"), 1)
            for k in range(2):
                ins = dve.tensor_tensor(wc[:, k], wc[:, k], bank[7][0:CT, 0:512], ALU.subtract)
            link(ins, "wprep_done")

            dve.wait_ge(sem("mask_in"), 16)
            link(dve.tensor_scalar(mask16[0:NCTX // P], mask8, BIG, -BIG, ALU.mult, ALU.add), "mask16_done")

            dve.wait_ge(sem("x_in"), 16)
            dve.wait_ge(sem("rows_in"), 16)
            twice_normed(xbuf, lat, lat, 0, "ln_l_g", "ln_l_b", "lat_once", "lat_done")
            link(dve.tensor_tensor(xbuf[:], xbuf[:], row2("bo"), ALU.add))
            link(dve.tensor_tensor(gqk, row("qn_g"), row("kn_g"), ALU.mult))

            dve.wait_ge(sem("q_raw_mm"), 1)
            qf, qn = kf[:, 1], kf[:, 0]
            link(dve.tensor_copy(v(qf, "p t n -> p (t n)"), bank[4]))
            link(dve.tensor_tensor(ksq, v(qf, "p t n -> p (t n)"), v(qf, "p t n -> p (t n)"), ALU.mult))
            link(dve.tensor_reduce(ss[:, 1], heads8(ksq), AX.X, ALU.add), "q_ss")
            dve.wait_ge(sem("q_sd"), 1)
            link(dve.tensor_scalar(krm, ksd[:, 1], RMS_EPS, None, ALU.max))
            link(dve.reciprocal(kr[:, 1], krm))
            link(dve.tensor_tensor(heads8(qn), heads8(qf), per_head(kr[:, 1]), ALU.mult))
            link(dve.tensor_tensor(heads8(qn), heads8(qn), gqk.unsqueeze(1).to_broadcast([P, 8, DH]), ALU.mult))
            for a in range(2):
                exact = v(qn[:, a], "p (h d) -> p h d", h=HEADS)
                link(dve.tensor_copy(q_max[:, a, :, 0:DH], exact))
                for c in range(2):
                    dve.tensor_copy(q_hh[:, a, :, c * DH:(c + 1) * DH], q_max[:, a, :, 0:DH])
                link(dve.tensor_tensor(q_exp[:, a, :, 0:DH], exact, q_max[:, a, :, 0:DH], ALU.subtract), "q_split")
            dve.wait_ge(sem("qT_mm"), 1)
            link(dve.tensor_copy(v(qT_max, "p h t -> p (h t)"), bank[4].bitcast(F16)[0:KR, :]))
            link(dve.tensor_copy(v(qT_hh, "p h t -> p (h t)"), bank[5].bitcast(F16)), "qT_ready")

            def ctx_stats(g, s):
                dve.wait_ge(sem(f"ctx_in{s}"), 16 * (g - s) + 32)
                for t in range(2):
                    ins = dve.bn_stats(c_st[:, s, t], ctxn[:, s, t])
                ins.then_inc(sem("ctx_bn"), 1)

            def ctx_aggr(g, s):
                for t in range(2):
                    ins = dve.bn_aggr(c_mv[:, s, t], c_st[:, s, t])
                ins.then_inc(sem("ctx_stats"), 1)

            def ctx_rstd(g, s):
                dve.wait_ge(sem("sd_ready"), g + 1)
                if not (isinstance(g, int) and g < 2):
                    dve.wait_ge(sem("v_done"), g - 1)
                dve.reciprocal(rs[:, s], sd[:, s]).then_inc(sem("rs_ready"), 1)

            def raw_keys(g, s):
                dve.wait_ge(sem("kv_mm"), g + 1)
                dve.wait_ge(sem("rs_ready"), g + 1)
                if not (isinstance(g, int) and g < 2):
                    dve.wait_ge(sem("khat"), g - 1)
                for t in range(2):
                    ins = dve.scalar_tensor_tensor(kf[:, s, t], bank[s][:, t * C:(t + 1) * C], rs[:, s, t:t + 1],
                                                   bw[:, 0:C], ALU.mult, ALU.add)
                ins.then_inc(sem("kraw"), 1)

            def latent_keys(g, s):
                dve.wait_ge(sem("kv_mm"), g + 1)
                dve.wait_ge(sem("khat"), g - 1)
                dve.tensor_copy(v(kf[:, s], "p t n -> p (t n)"), bank[s]).then_inc(sem("kraw"), 1)
                for t in range(2):
                    dve.tensor_tensor(val[:, 2 * g + t, :, 0:DH],
                                      v(bank[2 + s][:, t * C:(t + 1) * C], "p (h d) -> p h d", h=HEADS),
                                      v(bw[:, C:2 * C], "p (h d) -> p h d", h=HEADS), ALU.subtract
                                      ).then_inc(sem("vl_done"), 1)

            def sum_squares(g, s):
                dve.wait_ge(sem("sq_ready"), g + 1)
                dve.tensor_reduce(ss[:, s], heads8(ksq), AX.X, ALU.add).then_inc(sem("ss_ready"), 1)

            def key_scale(g, s):
                dve.wait_ge(sem("ksd_ready"), g + 1)
                dve.tensor_scalar(krm, ksd[:, s], RMS_EPS / RANGE, None, ALU.max).then_inc(sem("krm_done"), 1)
                dve.wait_ge(sem("krm_done"), g + 1)
                dve.reciprocal(kr[:, s], krm).then_inc(sem("kr_ready"), 1)

            def dve_step(g, s):
                static = isinstance(g, int)
                if static and g == NPAIR - 1:
                    latent_keys(g, s)
                else:
                    raw_keys(g, s)
                more = not static or g + 1 < NCP
                if more:
                    ctx_stats(g + 1, 1 - s)
                    dve.wait_ge(sem("ctx_bn"), g + 2)
                sum_squares(g, s)
                if more:
                    ctx_aggr(g + 1, 1 - s)
                key_scale(g, s)
                if more:
                    ctx_rstd(g + 1, 1 - s)

            dve.wait_ge(sem("bw_done"), 1)
            ctx_stats(0, 0)
            dve.wait_ge(sem("ctx_bn"), 1)
            ctx_aggr(0, 0)
            ctx_rstd(0, 0)
            for g in range(4):
                dve_step(g, g % 2)
            with dve.Fori(2, 7) as it:
                for s in range(2):
                    dve_step(2 * it + s, s)
            for g in range(14, NPAIR):
                dve_step(g, g % 2)

            def group_max(n, i, s):
                dve.wait_ge(sem("x_done"), n + 1)
                dve.tensor_reduce(pmax[:, :, bass.ds(i, 1)], v(bank[2 + s], "p (a k) -> p a k", a=2), AX.X, ALU.max
                                  ).then_inc(sem("max_done"), 1)

            def head_shift(h):
                dve.wait_ge(sem("max_done"), NPAIR * (h + 1))
                link(dve.tensor_reduce(shift, pmax, AX.X, ALU.max))
                link(dve.tensor_scalar(q_exp[:, :, h, DH], shift, -1.0, None, ALU.mult), "shift_done")
                dve.wait_ge(sem("qe_mm"), h + 1)
                link(dve.tensor_copy(qT_exp[:, h], bank[6].bitcast(F16)[0:KR, 0:T]), "qe_done")

            def head_output(h):
                dve.wait_ge(sem("pv_done"), NPAIR * (h + 1))
                acc = v(bank[4 + h % 2][:, 0:2 * (DH + 1)], "p (a d) -> p a d", a=2)
                link(dve.reciprocal(rden, acc[:, :, DH]))
                for a in range(2):
                    link(dve.scalar_tensor_tensor(o_sb[:, a, h * DH:(h + 1) * DH], acc[:, a, 0:DH], rden[:, a:a + 1],
                                                  bw[:, C + h * DH:C + (h + 1) * DH], ALU.mult, ALU.add), "o_done")

            for h in range(HEADS):
                p = (h * NPAIR) % 2
                with dve.Fori(0, NPAIR // 2) as it:
                    for k in range(2):
                        group_max(h * NPAIR + 2 * it + k, 2 * it + k, (p + k) % 2)
                group_max(h * NPAIR + NPAIR - 1, NPAIR - 1, p)
                head_shift(h)
                if h:
                    head_output(h - 1)
            head_output(HEADS - 1)

            def flat(a):
                return v(a, "p a b -> p (a b)")

            dve.wait_ge(sem("att_mm"), 1)
            link(dve.tensor_tensor(flat(x1), bank[7], flat(xbuf[:]), ALU.add))
            twice_normed(x1, xx, nrm, 2, "dn_g", "dn_b", "xx_ready", "nrm_done")
            dve.wait_ge(sem("k_mm"), 1)
            link(dve.tensor_tensor(kd, two(bank[1]), row2("gates_bk"), ALU.add))
            link(dve.tensor_tensor(vd, kd, kd, ALU.mult))
            link(dve.tensor_reduce(var_eps[:, 8:10], vd, AX.X, ALU.add), "var_ready")
            dve.wait_ge(sem("v_mm"), 1)
            link(dve.tensor_tensor(vd, two(bank[2]), row2("gates_bv"), ALU.add), "vd_ready")
            link(dve.tensor_tensor(lr, bank[4][:, 0:2], row("lr_b").to_broadcast([P, 2]), ALU.add), "lr_ready")
            dve.wait_ge(sem("rstd_ready"), 5)
            for a in range(2):
                ins = dve.tensor_scalar(kd[:, a], kd[:, a], rstd[:, 8 + a:9 + a], None, ALU.mult)
            link(ins, "kn_done")
            dve.wait_ge(sem("gram_mm"), 1)
            link(dve.tensor_copy(v(gram, "p b n -> p (b n)"), bank[6][:, 0:3 * P]), "gram_sb")
            diag = gram[:, 0:3:2, :]

            def both(m):
                return m.unsqueeze(1).to_broadcast([P, 2, P])

            link(dve.tensor_tensor(lv, diag, both(lower1), ALU.mult))
            link(dve.tensor_tensor(X, both(ident), lv, ALU.subtract))
            link(dve.tensor_tensor(lv, diag, both(upper(0)), ALU.mult))
            link(dve.tensor_tensor(XT, both(ident), lv, ALU.subtract))
            link(dve.tensor_tensor(bT[:, 0], diag, both(upper(1)), ALU.mult), "level0")
            for n in range(NLEV - 1):
                dve.wait_ge(sem("t1_mm"), n + 1)
                link(dve.tensor_copy(flat(T1), bank[0][:, 0:2 * P]), "t1_done")
                dve.wait_ge(sem("xx_mm"), n + 1)
                if n < NLEV - 2:
                    link(dve.tensor_tensor(flat(X), flat(X), bank[1][:, 0:2 * P], ALU.subtract), "x_next")
                link(dve.tensor_tensor(flat(XT), flat(XT), bank[2][:, 0:2 * P], ALU.subtract), "xt_next")
            dve.wait_ge(sem("u1_mm"), 1)
            link(dve.tensor_copy(u[:, 0], bank[3][:, 0:C]), "u_done")
            dve.wait_ge(sem("u01_mm"), 1)
            link(dve.tensor_tensor(vd[:, 1], vd[:, 1], bank[4][:, 0:C], ALU.subtract), "vd_ready")
            dve.wait_ge(sem("u2_mm"), 1)
            link(dve.tensor_copy(u[:, 1], bank[3][:, C:2 * C]), "u_done")
            dve.wait_ge(sem("xxb"), 1)
            dve.wait_ge(sem("delta_mm"), 1)
            link(dve.tensor_tensor(flat(xm), bank[6], flat(res2), ALU.add), "xm_ready")
            norm_stats(xm, 5)
            for a in range(2):
                ins = dve.scalar_tensor_tensor(nrm[:, a], xm[:, a], mv[:, a, 0:1], row("mn_g"),
                                               ALU.subtract, ALU.mult)
            link(ins)
            dve.wait_ge(sem("rstd_ready"), 6)
            for a in range(2):
                ins = dve.scalar_tensor_tensor(nrm[:, a], nrm[:, a], rstd[:, 10 + a:11 + a], row("mn_b"),
                                               ALU.mult, ALU.add)
            link(ins, "nrm_done")
            dve.wait_ge(sem("hm_mm"), 1)
            for a in range(2):
                ins = dve.tensor_scalar(hm[:, a], bank[0][:, a * T:(a + 1) * T], colv[:, 2 + a:3 + a], 0.0,
                                        ALU.add, ALU.max)
            link(ins, "hm_done")
            dve.wait_ge(sem("mlp_mm"), 1)
            dve.wait_ge(sem("res_ready"), 1)
            link(dve.tensor_tensor(flat(x2[:]), bank[1], flat(x1), ALU.add))

            twice_normed(x2, xn, tok, 6, "ffn_g", "ffn_b", "xn_ready", "tok_done")
            dve.wait_ge(sem("logit_mm"), 1)
            link(dve.tensor_copy(flat(logits), bank[3][:, 0:2 * E]))
            link(dve.tensor_reduce(lmax, logits, AX.X, ALU.max))
            link(dve.tensor_scalar(nlmax, lmax, -1.0, None, ALU.mult), "nlmax_ready")
            for a in range(2):
                ins = dve.tensor_scalar(cand[:, a], logits[:, a], lmax[:, a:a + 1], 100.0, ALU.is_lt, ALU.mult)
            link(ins)
            iota_e = iota[:, 0:E]
            link(dve.tensor_tensor(cand, cand, iota_e.unsqueeze(1).to_broadcast([P, 2, E]), ALU.add))
            link(dve.tensor_reduce(top, cand, AX.X, ALU.min))
            for a in range(2):
                ins = dve.tensor_scalar(hot[:, a], iota_e, top[:, a:a + 1], None, ALU.is_equal)
            link(ins, "hot_done")
            dve.wait_ge(sem("lsum_ready"), 2)
            link(dve.reciprocal(wtop, lsum))
            dve.wait_ge(sem("rank_mm"), 1)
            link(dve.tensor_copy(rk, bank[4][:, 0:3 * E]))
            link(dve.tensor_tensor(prod, two(rk[:, 0:2 * E]), hot, ALU.mult))
            link(dve.tensor_reduce(rank, prod, AX.X, ALU.add))
            n_e = rk[:, 2 * E:3 * E]
            link(dve.tensor_scalar(n_gt, n_e, float(W), None, ALU.is_gt))
            link(dve.scalar_tensor_tensor(over2, n_e, float(2 * W), n_gt, ALU.is_gt, ALU.add))
            link(dve.scalar_tensor_tensor(over, n_e, float(3 * W), over2, ALU.is_gt, ALU.add))
            link(dve.tensor_tensor_scan(incl, ones[:, 0:E], over, 0.0, ALU.mult, ALU.add))
            for k in range(NX):
                ins = dve.tensor_scalar(xcmp[:, k], incl, float(k), None, ALU.is_le)
            link(ins)
            link(dve.tensor_reduce(xid, xcmp, AX.X, ALU.add))
            link(dve.tensor_scalar(exid, xid, float(E - 1), None, ALU.min), "extra_ids")
            link(dve.tensor_tensor(offs, incl, over, ALU.subtract))
            link(dve.tensor_tensor(osel, hot, offs.unsqueeze(1).to_broadcast([P, 2, E]), ALU.mult))
            link(dve.tensor_reduce(offt, osel, AX.X, ALU.add))
            link(dve.tensor_scalar(win1, rank, float(W), None, ALU.is_ge))
            link(dve.scalar_tensor_tensor(win2, rank, float(2 * W), win1, ALU.is_ge, ALU.add))
            link(dve.scalar_tensor_tensor(win, rank, float(3 * W), win2, ALU.is_ge, ALU.add))
            link(dve.tensor_tensor(dtile, offt, win, ALU.add))
            link(dve.tensor_tensor(dtop, dtile, top, ALU.subtract))
            link(dve.scalar_tensor_tensor(dx, dtop, float(E - 1), win1, ALU.add, ALU.mult))
            link(dve.tensor_tensor(tile_, dx, top, ALU.add))
            link(dve.scalar_tensor_tensor(inpos, win, -float(W), rank, ALU.mult, ALU.add))
            link(dve.scalar_tensor_tensor(slot, tile_, float(W), inpos, ALU.mult, ALU.add))
            for a in range(2):
                link(dve.tensor_scalar(sel[:, a], iota, slot[:, a:a + 1], None, ALU.is_equal), "sel_done")
            dve.wait_ge(sem("xs_mm"), 1)
            link(dve.tensor_copy(xs[:, 0, 0:512], bank[0]), "xs0_done")
            dve.wait_ge(sem("xs_mm"), 3)
            link(dve.tensor_copy(xs[:, 0, 512:SLOTS], bank[2][:, 0:SLOTS - 512]), "xs0_done")
            tail = SLOTS - (NSG - 1) * P
            for q in range(NSG // 2):
                dve.wait_ge(sem("selT_mm"), q + 1)
                src = two(bank[4 + q % 2])
                if 2 * q + 2 < NSG:
                    ins = dve.tensor_copy(selT[:, 2 * q:2 * q + 2], src)
                else:
                    dve.tensor_copy(selT[:, 2 * q], src[:, 0])
                    ins = dve.tensor_copy(selT[0:tail, 2 * q + 1], src[0:tail, 1])
                link(ins, "selT_done")
            for q in range(NSG):
                n = min(P, SLOTS - q * P)
                dve.wait_ge(sem("window_mm"), min(2 * q + 2, NW))
                if q >= 2:
                    dve.wait_ge(sem("y_tr"), q - 1)
                link(dve.tensor_copy(yT_e[:, q % 2, :, 0:n], two(bank[2 + q % 2][:, 0:2 * P])[:, :, 0:n]), "yTe_done")
                dve.wait_ge(sem("y_tr"), q + 1)
                if q >= 2:
                    dve.wait_ge(sem("back_mm"), q - 1)
                link(dve.tensor_copy(ys[0:n, q % 2], bank[4 + q % 2][0:n, 0:C]), "ys_done")
            dve.wait_ge(sem("x2xn_ready"), 1)
            dve.wait_ge(sem("back_mm"), NSG)
            for a in range(2):
                dve.scalar_tensor_tensor(fin[:, a], bank[6 + a][:, 0:C], wtop[:, a:a + 1], x2xn[:, a],
                                         ALU.mult, ALU.add).then_inc(sem("y_out"), 1)

        @block.tensor
        def _(pe):
            def turn(dst, src, need, n, done):
                pe.wait_ge(sem(need), n)
                for c in range(2):
                    for a in range(2):
                        ins = pe.transpose(dst[:, c * T + a * P:c * T + (a + 1) * P], src[:, a, c * P:(c + 1) * P],
                                           ident)
                ins.then_inc(sem(done), 1)

            def product(dst, lhsT, rhs):
                n = len(lhsT)
                for k in range(n):
                    ins = pe.matmul(dst, lhsT[k], rhs[k], start=k == 0, stop=k == n - 1)
                return ins

            def by_token(dst, src, w):
                n = w.shape[2]
                for a in range(2):
                    ins = product(dst[:, a * n:(a + 1) * n], [src[:, k, a * P:(a + 1) * P] for k in range(2)],
                                  [w[:, k] for k in range(2)])
                return ins

            def by_channel(dst, src, w):
                for a in range(2):
                    ins = product(dst[:, a * T:(a + 1) * T], [w[:, k, a * P:(a + 1) * P] for k in range(2)],
                                  [src[:, k] for k in range(2)])
                return ins

            pe.wait_ge(sem("bfree_done"), 1)
            product(bank[6], [bfree[:, k] for k in range(2)], [wc[:, k] for k in range(2)]).then_inc(sem("bw_mm"), 1)
            pe.wait_ge(sem("wg_done"), 1)
            product(bank[7][0:CT], [cmean] * 2, [wc[:, k] for k in range(2)]).then_inc(sem("cmean_mm"), 1)
            pe.wait_ge(sem("cst_in"), 16)
            turn(bank[5], lat, "lat_done", 1, "lnT_mm")
            pe.wait_ge(sem("lnT_done"), 1)
            pe.wait_ge(sem("wq_in"), 16)
            by_token(bank[4], lnT, wq).then_inc(sem("q_raw_mm"), 1)
            pe.wait_ge(sem("q_split"), 2)
            pe.wait_ge(sem("id16_done"), 1)
            for src, dst, n in ((q_max, bank[4], KR), (q_hh, bank[5], P)):
                for h in range(HEADS):
                    for a in range(2):
                        ins = pe.transpose(dst.bitcast(F16)[0:n, h * T + a * P:h * T + (a + 1) * P],
                                           src[:, a, h, :], id16[:])
            ins.then_inc(sem("qT_mm"), 1)
            pe.wait_ge(sem("qT_ready"), 1)
            pe.wait_ge(sem("wprep_done"), 1)

            def keys_values(g, s):
                if isinstance(g, int) and g == NPAIR - 1:
                    pe.wait_ge(sem("wl_in"), 16)
                    src, w = lnT, wl
                else:
                    pe.wait_ge(sem(f"ctx_in{s}"), 16 * (g - s) + 32)
                    src, w = ctxt[:, s], wc
                if not (isinstance(g, int) and g < 2):
                    pe.wait_ge(sem("kraw"), g - 1)
                    pe.wait_ge(sem("v_done"), g - 1)
                for t in range(2):
                    mine = [src[:, k, t * P:(t + 1) * P] for k in range(2)]
                    product(bank[s][:, t * C:(t + 1) * C], mine, [w[:, k, 0:C] for k in range(2)])
                    ins = product(bank[2 + s][:, t * C:(t + 1) * C], mine, [w[:, k, C:2 * C] for k in range(2)])
                ins.then_inc(sem("kv_mm"), 1)

            def turn_keys(g, s):
                pe.wait_ge(sem("lo_done"), g + 1)
                if not (isinstance(g, int) and g < 2):
                    pe.wait_ge(sem("keyB_done"), g - 1)
                for h in range(HEADS):
                    for t in range(2):
                        ins = pe.transpose(bank[4 + s].bitcast(F16)[:, h * PAIR + t * P:h * PAIR + (t + 1) * P],
                                           k16[:, s, t, h, :], id16[:])
                ins.then_inc(sem("key_tr"), 1)

            def pe_step(g, s):
                static = isinstance(g, int)
                if not static or g < NPAIR:
                    keys_values(g, s)
                if not static or g >= 2:
                    turn_keys(g - 2, s)

            for g in range(4):
                pe_step(g, g % 2)
            with pe.Fori(2, 7) as it:
                for s in range(2):
                    pe_step(2 * it + s, s)
            for g in range(14, NPAIR + 2):
                pe_step(g, g % 2)

            def max_scores(h, i, n, s):
                if not (isinstance(n, int) and n < 2):
                    pe.wait_ge(sem("max_done"), n - 1)
                for a in range(2):
                    ins = pe.matmul(bank[2 + s][:, a * T:(a + 1) * T], qT_max[:, h, a * P:(a + 1) * P],
                                    keyA[0:KR, h, bass.ds(i * PAIR, PAIR)], start=True, stop=True)
                ins.then_inc(sem("x_done"), 1)

            def scores(h, i, n, s):
                if not (isinstance(n, int) and n < 2):
                    pe.wait_ge(sem("exp_done"), n - 1)
                for t in range(2):
                    at = bass.ds(i * PAIR + t * P, P)
                    pe.matmul(bank[s][:, t * T:(t + 1) * T], keyA[0:KR, h, at], qT_exp[:, h], start=True, stop=False)
                    ins = pe.matmul(bank[s][:, t * T:(t + 1) * T], keyB[:, h, at], qT_hh[:, h],
                                    start=False, stop=True)
                ins.then_inc(sem("s_done"), 1)

            def weighted_values(h, i, n, s, first=False, last=False):
                pe.wait_ge(sem("exp_done"), n + 1)
                for t in range(2):
                    for a in range(2):
                        ins = pe.matmul(bank[4 + h % 2][:, a * (DH + 1):(a + 1) * (DH + 1)],
                                        prob[:, s, t * T + a * P:t * T + (a + 1) * P],
                                        val[:, bass.ds(2 * i + t, 1), h, :].rearrange("p j d -> p (j d)"),
                                        start=first and t == 0 and a == 0, stop=last and t == 1,
                                        skip_group_check=True)
                ins.then_inc(sem("pv_done"), 1)

            pe.wait_ge(sem("keyA_in"), 16 * NPAIR)
            pe.wait_ge(sem("mrow_in"), 16 * HEADS)
            pe.wait_ge(sem("ones_in"), 16)
            pe.wait_ge(sem("kraw"), NPAIR)
            pe.wait_ge(sem("vl_done"), 2)
            for i in range(2):
                max_scores(0, i, i, i)
            with pe.Fori(1, NPAIR // 2) as it:
                for k in range(2):
                    max_scores(0, 2 * it + k, 2 * it + k, k)
            max_scores(0, NPAIR - 1, NPAIR - 1, (NPAIR - 1) % 2)
            for h in range(HEADS):
                base = h * NPAIR
                pe.wait_ge(sem("shift_done"), h + 1)
                for a in range(2):
                    ins = pe.transpose(bank[6].bitcast(F16)[0:KR, a * P:(a + 1) * P], q_exp[:, a, h, :], id16[:])
                ins.then_inc(sem("qe_mm"), 1)
                pe.wait_ge(sem("qe_done"), h + 1)
                if h >= 2:
                    pe.wait_ge(sem("o_done"), 2 * (h - 1))

                def group(i, s, before=None, last=False):
                    scores(h, i, base + i, s)
                    if h + 1 < HEADS:
                        max_scores(h + 1, i, base + NPAIR + i, 1 - s)
                    if before is not None:
                        weighted_values(h, before, base + before, 1 - s, first=isinstance(before, int) and before == 0)

                s0 = base % 2
                group(0, s0)
                group(1, 1 - s0, before=0)
                with pe.Fori(1, NPAIR // 2) as it:
                    for k in range(2):
                        i = 2 * it + k
                        group(i, (s0 + k) % 2, before=i - 1)
                group(NPAIR - 1, (s0 + NPAIR - 1) % 2, before=NPAIR - 2)
                weighted_values(h, NPAIR - 1, base + NPAIR - 1, (s0 + NPAIR - 1) % 2, last=True)

            turn(bank[6], o_sb, "o_done", 2 * HEADS, "oT_mm")
            pe.wait_ge(sem("oT_done"), 1)
            pe.wait_ge(sem("woa_in"), 16)
            by_token(bank[7], oT, wo_at).then_inc(sem("att_mm"), 1)

            turn(bank[0], nrm, "nrm_done", 1, "nT_mm")
            pe.wait_ge(sem("nT_done"), 1)
            pe.wait_ge(sem("gw_in"), 16)
            by_token(bank[1], nT, gw[:, :, C:2 * C]).then_inc(sem("k_mm"), 1)
            by_channel(bank[3], nT, gw[:, :, 0:C]).then_inc(sem("q_mm"), 1)
            by_token(bank[2], nT, gw[:, :, 2 * C:3 * C])
            pe.wait_ge(sem("gt_in"), 32)
            by_token(bank[4], nT, lrw_sb[:].unsqueeze(2)).then_inc(sem("v_mm"), 1)
            turn(bank[5], kd, "kn_done", 1, "knT_mm")
            pe.wait_ge(sem("knT_done"), 1)
            product(bank[6][:, 0:T], [knT[:, k, 0:P] for k in range(2)], [knT[:, k] for k in range(2)])
            product(bank[6][:, T:T + P], [knT[:, k, P:T] for k in range(2)], [knT[:, k, P:T] for k in range(2)]
                    ).then_inc(sem("gram_mm"), 1)
            pe.wait_ge(sem("qT_done"), 2)
            by_channel(bank[7], qT, knT).then_inc(sem("score_mm"), 1)
            for n in range(NLEV - 1):
                if n == 0:
                    pe.wait_ge(sem("level0"), 1)
                else:
                    pe.wait_ge(sem("bT_ready"), n)
                    pe.wait_ge(sem("x_next"), n)
                for b in range(2):
                    ins = pe.matmul(bank[0][:, b * P:(b + 1) * P], bT[:, n, b], X[:, b], start=True, stop=True)
                ins.then_inc(sem("t1_mm"), 1)
                pe.wait_ge(sem("t1_done"), n + 1)
                if n:
                    pe.wait_ge(sem("xt_next"), n)
                for b in range(2):
                    if n < NLEV - 2:
                        pe.matmul(bank[1][:, b * P:(b + 1) * P], XT[:, b], T1[:, b], start=True, stop=True)
                for b in range(2):
                    ins = pe.matmul(bank[2][:, b * P:(b + 1) * P], T1[:, b], XT[:, b], start=True, stop=True)
                ins.then_inc(sem("xx_mm"), 1)
            pe.wait_ge(sem("xt_next"), NLEV - 1)
            pe.matmul(bank[3][:, 0:C], XT[:, 0], vd[:, 0], start=True, stop=True).then_inc(sem("u1_mm"), 1)
            pe.wait_ge(sem("u_done"), 1)
            pe.matmul(bank[4][:, 0:C], gram[:, 1], u[:, 0], start=True, stop=True).then_inc(sem("u01_mm"), 1)
            pe.wait_ge(sem("vd_ready"), 2)
            pe.matmul(bank[3][:, C:2 * C], XT[:, 1], vd[:, 1], start=True, stop=True).then_inc(sem("u2_mm"), 1)
            pe.wait_ge(sem("u_done"), 2)
            pe.wait_ge(sem("score_done"), 2)
            by_channel(bank[5], score, u).then_inc(sem("yT_mm"), 1)
            pe.wait_ge(sem("yT_done"), 1)
            pe.wait_ge(sem("ow_in"), 16)
            by_token(bank[6], yT, ow).then_inc(sem("delta_mm"), 1)
            turn(bank[7], nrm, "nrm_done", 2, "nT_mm")
            pe.wait_ge(sem("nT_done"), 2)
            pe.wait_ge(sem("w1_in"), 16)
            by_channel(bank[0], nT, w1_sb).then_inc(sem("hm_mm"), 1)
            pe.wait_ge(sem("hm_done"), 1)
            pe.wait_ge(sem("w2_in"), 16)
            by_token(bank[1], hm, w2_sb).then_inc(sem("mlp_mm"), 1)

            turn(bank[2], tok, "tok_done", 1, "nT_mm")
            pe.wait_ge(sem("nT_done"), 3)
            by_token(bank[3], tokT, gt_sb[:]).then_inc(sem("logit_mm"), 1)
            pe.wait_ge(sem("hot_done"), 1)
            product(bank[4][:, 0:E], [tri], [hot[:, 0]])
            product(bank[4][:, E:2 * E], [ones[:], tri], [hot[:, 0], hot[:, 1]])
            product(bank[4][:, 2 * E:3 * E], [ones[:], ones[:]], [hot[:, 0], hot[:, 1]]).then_inc(sem("rank_mm"), 1)
            pe.wait_ge(sem("sel_done"), 2)
            for m, (at, n) in enumerate(((0, 512), (512, SLOTS - 512))):
                for c in range(2):
                    product(bank[2 * m + c][:, 0:n], [tok[:, a, c * P:(c + 1) * P] for a in range(2)],
                            [sel[:, a, at:at + n] for a in range(2)]).then_inc(sem("xs_mm"), 1)

            def turn_sel(q):
                if q >= 2:
                    pe.wait_ge(sem("selT_done"), q - 1)
                for j in range(2):
                    grp = 2 * q + j
                    n = min(P, SLOTS - grp * P)
                    for a in range(2):
                        ins = pe.transpose(bank[4 + q % 2][0:n, j * T + a * P:j * T + (a + 1) * P],
                                           sel[:, a, grp * P:grp * P + n], ident)
                ins.then_inc(sem("selT_mm"), 1)

            for q in range(NSG // 2):
                turn_sel(q)

            def first_product(n):
                e = n if n < E else n - E
                pe.wait_ge(sem(f"wi_in{e}"), 16 if n < E else 32)
                if n == 0:
                    pe.wait_ge(sem("xs0_done"), 2)
                    pe.wait_ge(sem("xs1_done"), 2)
                if n >= 2:
                    pe.wait_ge(sem("gelu_done"), n - 1)
                for i in range(IT):
                    ins = product(bank[n % 2][:, i * W:(i + 1) * W],
                                  [wi_of(e)[:, k, i * P:(i + 1) * P] for k in range(2)],
                                  [xs[:, k, n * W:(n + 1) * W] for k in range(2)])
                ins.then_inc(sem("h_mm"), 1)

            def second_product(n):
                e = n if n < E else n - E
                q = n // 2
                pe.wait_ge(sem(f"wo_in{e}"), 16 if n < E else 32)
                pe.wait_ge(sem("gelu_done"), n + 1)
                if n % 2 == 0 and q >= 2:
                    pe.wait_ge(sem("yTe_done"), q - 1)
                for c in range(2):
                    at = c * P + (n % 2) * W
                    ins = product(bank[2 + q % 2][:, at:at + W],
                                  [wo_sb[:, e, i, c * P:(c + 1) * P] for i in range(IT)],
                                  [hT[:, n % 2, i] for i in range(IT)])
                ins.then_inc(sem("window_mm"), 1)

            def back(q):
                n = min(P, SLOTS - q * P)
                pe.wait_ge(sem("yTe_done"), q + 1)
                if q == 0:
                    pe.wait_ge(sem("selT_done"), NSG // 2)
                if q >= 2:
                    pe.wait_ge(sem("ys_done"), q - 1)
                for c in range(2):
                    ins = pe.transpose(bank[4 + q % 2][0:n, c * P:(c + 1) * P], yT_e[:, q % 2, c, 0:n], ident)
                ins.then_inc(sem("y_tr"), 1)
                pe.wait_ge(sem("ys_done"), q + 1)
                for a in range(2):
                    ins = pe.matmul(bank[6 + a][:, 0:C], selT[0:n, q, a * P:(a + 1) * P], ys[0:n, q % 2],
                                    start=q == 0, stop=q == NSG - 1)
                ins.then_inc(sem("back_mm"), 1)

            first_product(0)
            for n in range(NW):
                if n + 1 < NW:
                    first_product(n + 1)
                second_product(n)
                if n % 2 == 0 and n >= 2:
                    back(n // 2 - 1)
            back(NSG - 1)


_OUTS = [((1, T, C), 'float32')]


def kernel(**inputs):
    import numpy as _np
    import concourse.bacc as _bacc
    from concourse import mybir as _mybir
    from concourse.bass_utils import run_bass_kernel_spmd as _run

    g = {k: _np.asarray(a) for k, a in inputs.items()}
    gb = g["L0_attn_gates_b"]
    vec = {"ln_l_g": g["L0_xattn_ln_l_g"], "ln_l_b": g["L0_xattn_ln_l_b"], "qn_g": g["L0_xattn_qn_g"],
           "kn_g": g["L0_xattn_kn_g"], "bo": g["L0_xattn_bo"], "dn_g": g["L0_attn_dn_g"], "dn_b": g["L0_attn_dn_b"],
           "gates_bk": gb[C:2 * C], "gates_bv": gb[2 * C:3 * C], "lr_b": g["L0_attn_lr_b"],
           "out_b": g["L0_attn_out_b"], "mn_g": g["L0_attn_mn_g"], "mn_b": g["L0_attn_mn_b"],
           "b2": g["L0_attn_b2"], "ffn_g": g["L0_ffn_ln_gamma"], "ffn_b": g["L0_ffn_ln_beta"]}
    r, c = _np.arange(P)[:, None], _np.arange(P)[None, :]
    consts = _np.zeros((P, NCONST), _np.float32)
    for n in range(NLEV):
        s = 1 << n
        below = (r // (2 * s) == c // (2 * s)) & (r // s % 2 == 1) & (c // s % 2 == 0)
        consts[:, (1 + n) * P:(2 + n) * P] = below.T
        if n == 0:
            consts[:, 0:P] = below
    consts[:, C_ID:C_ID + P] = r == c
    consts[:, C_TRI:C_TRI + P] = r < c
    consts[:, C_IOTA:] = _np.arange(SLOTS)
    arrays_in = {
        "x": g["x"], "ctx": g["ctx_768"], "ctxT": g["ctx_768"][0].T, "mask": g["mask_BxS2_bk0"],
        "wkvT": g["L0_xattn_Wkv"].T, "wqT": g["L0_xattn_Wq"].T, "wlkvT": g["L0_xattn_Wlkv"].T,
        "woT": g["L0_xattn_Wo"].T, "gates": g["L0_attn_gates_w"], "lrw": g["L0_attn_lr_w"].reshape(2, P).T,
        "outw": g["L0_attn_out_w"], "w1": g["L0_attn_w1"], "w2": g["L0_attn_w2"],
        "gateT": g["L0_ffn_gate_weight"].T, "wi": g["L0_ffn_wi"], "wo": g["L0_ffn_wo"],
        "rows": _np.concatenate([vec[k] for k in ROW]),
        "cols": _np.concatenate([gb[0:C].reshape(2, P), g["L0_attn_b1"].reshape(2, P)]).T,
        "cols_ctx": _np.concatenate([g["L0_xattn_ln_x_g"].reshape(2, CT), g["L0_xattn_ln_x_b"].reshape(2, CT)]).T,
        "consts": consts, "key_ones": _np.ones((1, HEADS, NKEY), _np.float16),
    }
    nc = _bacc.Bacc("TRN2", target_bir_lowering=False, num_devices=1)
    arrays, args = {}, []
    for name, a in arrays_in.items():
        a = _np.ascontiguousarray(a)
        arrays[f"in_{name}_dram"] = a
        args.append(nc.dram_tensor(f"in_{name}_dram", a.shape, _mybir.dt.from_np(a.dtype), kind="ExternalInput").ap())
    for i, (shape, dtype) in enumerate(_OUTS):
        dt = _mybir.dt.from_np(_np.dtype(dtype))
        args.append(nc.dram_tensor(f"out_{i}_dram", shape, dt, kind="ExternalOutput").ap())
    perceiver_layer(nc, *args)
    r = _run(nc, [arrays], core_ids=[0])
    return r.results[0]["out_0_dram"]
```

```python
from contextlib import ExitStack

import concourse.bass as bass
from concourse import mybir

F32 = mybir.dt.float32
F16 = mybir.dt.float16
I32 = mybir.dt.int32
U8 = mybir.dt.uint8
ALU = mybir.AluOpType
ACT = mybir.ActivationFunctionType
AX = mybir.AxisListType

P = 128
T = 256
C = 256
H2 = T // P
NCTX = 4096
DC = 192
CT = DC // 2
HEADS = 4
DH = 64
NKEY = NCTX + T
PAIR = 2 * P
NCP = NCTX // PAIR
NPAIR = NKEY // PAIR
KR = DH + 2
LN_EPS = 1e-5
RMS_EPS = 1e-8
RANGE = 8.0
BIG = 30000.0
E = 8
I = 1024
IT = I // P
W = 128
NX = (T - 1) // W
NW = E + NX
SLOTS = NW * W
NRES = 3
YS = NW // 2
assert W == P and NX == 1
VW = 96

ROW = {}
_at = 0
for _n, _w in (("ln_l_g", C), ("ln_l_b", C), ("qn_g", DH), ("kn_g", DH), ("bo", C), ("dn_g", C), ("dn_b", C),
               ("gates_bk", C), ("gates_bv", C), ("lr_b", 1), ("out_b", C), ("mn_g", C), ("mn_b", C), ("b2", C),
               ("ffn_g", C), ("ffn_b", C)):
    ROW[_n] = (_at, _at + _w)
    _at += _w
NROW = _at
NLEV = 7
C_ID = 0
C_TRI = C_ID + P
C_IOTA = C_TRI + P
NCONST = C_IOTA + SLOTS
XS_CUTS = [(at, min(512, SLOTS - at)) for at in range(0, SLOTS, 512)]


def perceiver_layer(nc, x, ctx, ctxT, mask, wkvT, wqT, wlkvT, woT, gates, lrw, outw, w1, w2, gateT, wi, wo,
                    rows, cols, cols_ctx, consts, levels, key_ones, out):
    with ExitStack() as stack:
        def sb(name, shape, dt=F32):
            return stack.enter_context(nc.sbuf_tensor(name, shape, dt))

        sems = {}

        def sem(name):
            if name not in sems:
                sems[name] = stack.enter_context(nc.semaphore(name))
            return sems[name]

        bank = [stack.enter_context(nc.psum_tensor(f"bank{i}", [P, 512], F32))[:] for i in range(8)]

        def region(tensor, at=0):
            pos = [at]

            def take(cols, dt=F32, parts=P, **dims):
                n = cols if dt in (F32, I32) else cols // 2
                a = tensor[0:parts, pos[0]:pos[0] + n]
                pos[0] += n
                assert pos[0] <= tensor.shape[1], (pos, tensor.shape)
                return a if dt == F32 else a.bitcast(dt)
            return take, pos

        def v(ap, spec, /, **dims):
            return ap.rearrange(spec, **dims)

        def two(a):
            return a.rearrange("p (a b) -> p a b", a=2)

        rowv = sb("rowv", [P, NROW])
        colv = sb("colv", [P, 4])
        cst = sb("cst", [P, NCONST])
        ident = cst[:, C_ID:C_ID + P]
        tri = cst[:, C_TRI:C_TRI + P]
        iota = cst[:, C_IOTA:C_IOTA + SLOTS]
        id16 = sb("id16", [P, P], F16)
        ones = sb("ones", [P, P])
        xbuf = sb("xbuf", [P, H2, C])
        var_eps = sb("var_eps", [P, 16])
        rstd = sb("rstd", [P, 16])
        mhalf = sb("mhalf", [P, 2])
        stats = sb("stats", [P, H2, 6])
        mv = sb("mv", [P, H2, 2])
        eps_c = sb("eps_c", [P, 1])
        gt_sb = sb("gt_sb", [P, 2, E])
        lrw_sb = sb("lrw_sb", [P, 2])
        small = sb("small", [P, 140])
        rt = sb("rt", [P, 232])
        wi_res = sb("wi_res", [P, NRES, H2, I])

        R = sb("R", [P, HEADS * NKEY + (E - NRES) * H2 * I])
        take, _ = region(R)
        key16 = v(take(HEADS * 2 * NKEY, F16), "p (h o k) -> p h o k", h=HEADS, o=2)
        keyA = key16[:, :, 0]
        keyB = key16[:, :, 1]
        NVAL = 2 * NPAIR * HEADS * (DH + 1)
        val_flat = take(NVAL + VW)
        val = v(val_flat[:, 0:NVAL], "p (j h d) -> p j h d", h=HEADS, d=DH + 1)
        per_head_room = v(R[:, 0:HEADS * NKEY], "p (h n) -> p h n", h=HEADS)

        def wo_of(e):
            return v(per_head_room[:, e // 2, (e % 2) * IT * C:(e % 2 + 1) * IT * C], "p (i c) -> p i c", i=IT)

        def level_pair(h):
            return per_head_room[:, h, 2 * IT * C:2 * IT * C + 2 * P]

        def level(n):
            return level_pair(n // 2)[:, (n % 2) * P:(n % 2 + 1) * P]

        lower1 = level(0)

        def upper(n):
            return level(n + 1)

        wi_late = v(R[:, HEADS * NKEY:], "p (e k n) -> p e k n", e=E - NRES, k=H2)

        def wi_of(e):
            return wi_res[:, e] if e < NRES else wi_late[:, e - NRES]

        S = sb("S", [P, 13184])
        take, pos = region(S)
        ctxn = v(take(2 * 2 * DC), "p (s t c) -> p s t c", s=2, t=2)
        ctxt = v(take(2 * 2 * PAIR, parts=CT), "p (s k n) -> p s k n", s=2, k=2)
        wc = two(take(2 * 512, parts=CT))
        wq = two(take(2 * C))
        wl = two(take(2 * 512))
        bw = take(512)
        kf = v(take(2 * 512), "p (s t n) -> p s t n", s=2, t=2)
        ksq = v(take(2 * 512), "p (s n) -> p s n", s=2)
        kh = v(take(2 * 512), "p (s t n) -> p s t n", s=2, t=2)
        k16 = v(take(2 * 2 * HEADS * P, F16), "p (s t h d) -> p s t h d", s=2, t=2, h=HEADS)
        qT_max = v(take(HEADS * T, F16), "p (h t) -> p h t", h=HEADS)
        qT_exp = v(take(HEADS * T, F16), "p (h t) -> p h t", h=HEADS)
        qT_hh = v(take(HEADS * T, F16), "p (h t) -> p h t", h=HEADS)
        q_exp = v(take(H2 * HEADS * KR, F16), "p (a h d) -> p a h d", a=H2, h=HEADS)
        mask8 = take(P // 4)[0:NCTX // P].bitcast(U8)
        mask16 = take(P, F16, parts=NKEY // P)
        pmax = v(take(H2 * NPAIR), "p (a n) -> p a n", a=H2)
        prob = v(take(2 * 512), "p (s n) -> p s n", s=2)
        o_sb = two(take(H2 * C))
        oT = two(take(H2 * T))
        lnT = oT
        wo_at = two(S[:, 3584:3584 + 2 * C])
        take, _ = region(wi_res[:].rearrange("p e k n -> p (e k n)"))
        lat = two(take(H2 * C))
        q_max = v(take(H2 * HEADS * KR, F16), "p (a h d) -> p a h d", a=H2, h=HEADS)
        q_hh = v(take(H2 * HEADS * P, F16), "p (a h d) -> p a h d", a=H2, h=HEADS)
        qf = take(512)
        qn = take(512)
        qsq = take(512)
        gqk = take(DH)
        cmean = take(CT, parts=CT)
        bfree = two(take(2 * P, parts=CT))
        take, pos = region(S)
        gw = two(take(2 * 3 * C))
        ow = two(take(2 * C))
        w1_sb = two(take(2 * C))
        w2_sb = two(take(2 * C))
        DELTA_W = pos[0]
        assert DELTA_W <= 8448
        x1 = two(take(H2 * C))
        xx = two(take(H2 * C))
        nrm = two(take(H2 * C))
        nT = two(take(H2 * T))
        knT = two(take(H2 * T))
        qT = two(take(H2 * T))
        kd = two(take(H2 * C))
        vd = two(take(H2 * C))
        score = two(take(H2 * T))
        yT = two(take(H2 * T))
        u = two(take(H2 * C))
        xm = two(take(H2 * C))
        res2 = two(take(H2 * C))
        hm = two(take(H2 * T))
        gram = v(take(3 * P), "p (b n) -> p b n", b=3)
        bT = v(take((NLEV - 1) * 2 * P), "p (l b n) -> p l b n", l=NLEV - 1, b=2)
        X = two(take(2 * P))
        XT = two(take(2 * P))
        T1 = two(take(2 * P))
        lv = two(take(2 * P))
        x2 = xbuf
        take, _ = region(S)
        xn = two(take(H2 * C))
        tok = two(take(H2 * C))
        tokT = two(take(H2 * T))
        fin = two(take(H2 * C))
        x2xn = two(take(H2 * C))
        sel = two(take(H2 * SLOTS))
        xs = two(take(H2 * SLOTS))
        selT = v(take(NW * T), "p (g t) -> p g t", g=NW)
        hT = v(take(2 * IT * W), "p (s i w) -> p s i w", s=2, i=IT)
        yT_e = v(take(2 * C), "p (s c w) -> p s c w", s=2, c=2)
        ys = v(take(YS * C), "p (s c) -> p s c", s=YS)

        colc = small[0:CT, 0:4]
        c_st = v(small[:, 8:32], "p (s t n) -> p s t n", s=2, t=2)
        c_mv = v(small[:, 32:40], "p (s t n) -> p s t n", s=2, t=2)
        sd = two(small[:, 40:44])
        rs = two(small[:, 44:48])
        ss = two(small[:, 48:64])
        ksd = two(small[:, 64:80])
        krm = small[:, 80:88]
        qss = small[:, 88:96]
        kr = two(small[:, 96:112])
        shift = small[:, 128:130]
        rden = small[:, 130:132]
        var2 = small[:, 132:134]
        lr = small[:, 134:136]
        qsd = small[:, 112:120]
        qr = small[:, 120:128]

        def row(name):
            return rowv[:, ROW[name][0]:ROW[name][1]]

        def row2(name):
            return row(name).unsqueeze(1).to_broadcast([P, 2, C])

        def per_head(a, n=2 * HEADS):
            return a.unsqueeze(2).to_broadcast([P, n, DH])

        def heads8(a):
            if len(a.shape) == 3:
                a = v(a, "p t n -> p (t n)")
            return v(a, "p (g d) -> p g d", g=2 * HEADS)

        rtake, _ = region(rt)
        logits = two(rtake(2 * E))
        lexp = two(rtake(2 * E))
        cand = two(rtake(2 * E))
        hot = two(rtake(2 * E))
        rk = rtake(3 * E)
        prod = two(rtake(2 * E))
        over = rtake(E)
        xid = rtake(NX)
        exid = rtake(NX, I32)
        lmax, nlmax, lsum, wtop, top, rank, win, dtop, dx, tile_, inpos, slot = (rtake(2) for _ in range(12))

        block = stack.enter_context(nc.Block())

        cn = v(ctx[0], "(g t p) c -> g p t c", t=2, p=P)
        cT = v(ctxT, "(k p) (g n) -> g p k n", k=2, g=NCP)

        @block.sync
        def _(sp):
            def load_ctx(g, s):
                sp.dma_start(ctxn[:, s], cn[bass.ds(g, 1)].rearrange("g p t c -> p (g t) c")
                             ).then_inc(sem(f"ctx_in{s}"), 16)
                sp.dma_start(ctxt[:, s], cT[bass.ds(g, 1)].rearrange("g p k n -> p (g k) n")
                             ).then_inc(sem(f"ctx_in{s}"), 16)

            def reload(g, s):
                sp.wait_ge(sem("ctx_stats"), g + 1)
                sp.wait_ge(sem("kv_mm"), g + 1)
                load_ctx(g + 2, s)

            def copy_high(g):
                sp.wait_ge(sem("keyB_done"), 16 * (g + 1))
                sp.wait_ge(sem("keyA_in"), 16 * (g + 1))
                sp.dma_start(keyA[0:DH, :, bass.ds(g * PAIR, PAIR)], keyB[0:DH, :, bass.ds(g * PAIR, PAIR)]
                             ).then_inc(sem("keyA_in"), 16)

            sp.dma_start(wc, v(wkvT, "(k p) n -> p k n", k=2)).then_inc(sem("wc_in"), 16)
            sp.dma_start(colc, cols_ctx).then_inc(sem("wc_in"), 16)
            load_ctx(0, 0)
            load_ctx(1, 1)
            sp.dma_start(wq, v(wqT, "(k p) n -> p k n", k=2)).then_inc(sem("wq_in"), 16)
            sp.dma_start(wl, v(wlkvT, "(k p) n -> p k n", k=2)).then_inc(sem("wl_in"), 16)
            for g in range(4):
                reload(g, g % 2)
            with sp.Fori(2, NCP // 2 - 1) as it:
                for s in range(2):
                    reload(2 * it + s, s)
                    copy_high(2 * it + s - 4)
            for g in range(NCP - 6, NPAIR):
                copy_high(g)
            sp.dma_start(gw, v(gates, "(k p) n -> p k n", p=P)).then_inc(sem("gw_in"), 16)
            sp.dma_start(ow, v(outw, "(k p) n -> p k n", p=P)).then_inc(sem("ow_in"), 16)
            sp.dma_start(w1_sb, v(w1, "(k p) n -> p k n", p=P)).then_inc(sem("w1_in"), 16)
            sp.dma_start(w2_sb, v(w2, "(k p) n -> p k n", p=P)).then_inc(sem("w2_in"), 16)
            sp.dma_start(wo_at, v(woT, "(k p) n -> p k n", k=2)).then_inc(sem("woa_in"), 16)
            for e in range(NRES):
                sp.dma_start(wi_of(e), v(wi[e], "(k p) n -> p k n", p=P)).then_inc(sem(f"wi_in{e}"), 16)
            for h in range(HEADS):
                sp.wait_ge(sem("pv_done"), (h + 1) * NPAIR)
                sp.dma_start(level_pair(h), levels[:, 2 * h * P:2 * (h + 1) * P]).then_inc(sem("levels_in"), 16)
                for e in (2 * h, 2 * h + 1):
                    sp.dma_start(wo_of(e), v(wo[e], "(i p) c -> p i c", p=P)).then_inc(sem(f"wo_in{e}"), 16)
            for e in range(NRES, E):
                sp.dma_start(wi_of(e), v(wi[e], "(k p) n -> p k n", p=P)).then_inc(sem(f"wi_in{e}"), 16)
            sp.wait_ge(sem("extra_ids"), 1)
            for k in range(NX):
                ex = sp.value_load(exid[0:1, k:k + 1], min_val=0, max_val=E - 1)
                sp.wait_ge(sem("window_mm"), k + 1)
                sp.dma_start(wi_of(k), v(wi[bass.ds(ex, 1)], "e (k p) n -> p (e k) n", p=P)
                             ).then_inc(sem(f"wi_in{k}"), 16)
                sp.dma_start(wo_of(k), v(wo[bass.ds(ex, 1)], "e (i p) c -> p (e i) c", p=P)
                             ).then_inc(sem(f"wo_in{k}"), 16)
            for h in range(H2):
                sp.wait_ge(sem("y_out"), h + 1)
                sp.dma_start(v(out[0], "(h p) c -> p h c", p=P)[:, h], fin[:, h]).then_inc(sem("stored"), 16)
            sp.wait_ge(sem("stored"), 16 * H2)

        @block.gpsimd
        def _(pool):
            pool.memset(mhalf[:], -0.5)
            pool.memset(eps_c[:], LN_EPS)
            pool.memset(ones[:], 1.0)
            pool.memset(cmean, 1.0 / DC)
            pool.memset(q_max[:, :, :, DH:DH + 1], 0.0)
            pool.memset(q_max[:, :, :, DH + 1:KR], BIG)
            pool.memset(q_exp[:, :, :, DH + 1:KR], BIG)
            pool.memset(mask16, 0.0)
            pool.memset(val_flat[:, NVAL:], 0.0)
            pool.memset(val[:, :, :, DH:DH + 1], 1.0).then_inc(sem("pool_consts"), 1)

            def power(job):
                pool.wait_ge(sem("var_ready"), job + 1)
                pool.tensor_tensor(rstd[:, 2 * job:2 * job + 2], var_eps[:, 2 * job:2 * job + 2], mhalf[:], ALU.pow
                                   ).then_inc(sem("rstd_ready"), 1)

            pool.wait_ge(sem("pool_consts"), 1)
            power(0)
            power(1)
            pool.memset(qT_max, 0.0)
            pool.memset(qT_exp, 0.0)
            pool.memset(per_head_room[:, :, 0:NKEY // 2], 0.0).then_inc(sem("rows_clear"), 1)

            pool.wait_ge(sem("lat_done"), 1)
            pool.wait_ge(sem("rows_in"), 16)
            pool.tensor_tensor(xbuf[:], xbuf[:], row2("bo"), ALU.add).then_inc(sem("xbo_done"), 1)

            def low(g, s):
                pool.wait_ge(sem("hi_done"), g + 1)
                for t in range(2):
                    a = v(kh[:, s, t], "p (h d) -> p h d", h=HEADS)
                    ins = pool.tensor_tensor(k16[:, s, t, :, DH:2 * DH], a, k16[:, s, t, :, 0:DH], ALU.subtract)
                ins.then_inc(sem("lo_done"), 1)

            def scale_keys(g, s):
                pool.wait_ge(sem("kr_ready"), g + 1)
                pool.tensor_tensor(heads8(kh[:, s]), heads8(kf[:, s]), per_head(kr[:, s]), ALU.mult
                                   ).then_inc(sem("khat"), 1)

            def pool_step(g, s):
                if not isinstance(g, int) or 2 <= g < NPAIR + 2:
                    low(g - 2, s)
                if not isinstance(g, int) or 1 <= g < NPAIR + 1:
                    scale_keys(g - 1, 1 - s)

            for g in range(7):
                pool_step(g, g % 2)
            with pool.Fori(0, 4) as it:
                for k in range(2):
                    pool_step(2 * it + 7 + k, (7 + k) % 2)
            for g in range(15, NPAIR + 2):
                pool_step(g, g % 2)

            power(2)
            power(3)
            pool.wait_ge(sem("xx_ready"), 2)
            pool.tensor_tensor(res2, xx, row2("out_b"), ALU.add).then_inc(sem("xxb"), 1)
            power(4)
            pool.wait_ge(sem("gram_sb"), 1)
            pool.wait_ge(sem("levels_in"), 16 * HEADS)
            for n in range(1, NLEV - 1):
                pool.tensor_tensor(bT[:, n], gram[:, 0:3:2, :], upper(n + 1).unsqueeze(1).to_broadcast([P, 2, P]),
                                   ALU.mult).then_inc(sem("bT_ready"), 1)
            pool.tensor_tensor(x1, x1, row2("b2"), ALU.add).then_inc(sem("pool_link"), 1)
            pool.wait_ge(sem("xm_ready"), 1)
            pool.wait_ge(sem("pool_link"), 1)
            pool.tensor_tensor(x1, x1, xm, ALU.add).then_inc(sem("res_ready"), 1)
            power(5)
            power(6)
            power(7)
            pool.wait_ge(sem("xn_ready"), 2)
            pool.tensor_tensor(x2xn, x2[:], xn, ALU.add).then_inc(sem("x2xn_ready"), 1)

        @block.scalar
        def _(act):
            early = ROW["bo"][0]
            act.dma_start(xbuf[:], v(x[0], "(h p) c -> p h c", p=P)).then_inc(sem("x_in"), 16)
            act.dma_start(rowv[:, 0:early], rows[0:early].partition_broadcast(P)).then_inc(sem("rows0_in"), 16)
            act.dma_start(cst[:, 0:C_TRI], consts[:, 0:C_TRI]).then_inc(sem("ident_in"), 16)
            act.dma_start(mask8, v(mask, "o (p n) -> (o p) n", n=P)).then_inc(sem("mask_in"), 16)
            act.dma_start(rowv[:, early:], rows[early:].partition_broadcast(P)).then_inc(sem("rows_in"), 16)
            act.dma_start(cst[:, C_TRI:], consts[:, C_TRI:]).then_inc(sem("cst_in"), 16)
            act.dma_start(colv[:], cols).then_inc(sem("cols_in"), 16)
            act.dma_start(gt_sb[:], v(gateT, "(k p) n -> p k n", p=P)).then_inc(sem("gt_in"), 16)
            act.dma_start(lrw_sb[:], lrw).then_inc(sem("gt_in"), 16)
            nc.scalar.preload_act_table(ACT.Sqrt)
            act.wait_ge(sem("ident_in"), 16)
            act.activation(id16[:], ident, ACT.Copy).then_inc(sem("id16_done"), 1)

            def evac(dst, src, need, n, done):
                act.wait_ge(sem(need), n)
                act.activation(dst, src, ACT.Copy).then_inc(sem(done), 1)

            evac(bw, bank[6][:, 0:512], "bw_mm", 1, "bw_done")
            evac(v(lnT, "p a b -> p (a b)"), bank[5], "lnT_mm", 1, "lnT_done")

            def values(g, s):
                act.wait_ge(sem("kv_mm"), g + 1)
                act.wait_ge(sem("rs_ready"), g + 1)
                for t in range(2):
                    ins = act.activation(val[:, bass.ds(2 * g + t, 1), :, 0:DH].rearrange("p j h d -> p (j h) d"),
                                         v(bank[2 + s][:, t * C:(t + 1) * C], "p (h d) -> p h d", h=HEADS),
                                         ACT.Copy, scale=rs[:, s, t:t + 1])
                ins.then_inc(sem("v_done"), 1)

            def deviation(g, s):
                act.wait_ge(sem("ctx_stats"), g + 1)
                act.activation(sd[:, s], c_mv[:, s, :, 1], ACT.Sqrt, bias=eps_c[:]).then_inc(sem("sd_ready"), 1)

            def high(g, s):
                act.wait_ge(sem("khat"), g + 1)
                if not isinstance(g, int) or g >= 2:
                    act.wait_ge(sem("key_tr"), g - 1)
                for t in range(2):
                    ins = act.activation(k16[:, s, t, :, 0:DH], v(kh[:, s, t], "p (h d) -> p h d", h=HEADS), ACT.Copy)
                ins.then_inc(sem("hi_done"), 1)

            def square(g, s):
                act.wait_ge(sem("kraw"), g + 1)
                if not isinstance(g, int) or g >= 2:
                    act.wait_ge(sem("ss_ready"), g - 1)
                act.activation(ksq[:, s], v(kf[:, s], "p t n -> p (t n)"), ACT.Square).then_inc(sem("sq_ready"), 1)

            def key_norm(g, s):
                act.wait_ge(sem("ss_ready"), g + 1)
                act.activation(ksd[:, s], ss[:, s], ACT.Sqrt, scale=1.0 / (DH * RANGE * RANGE)
                               ).then_inc(sem("ksd_ready"), 1)

            def store_keys(g, s):
                act.wait_ge(sem("key_tr"), g + 1)
                act.activation(keyB[:, :, bass.ds(g * PAIR, PAIR)],
                               v(bank[4 + s].bitcast(F16), "p (h k) -> p h k", h=HEADS), ACT.Copy
                               ).then_inc(sem("keyB_done"), 16)

            def act_step(g, s):
                def has(p, n):
                    return not isinstance(p, int) or 0 <= p < n
                if has(g, NCP):
                    values(g, s)
                if has(g - 2, NPAIR):
                    high(g - 2, s)
                if has(g, NPAIR):
                    square(g, s)
                if has(g + 1, NCP):
                    deviation(g + 1, 1 - s)
                if has(g - 1, NPAIR):
                    key_norm(g - 1, 1 - s)
                if has(g - 4, NPAIR):
                    store_keys(g - 4, s)

            deviation(0, 0)
            for g in range(7):
                act_step(g, g % 2)
                if g == 1:
                    act.wait_ge(sem("q_ss"), 1)
                    act.activation(qsd, qss, ACT.Sqrt, scale=1.0 / DH).then_inc(sem("q_sd"), 1)
                    act.wait_ge(sem("rows_clear"), 1)
                    act.dma_start(keyA[DH:DH + 1], key_ones).then_inc(sem("keyA_in"), 16)
                    act.wait_ge(sem("mask16_done"), 1)
                    for h in range(HEADS):
                        act.dma_start(keyA[DH + 1:KR, h, :], mask16).then_inc(sem("mrow_in"), 16)
            with act.Fori(0, 4) as it:
                for k in range(2):
                    act_step(2 * it + 7 + k, (7 + k) % 2)
            for g in range(15, NPAIR + 4):
                act_step(g, g % 2)

            nc.scalar.preload_act_table(ACT.Exp)

            def exp_group(n, s):
                act.wait_ge(sem("s_done"), n + 1)
                if not (isinstance(n, int) and n < 2):
                    act.wait_ge(sem("pv_done"), n - 1)
                act.activation(prob[:, s], bank[s], ACT.Exp, scale=1.0 / (RANGE * RANGE)
                               ).then_inc(sem("exp_done"), 1)

            exp_group(0, 0)
            exp_group(1, 1)
            with act.Fori(1, HEADS * NPAIR // 2) as it:
                for s in range(2):
                    exp_group(2 * it + s, s)

            evac(v(oT, "p a b -> p (a b)"), bank[6], "oT_mm", 1, "oT_done")
            evac(v(nT, "p a b -> p (a b)"), bank[0], "nT_mm", 1, "nT_done")
            act.wait_ge(sem("cols_in"), 16)
            act.wait_ge(sem("q_mm"), 1)
            for a in range(2):
                act.activation(qT[:, a], bank[3][:, a * T:(a + 1) * T], ACT.Identity, bias=colv[:, a:a + 1]
                               ).then_inc(sem("qT_done"), 1)
            evac(v(knT, "p a b -> p (a b)"), bank[5], "knT_mm", 1, "knT_done")
            act.wait_ge(sem("score_mm"), 1)
            act.wait_ge(sem("lr_ready"), 1)
            for a in range(2):
                act.activation(score[:, a], bank[7][:, a * T:(a + 1) * T], ACT.Copy, scale=lr[:, a:a + 1]
                               ).then_inc(sem("score_done"), 1)
            evac(v(yT, "p a b -> p (a b)"), bank[5], "yT_mm", 1, "yT_done")
            evac(v(nT, "p a b -> p (a b)"), bank[7], "nT_mm", 2, "nT_done")
            evac(v(tokT, "p a b -> p (a b)"), bank[2], "nT_mm", 3, "nT_done")
            act.wait_ge(sem("nlmax_ready"), 1)
            for a in range(2):
                act.activation(lexp[:, a], logits[:, a], ACT.Exp, bias=nlmax[:, a:a + 1],
                               accum_out=lsum[:, a:a + 1]).then_inc(sem("lsum_ready"), 1)
            nc.scalar.preload_act_table(ACT.Gelu)
            for m, (at, n) in enumerate(XS_CUTS):
                act.wait_ge(sem("xs_mm"), 2 * m + 2)
                act.activation(xs[:, 1, at:at + n], bank[2 * m + 1][:, 0:n], ACT.Copy).then_inc(sem("xs1_done"), 1)
            for n in range(NW):
                for j in range(2):
                    act.wait_ge(sem("h_mm"), 2 * n + j + 1)
                    if n >= 2:
                        act.wait_ge(sem("window_mm"), n - 1)
                    act.activation(v(hT[:, n % 2, j * (IT // 2):(j + 1) * (IT // 2)], "p i w -> p (i w)"),
                                   bank[2 * (n % 2) + j], ACT.Gelu).then_inc(sem("gelu_done"), 1)

        @block.vector
        def _(dve):
            done = {}

            def link(ins, name="dve_link"):
                done[name] = done.get(name, 0) + 1
                ins.then_inc(sem(name), 1)
                dve.wait_ge(sem(name), done[name])

            def norm_stats(src, job):
                for a in range(2):
                    ins = dve.bn_stats(stats[:, a], src[:, a])
                link(ins)
                for a in range(2):
                    ins = dve.bn_aggr(mv[:, a], stats[:, a])
                link(ins)
                link(dve.tensor_scalar(var_eps[:, 2 * job:2 * job + 2], mv[:, :, 1], LN_EPS, None, ALU.add), "var_ready")

            def second_norm(job):
                r = rstd[:, 2 * job - 2:2 * job]
                link(dve.tensor_tensor(var2, mv[:, :, 1], r, ALU.mult))
                link(dve.tensor_tensor(var2, var2, r, ALU.mult))
                link(dve.tensor_scalar(var_eps[:, 2 * job:2 * job + 2], var2, LN_EPS, None, ALU.add), "var_ready")

            def twice_normed(src, once, twice, job, gamma, beta, once_done, twice_done):
                norm_stats(src, job)
                dve.wait_ge(sem("rstd_ready"), job + 1)
                for a in range(2):
                    ins = dve.tensor_scalar(once[:, a], src[:, a], mv[:, a, 0:1], rstd[:, 2 * job + a:2 * job + a + 1],
                                            ALU.subtract, ALU.mult)
                    link(ins, once_done)
                second_norm(job + 1)
                dve.wait_ge(sem("rstd_ready"), job + 2)
                for a in range(2):
                    r = rstd[:, 2 * job + 2 + a:2 * job + 3 + a]
                    ins = dve.scalar_tensor_tensor(twice[:, a], once[:, a], r, row(gamma), ALU.mult, ALU.mult)
                link(ins)
                link(dve.tensor_tensor(twice, twice, row2(beta), ALU.add), twice_done)

            dve.wait_ge(sem("pool_consts"), 1)
            dve.wait_ge(sem("x_in"), 16)
            norm_stats(xbuf, 0)
            dve.wait_ge(sem("wc_in"), 32)
            for k in range(2):
                ins = dve.tensor_scalar(bfree[:, k], ones[0:CT], colc[:, 2 + k:3 + k], None, ALU.mult)
            link(ins, "bfree_done")
            dve.wait_ge(sem("rstd_ready"), 1)
            for a in range(2):
                link(dve.tensor_scalar(lat[:, a], xbuf[:, a], mv[:, a, 0:1], rstd[:, a:a + 1],
                                       ALU.subtract, ALU.mult), "lat_once")
            second_norm(1)
            dve.wait_ge(sem("bw_mm"), 1)
            for k in range(2):
                ins = dve.tensor_scalar(wc[:, k], wc[:, k], colc[:, k:k + 1], None, ALU.mult)
            link(ins, "wg_done")
            dve.wait_ge(sem("rstd_ready"), 2)
            dve.wait_ge(sem("rows0_in"), 16)
            for a in range(2):
                ins = dve.scalar_tensor_tensor(lat[:, a], lat[:, a], rstd[:, 2 + a:3 + a], row("ln_l_g"),
                                               ALU.mult, ALU.mult)
            link(ins)
            link(dve.tensor_tensor(lat, lat, row2("ln_l_b"), ALU.add), "lat_done")
            dve.wait_ge(sem("cmean_mm"), 1)
            for k in range(2):
                ins = dve.tensor_tensor(wc[:, k], wc[:, k], bank[7][0:CT, 0:512], ALU.subtract)
            link(ins, "wprep_done")

            def q_squares():
                dve.wait_ge(sem("q_raw_mm"), 1)
                link(dve.tensor_copy(qf, bank[4]))
                link(dve.tensor_tensor(qsq, qf, qf, ALU.mult))
                link(dve.tensor_reduce(qss, heads8(qsq), AX.X, ALU.add), "q_ss")

            def q_split():
                dve.wait_ge(sem("q_sd"), 1)
                link(dve.tensor_scalar(qsd, qsd, RMS_EPS, None, ALU.max))
                link(dve.reciprocal(qr, qsd))
                link(dve.tensor_tensor(gqk, row("qn_g"), row("kn_g"), ALU.mult))
                link(dve.tensor_tensor(heads8(qn), heads8(qf), per_head(qr), ALU.mult))
                link(dve.tensor_tensor(heads8(qn), heads8(qn), gqk.unsqueeze(1).to_broadcast([P, 8, DH]), ALU.mult))
                for a in range(2):
                    exact = v(qn[:, a * C:(a + 1) * C], "p (h d) -> p h d", h=HEADS)
                    link(dve.tensor_copy(q_max[:, a, :, 0:DH], exact))
                    for c in range(2):
                        dve.tensor_copy(q_hh[:, a, :, c * DH:(c + 1) * DH], q_max[:, a, :, 0:DH])
                    link(dve.tensor_tensor(q_exp[:, a, :, 0:DH], exact, q_max[:, a, :, 0:DH], ALU.subtract), "q_split")

            def q_store():
                dve.wait_ge(sem("qT_mm"), 1)
                dve.wait_ge(sem("rows_clear"), 1)
                link(dve.tensor_copy(v(qT_max[0:KR], "p h t -> p (h t)"), bank[6].bitcast(F16)[0:KR, :]))
                link(dve.tensor_copy(v(qT_hh, "p h t -> p (h t)"), bank[7].bitcast(F16)), "qT_ready")

            def ctx_stats(g, s):
                dve.wait_ge(sem(f"ctx_in{s}"), 16 * (g - s) + 32)
                for t in range(2):
                    ins = dve.bn_stats(c_st[:, s, t], ctxn[:, s, t])
                ins.then_inc(sem("ctx_bn"), 1)

            def ctx_aggr(g, s):
                for t in range(2):
                    ins = dve.bn_aggr(c_mv[:, s, t], c_st[:, s, t])
                ins.then_inc(sem("ctx_stats"), 1)

            def ctx_rstd(g, s):
                dve.wait_ge(sem("sd_ready"), g + 1)
                if not (isinstance(g, int) and g < 2):
                    dve.wait_ge(sem("v_done"), g - 1)
                dve.reciprocal(rs[:, s], sd[:, s]).then_inc(sem("rs_ready"), 1)

            def raw_keys(g, s):
                dve.wait_ge(sem("kv_mm"), g + 1)
                dve.wait_ge(sem("rs_ready"), g + 1)
                if not (isinstance(g, int) and g < 2):
                    dve.wait_ge(sem("khat"), g - 1)
                    dve.wait_ge(sem("sq_ready"), g - 1)
                for t in range(2):
                    ins = dve.scalar_tensor_tensor(kf[:, s, t], bank[s][:, t * C:(t + 1) * C], rs[:, s, t:t + 1],
                                                   bw[:, 0:C], ALU.mult, ALU.add)
                ins.then_inc(sem("kraw"), 1)

            def latent_keys(g, s):
                dve.wait_ge(sem("kv_mm"), g + 1)
                dve.wait_ge(sem("khat"), g - 1)
                dve.wait_ge(sem("sq_ready"), g - 1)
                dve.tensor_copy(v(kf[:, s], "p t n -> p (t n)"), bank[s]).then_inc(sem("kraw"), 1)
                for t in range(2):
                    dve.tensor_tensor(val[:, 2 * g + t, :, 0:DH],
                                      v(bank[2 + s][:, t * C:(t + 1) * C], "p (h d) -> p h d", h=HEADS),
                                      v(bw[:, C:2 * C], "p (h d) -> p h d", h=HEADS), ALU.subtract
                                      ).then_inc(sem("vl_done"), 1)

            def sum_squares(g, s):
                dve.wait_ge(sem("sq_ready"), g + 1)
                dve.tensor_reduce(ss[:, s], heads8(ksq[:, s]), AX.X, ALU.add).then_inc(sem("ss_ready"), 1)

            def key_scale(g, s):
                dve.wait_ge(sem("ksd_ready"), g + 1)
                dve.tensor_scalar(krm, ksd[:, s], RMS_EPS / RANGE, None, ALU.max).then_inc(sem("krm_done"), 1)
                dve.wait_ge(sem("krm_done"), g + 1)
                dve.reciprocal(kr[:, s], krm).then_inc(sem("kr_ready"), 1)

            def group_max(n, i, banks, s):
                dve.wait_ge(sem("x_done"), n + 1)
                dve.tensor_reduce(pmax[:, :, bass.ds(i, 1)], v(bank[banks + s], "p (a k) -> p a k", a=2), AX.X, ALU.max
                                  ).then_inc(sem("max_done"), 1)

            def dve_step(g, s):
                def has(p, n):
                    return not isinstance(p, int) or 0 <= p < n
                if isinstance(g, int) and g == NPAIR - 1:
                    latent_keys(g, s)
                elif has(g, NCP):
                    raw_keys(g, s)
                if has(g + 1, NCP):
                    ctx_stats(g + 1, 1 - s)
                    dve.wait_ge(sem("ctx_bn"), g + 2)
                if has(g - 1, NPAIR):
                    sum_squares(g - 1, 1 - s)
                if has(g + 1, NCP):
                    ctx_aggr(g + 1, 1 - s)
                if has(g - 1, NPAIR):
                    key_scale(g - 1, 1 - s)
                if has(g + 1, NCP):
                    ctx_rstd(g + 1, 1 - s)
                if has(g - 6, NPAIR):
                    group_max(g - 6, g - 6, 6, s)

            dve.wait_ge(sem("bw_done"), 1)
            ctx_stats(0, 0)
            dve.wait_ge(sem("ctx_bn"), 1)
            ctx_aggr(0, 0)
            ctx_rstd(0, 0)
            for g in range(7):
                dve_step(g, g % 2)
                if g == 0:
                    q_squares()
                    dve.wait_ge(sem("mask_in"), 16)
                    link(dve.tensor_scalar(mask16[0:NCTX // P], mask8, BIG, -BIG, ALU.mult, ALU.add), "mask16_done")
                if g == 1:
                    q_split()
                if g == 2:
                    q_store()
            with dve.Fori(0, 4) as it:
                for k in range(2):
                    dve_step(2 * it + 7 + k, (7 + k) % 2)
            for g in range(15, NPAIR + 6):
                dve_step(g, g % 2)

            def head_shift(h):
                dve.wait_ge(sem("max_done"), NPAIR * (h + 1))
                link(dve.tensor_reduce(shift, pmax, AX.X, ALU.max))
                link(dve.tensor_scalar(q_exp[:, :, h, DH], shift, -1.0, None, ALU.mult), "shift_done")
                dve.wait_ge(sem("qe_mm"), h + 1)
                link(dve.tensor_copy(qT_exp[0:KR, h], bank[6].bitcast(F16)[0:KR, 0:T]), "qe_done")

            def head_output(h):
                dve.wait_ge(sem("pv_done"), NPAIR * (h + 1))
                acc = v(bank[4 + h % 2][:, 0:2 * VW], "p (a d) -> p a d", a=2)
                link(dve.reciprocal(rden, acc[:, :, DH]))
                for a in range(2):
                    link(dve.scalar_tensor_tensor(o_sb[:, a, h * DH:(h + 1) * DH], acc[:, a, 0:DH], rden[:, a:a + 1],
                                                  bw[:, C + h * DH:C + (h + 1) * DH], ALU.mult, ALU.add), "o_done")

            for h in range(HEADS):
                if h:
                    p = (h * NPAIR) % 2
                    with dve.Fori(0, NPAIR // 2) as it:
                        for k in range(2):
                            group_max(h * NPAIR + 2 * it + k, 2 * it + k, 2, (p + k) % 2)
                    group_max(h * NPAIR + NPAIR - 1, NPAIR - 1, 2, p)
                head_shift(h)
                if h:
                    head_output(h - 1)
            head_output(HEADS - 1)

            def flat(a):
                return v(a, "p a b -> p (a b)")

            dve.wait_ge(sem("att_mm"), 1)
            dve.wait_ge(sem("xbo_done"), 1)
            dve.wait_ge(sem("rows_in"), 16)
            link(dve.tensor_tensor(flat(x1), bank[7], flat(xbuf[:]), ALU.add))
            twice_normed(x1, xx, nrm, 2, "dn_g", "dn_b", "xx_ready", "nrm_done")
            dve.wait_ge(sem("k_mm"), 1)
            link(dve.tensor_tensor(kd, two(bank[1]), row2("gates_bk"), ALU.add))
            link(dve.tensor_tensor(vd, kd, kd, ALU.mult))
            link(dve.tensor_reduce(var_eps[:, 8:10], vd, AX.X, ALU.add), "var_ready")
            dve.wait_ge(sem("v_mm"), 1)
            link(dve.tensor_tensor(vd, two(bank[2]), row2("gates_bv"), ALU.add), "vd_ready")
            link(dve.tensor_tensor(lr, bank[4][:, 0:2], row("lr_b").to_broadcast([P, 2]), ALU.add), "lr_ready")
            dve.wait_ge(sem("rstd_ready"), 5)
            for a in range(2):
                ins = dve.tensor_scalar(kd[:, a], kd[:, a], rstd[:, 8 + a:9 + a], None, ALU.mult)
            link(ins, "kn_done")
            dve.wait_ge(sem("gram_mm"), 1)
            link(dve.tensor_copy(v(gram, "p b n -> p (b n)"), bank[6][:, 0:3 * P]), "gram_sb")
            diag = gram[:, 0:3:2, :]
            dve.wait_ge(sem("levels_in"), 16 * HEADS)

            def both(m):
                return m.unsqueeze(1).to_broadcast([P, 2, P])

            link(dve.tensor_tensor(lv, diag, both(lower1), ALU.mult))
            link(dve.tensor_tensor(X, both(ident), lv, ALU.subtract))
            link(dve.tensor_tensor(lv, diag, both(upper(0)), ALU.mult))
            link(dve.tensor_tensor(XT, both(ident), lv, ALU.subtract))
            link(dve.tensor_tensor(bT[:, 0], diag, both(upper(1)), ALU.mult), "level0")
            for n in range(NLEV - 1):
                dve.wait_ge(sem("t1_mm"), n + 1)
                link(dve.tensor_copy(flat(T1), bank[0][:, 0:2 * P]), "t1_done")
                dve.wait_ge(sem("xx_mm"), n + 1)
                if n < NLEV - 2:
                    link(dve.tensor_tensor(flat(X), flat(X), bank[1][:, 0:2 * P], ALU.subtract), "x_next")
                link(dve.tensor_tensor(flat(XT), flat(XT), bank[2][:, 0:2 * P], ALU.subtract), "xt_next")
            dve.wait_ge(sem("u1_mm"), 1)
            link(dve.tensor_copy(u[:, 0], bank[3][:, 0:C]), "u_done")
            dve.wait_ge(sem("u01_mm"), 1)
            link(dve.tensor_tensor(vd[:, 1], vd[:, 1], bank[4][:, 0:C], ALU.subtract), "vd_ready")
            dve.wait_ge(sem("u2_mm"), 1)
            link(dve.tensor_copy(u[:, 1], bank[3][:, C:2 * C]), "u_done")
            dve.wait_ge(sem("xxb"), 1)
            dve.wait_ge(sem("delta_mm"), 1)
            link(dve.tensor_tensor(flat(xm), bank[6], flat(res2), ALU.add), "xm_ready")
            norm_stats(xm, 5)
            for a in range(2):
                ins = dve.scalar_tensor_tensor(nrm[:, a], xm[:, a], mv[:, a, 0:1], row("mn_g"),
                                               ALU.subtract, ALU.mult)
            link(ins)
            dve.wait_ge(sem("rstd_ready"), 6)
            for a in range(2):
                ins = dve.scalar_tensor_tensor(nrm[:, a], nrm[:, a], rstd[:, 10 + a:11 + a], row("mn_b"),
                                               ALU.mult, ALU.add)
            link(ins, "nrm_done")
            dve.wait_ge(sem("hm_mm"), 1)
            for a in range(2):
                ins = dve.tensor_scalar(hm[:, a], bank[0][:, a * T:(a + 1) * T], colv[:, 2 + a:3 + a], 0.0,
                                        ALU.add, ALU.max)
            link(ins, "hm_done")
            dve.wait_ge(sem("mlp_mm"), 1)
            dve.wait_ge(sem("res_ready"), 1)
            link(dve.tensor_tensor(flat(x2[:]), bank[1], flat(x1), ALU.add))

            dve.wait_ge(sem("cst_in"), 16)
            twice_normed(x2, xn, tok, 6, "ffn_g", "ffn_b", "xn_ready", "tok_done")
            dve.wait_ge(sem("logit_mm"), 1)
            link(dve.tensor_copy(flat(logits), bank[3][:, 0:2 * E]))
            link(dve.tensor_reduce(lmax, logits, AX.X, ALU.max))
            link(dve.tensor_scalar(nlmax, lmax, -1.0, None, ALU.mult), "nlmax_ready")
            for a in range(2):
                ins = dve.tensor_scalar(cand[:, a], logits[:, a], lmax[:, a:a + 1], 100.0, ALU.is_lt, ALU.mult)
            link(ins)
            iota_e = iota[:, 0:E]
            link(dve.tensor_tensor(cand, cand, iota_e.unsqueeze(1).to_broadcast([P, 2, E]), ALU.add))
            link(dve.tensor_reduce(top, cand, AX.X, ALU.min))
            for a in range(2):
                ins = dve.tensor_scalar(hot[:, a], iota_e, top[:, a:a + 1], None, ALU.is_equal)
            link(ins, "hot_done")
            dve.wait_ge(sem("lsum_ready"), 2)
            link(dve.reciprocal(wtop, lsum))
            dve.wait_ge(sem("rank_mm"), 1)
            link(dve.tensor_copy(rk, bank[4][:, 0:3 * E]))
            link(dve.tensor_tensor(prod, two(rk[:, 0:2 * E]), hot, ALU.mult))
            link(dve.tensor_reduce(rank, prod, AX.X, ALU.add))
            n_e = rk[:, 2 * E:3 * E]
            link(dve.tensor_scalar(over, n_e, float(W), None, ALU.is_gt))
            link(dve.tensor_tensor(over, over, iota_e, ALU.mult))
            link(dve.tensor_reduce(xid, over, AX.X, ALU.add))
            link(dve.tensor_copy(exid, xid), "extra_ids")
            link(dve.tensor_scalar(win, rank, float(W), None, ALU.is_ge))
            link(dve.tensor_scalar(dtop, top, -1.0, float(E), ALU.mult, ALU.add))
            link(dve.tensor_tensor(dx, dtop, win, ALU.mult))
            link(dve.tensor_tensor(tile_, dx, top, ALU.add))
            link(dve.scalar_tensor_tensor(inpos, win, -float(W), rank, ALU.mult, ALU.add))
            link(dve.scalar_tensor_tensor(slot, tile_, float(W), inpos, ALU.mult, ALU.add))
            for a in range(2):
                link(dve.tensor_scalar(sel[:, a], iota, slot[:, a:a + 1], None, ALU.is_equal), "sel_done")
            for m, (at, n) in enumerate(XS_CUTS):
                dve.wait_ge(sem("xs_mm"), 2 * m + 1)
                link(dve.tensor_copy(xs[:, 0, at:at + n], bank[2 * m][:, 0:n]), "xs0_done")

            def store_selT(q):
                n = min(2, NW - 2 * q)
                dve.wait_ge(sem("selT_mm"), q + 1)
                link(dve.tensor_copy(v(selT[:, 2 * q:2 * q + n], "p g t -> p (g t)"), bank[6 + q % 2][:, 0:n * T]),
                     "selT_done")

            store_selT(0)
            for n in range(NW):
                if 1 <= n <= NW // 2:
                    store_selT(n)
                y = bank[4 + n % 2]
                dve.wait_ge(sem("window_mm"), n + 1)
                if n >= 2:
                    dve.wait_ge(sem("y_tr"), n - 1)
                link(dve.tensor_copy(v(yT_e[:, n % 2], "p c w -> p (c w)"), y[:, 0:C]), "yTe_done")
                dve.wait_ge(sem("y_tr"), n + 1)
                if n >= YS:
                    dve.wait_ge(sem("back_mm"), n - YS + 1)
                link(dve.tensor_copy(ys[:, n % YS], y[:, C:2 * C]), "ys_done")
            dve.wait_ge(sem("x2xn_ready"), 1)
            dve.wait_ge(sem("back_mm"), NW)
            for a in range(2):
                dve.scalar_tensor_tensor(fin[:, a], bank[6][:, a * C:(a + 1) * C], wtop[:, a:a + 1], x2xn[:, a],
                                         ALU.mult, ALU.add).then_inc(sem("y_out"), 1)

        @block.tensor
        def _(pe):
            def turn(dst, src, need, n, done):
                pe.wait_ge(sem(need), n)
                for c in range(2):
                    for a in range(2):
                        ins = pe.transpose(dst[:, c * T + a * P:c * T + (a + 1) * P], src[:, a, c * P:(c + 1) * P],
                                           ident)
                ins.then_inc(sem(done), 1)

            def product(dst, lhsT, rhs):
                n = len(lhsT)
                for k in range(n):
                    ins = pe.matmul(dst, lhsT[k], rhs[k], start=k == 0, stop=k == n - 1)
                return ins

            def by_token(dst, src, w):
                n = w.shape[2]
                for a in range(2):
                    ins = product(dst[:, a * n:(a + 1) * n], [src[:, k, a * P:(a + 1) * P] for k in range(2)],
                                  [w[:, k] for k in range(2)])
                return ins

            def by_channel(dst, src, w):
                for a in range(2):
                    ins = product(dst[:, a * T:(a + 1) * T], [w[:, k, a * P:(a + 1) * P] for k in range(2)],
                                  [src[:, k] for k in range(2)])
                return ins

            pe.wait_ge(sem("bfree_done"), 1)
            product(bank[6], [bfree[:, k] for k in range(2)], [wc[:, k] for k in range(2)]).then_inc(sem("bw_mm"), 1)
            pe.wait_ge(sem("wg_done"), 1)
            product(bank[7][0:CT], [cmean] * 2, [wc[:, k] for k in range(2)]).then_inc(sem("cmean_mm"), 1)
            pe.wait_ge(sem("ident_in"), 16)
            turn(bank[5], lat, "lat_done", 1, "lnT_mm")
            pe.wait_ge(sem("lnT_done"), 1)
            pe.wait_ge(sem("wq_in"), 16)
            by_token(bank[4], lnT, wq).then_inc(sem("q_raw_mm"), 1)
            pe.wait_ge(sem("wprep_done"), 1)
            pe.wait_ge(sem("bw_done"), 1)

            def turn_q():
                pe.wait_ge(sem("q_split"), 2)
                pe.wait_ge(sem("id16_done"), 1)
                for src, dst, n in ((q_max, bank[6], KR), (q_hh, bank[7], P)):
                    for h in range(HEADS):
                        for a in range(2):
                            ins = pe.transpose(dst.bitcast(F16)[0:n, h * T + a * P:h * T + (a + 1) * P],
                                               src[:, a, h, :], id16[:])
                ins.then_inc(sem("qT_mm"), 1)

            def keys_values(g, s):
                if isinstance(g, int) and g == NPAIR - 1:
                    pe.wait_ge(sem("wl_in"), 16)
                    src, w = lnT, wl
                else:
                    pe.wait_ge(sem(f"ctx_in{s}"), 16 * (g - s) + 32)
                    src, w = ctxt[:, s], wc
                if not (isinstance(g, int) and g < 2):
                    pe.wait_ge(sem("kraw"), g - 1)
                    pe.wait_ge(sem("v_done"), g - 1)
                for t in range(2):
                    mine = [src[:, k, t * P:(t + 1) * P] for k in range(2)]
                    product(bank[s][:, t * C:(t + 1) * C], mine, [w[:, k, 0:C] for k in range(2)])
                    ins = product(bank[2 + s][:, t * C:(t + 1) * C], mine, [w[:, k, C:2 * C] for k in range(2)])
                ins.then_inc(sem("kv_mm"), 1)

            def turn_keys(g, s):
                pe.wait_ge(sem("lo_done"), g + 1)
                if not (isinstance(g, int) and g < 2):
                    pe.wait_ge(sem("keyB_done"), 16 * (g - 1))
                for h in range(HEADS):
                    for t in range(2):
                        ins = pe.transpose(bank[4 + s].bitcast(F16)[:, h * PAIR + t * P:h * PAIR + (t + 1) * P],
                                           k16[:, s, t, h, :], id16[:])
                ins.then_inc(sem("key_tr"), 1)

            def max_scores(h, i, n, banks, s):
                if not (isinstance(n, int) and n < 2):
                    pe.wait_ge(sem("max_done"), n - 1)
                for a in range(2):
                    ins = pe.matmul(bank[banks + s][:, a * T:(a + 1) * T], qT_max[:, h, a * P:(a + 1) * P],
                                    keyA[:, h, bass.ds(i * PAIR, PAIR)], start=True, stop=True)
                ins.then_inc(sem("x_done"), 1)

            def pe_step(g, s):
                def has(p, n):
                    return not isinstance(p, int) or 0 <= p < n
                if has(g, NPAIR):
                    keys_values(g, s)
                if has(g - 3, NPAIR):
                    turn_keys(g - 3, 1 - s)
                if has(g - 6, NPAIR):
                    pe.wait_ge(sem("keyA_in"), 16 * (g - 6) + 32)
                    max_scores(0, g - 6, g - 6, 6, s)

            for g in range(7):
                pe_step(g, g % 2)
                if g == 2:
                    turn_q()
                if g == 4:
                    pe.wait_ge(sem("qT_ready"), 1)
                    pe.wait_ge(sem("mrow_in"), 16 * HEADS)
            with pe.Fori(0, 4) as it:
                for k in range(2):
                    pe_step(2 * it + 7 + k, (7 + k) % 2)
            for g in range(15, NPAIR + 6):
                pe_step(g, g % 2)

            def scores(h, i, n, s):
                if not (isinstance(n, int) and n < 2):
                    pe.wait_ge(sem("exp_done"), n - 1)
                for t in range(2):
                    at = bass.ds(i * PAIR + t * P, P)
                    pe.matmul(bank[s][:, t * T:(t + 1) * T], keyA[:, h, at], qT_exp[:, h], start=True, stop=False)
                    ins = pe.matmul(bank[s][:, t * T:(t + 1) * T], keyB[:, h, at], qT_hh[:, h],
                                    start=False, stop=True)
                ins.then_inc(sem("s_done"), 1)

            def weighted_values(h, i, n, s, first=False, last=False):
                pe.wait_ge(sem("exp_done"), n + 1)
                for t in range(2):
                    for a in range(2):
                        ins = pe.matmul(bank[4 + h % 2][:, a * VW:(a + 1) * VW],
                                        prob[:, s, t * T + a * P:t * T + (a + 1) * P],
                                        val_flat[:, bass.ds((2 * i + t) * HEADS * (DH + 1) + h * (DH + 1), VW)],
                                        start=first and t == 0 and a == 0, stop=last and t == 1,
                                        skip_group_check=True)
                ins.then_inc(sem("pv_done"), 1)

            pe.wait_ge(sem("vl_done"), 2)
            for h in range(HEADS):
                base = h * NPAIR
                pe.wait_ge(sem("shift_done"), h + 1)
                for a in range(2):
                    ins = pe.transpose(bank[6].bitcast(F16)[0:KR, a * P:(a + 1) * P], q_exp[:, a, h, :], id16[:])
                ins.then_inc(sem("qe_mm"), 1)
                pe.wait_ge(sem("qe_done"), h + 1)
                if h >= 2:
                    pe.wait_ge(sem("o_done"), 2 * (h - 1))

                def group(i, s, before=None, last=False):
                    scores(h, i, base + i, s)
                    if h + 1 < HEADS:
                        max_scores(h + 1, i, base + NPAIR + i, 2, 1 - s)
                    if before is not None:
                        weighted_values(h, before, base + before, 1 - s, first=isinstance(before, int) and before == 0)

                s0 = base % 2
                group(0, s0)
                group(1, 1 - s0, before=0)
                with pe.Fori(1, NPAIR // 2) as it:
                    for k in range(2):
                        i = 2 * it + k
                        group(i, (s0 + k) % 2, before=i - 1)
                group(NPAIR - 1, (s0 + NPAIR - 1) % 2, before=NPAIR - 2)
                weighted_values(h, NPAIR - 1, base + NPAIR - 1, (s0 + NPAIR - 1) % 2, last=True)

            turn(bank[6], o_sb, "o_done", 2 * HEADS, "oT_mm")
            pe.wait_ge(sem("oT_done"), 1)
            pe.wait_ge(sem("woa_in"), 16)
            by_token(bank[7], oT, wo_at).then_inc(sem("att_mm"), 1)

            turn(bank[0], nrm, "nrm_done", 1, "nT_mm")
            pe.wait_ge(sem("nT_done"), 1)
            pe.wait_ge(sem("gw_in"), 16)
            by_token(bank[1], nT, gw[:, :, C:2 * C]).then_inc(sem("k_mm"), 1)
            by_channel(bank[3], nT, gw[:, :, 0:C]).then_inc(sem("q_mm"), 1)
            by_token(bank[2], nT, gw[:, :, 2 * C:3 * C])
            pe.wait_ge(sem("gt_in"), 32)
            by_token(bank[4], nT, lrw_sb[:].unsqueeze(2)).then_inc(sem("v_mm"), 1)
            turn(bank[5], kd, "kn_done", 1, "knT_mm")
            pe.wait_ge(sem("knT_done"), 1)
            product(bank[6][:, 0:T], [knT[:, k, 0:P] for k in range(2)], [knT[:, k] for k in range(2)])
            product(bank[6][:, T:T + P], [knT[:, k, P:T] for k in range(2)], [knT[:, k, P:T] for k in range(2)]
                    ).then_inc(sem("gram_mm"), 1)
            pe.wait_ge(sem("qT_done"), 2)
            by_channel(bank[7], qT, knT).then_inc(sem("score_mm"), 1)
            for n in range(NLEV - 1):
                if n == 0:
                    pe.wait_ge(sem("level0"), 1)
                else:
                    pe.wait_ge(sem("bT_ready"), n)
                    pe.wait_ge(sem("x_next"), n)
                for b in range(2):
                    ins = pe.matmul(bank[0][:, b * P:(b + 1) * P], bT[:, n, b], X[:, b], start=True, stop=True)
                ins.then_inc(sem("t1_mm"), 1)
                pe.wait_ge(sem("t1_done"), n + 1)
                if n:
                    pe.wait_ge(sem("xt_next"), n)
                for b in range(2):
                    if n < NLEV - 2:
                        pe.matmul(bank[1][:, b * P:(b + 1) * P], XT[:, b], T1[:, b], start=True, stop=True)
                for b in range(2):
                    ins = pe.matmul(bank[2][:, b * P:(b + 1) * P], T1[:, b], XT[:, b], start=True, stop=True)
                ins.then_inc(sem("xx_mm"), 1)
            pe.wait_ge(sem("xt_next"), NLEV - 1)
            pe.matmul(bank[3][:, 0:C], XT[:, 0], vd[:, 0], start=True, stop=True).then_inc(sem("u1_mm"), 1)
            pe.wait_ge(sem("u_done"), 1)
            pe.matmul(bank[4][:, 0:C], gram[:, 1], u[:, 0], start=True, stop=True).then_inc(sem("u01_mm"), 1)
            pe.wait_ge(sem("vd_ready"), 2)
            pe.matmul(bank[3][:, C:2 * C], XT[:, 1], vd[:, 1], start=True, stop=True).then_inc(sem("u2_mm"), 1)
            pe.wait_ge(sem("u_done"), 2)
            pe.wait_ge(sem("score_done"), 2)
            by_channel(bank[5], score, u).then_inc(sem("yT_mm"), 1)
            pe.wait_ge(sem("yT_done"), 1)
            pe.wait_ge(sem("ow_in"), 16)
            by_token(bank[6], yT, ow).then_inc(sem("delta_mm"), 1)
            turn(bank[7], nrm, "nrm_done", 2, "nT_mm")
            pe.wait_ge(sem("nT_done"), 2)
            pe.wait_ge(sem("w1_in"), 16)
            by_channel(bank[0], nT, w1_sb).then_inc(sem("hm_mm"), 1)
            pe.wait_ge(sem("hm_done"), 1)
            pe.wait_ge(sem("w2_in"), 16)
            by_token(bank[1], hm, w2_sb).then_inc(sem("mlp_mm"), 1)

            turn(bank[2], tok, "tok_done", 1, "nT_mm")
            pe.wait_ge(sem("nT_done"), 3)
            by_token(bank[3], tokT, gt_sb[:]).then_inc(sem("logit_mm"), 1)
            pe.wait_ge(sem("hot_done"), 1)
            product(bank[4][:, 0:E], [tri], [hot[:, 0]])
            product(bank[4][:, E:2 * E], [ones[:], tri], [hot[:, 0], hot[:, 1]])
            product(bank[4][:, 2 * E:3 * E], [ones[:], ones[:]], [hot[:, 0], hot[:, 1]]).then_inc(sem("rank_mm"), 1)
            pe.wait_ge(sem("sel_done"), 2)
            for m, (at, n) in enumerate(XS_CUTS):
                for c in range(2):
                    product(bank[2 * m + c][:, 0:n], [tok[:, a, c * P:(c + 1) * P] for a in range(2)],
                            [sel[:, a, at:at + n] for a in range(2)]).then_inc(sem("xs_mm"), 1)

            def turn_sel(q):
                n = min(2, NW - 2 * q)
                if q >= 2:
                    pe.wait_ge(sem("selT_done"), q - 1)
                for j in range(n):
                    for a in range(2):
                        ins = pe.transpose(bank[6 + q % 2][:, j * T + a * P:j * T + (a + 1) * P],
                                           sel[:, a, (2 * q + j) * P:(2 * q + j + 1) * P], ident)
                ins.then_inc(sem("selT_mm"), 1)

            turn_sel(0)
            turn_sel(1)

            def first_product(n):
                e = n if n < E else 0
                pe.wait_ge(sem(f"wi_in{e}"), 16 if n < E else 32)
                if n == 0:
                    pe.wait_ge(sem("xs0_done"), len(XS_CUTS))
                    pe.wait_ge(sem("xs1_done"), len(XS_CUTS))
                if n >= 2:
                    pe.wait_ge(sem("gelu_done"), 2 * (n - 1))
                for i in range(IT):
                    b = bank[2 * (n % 2) + i // (IT // 2)]
                    at = i % (IT // 2) * W
                    ins = product(b[:, at:at + W], [wi_of(e)[:, k, i * P:(i + 1) * P] for k in range(2)],
                                  [xs[:, k, n * W:(n + 1) * W] for k in range(2)])
                    if i % (IT // 2) == IT // 2 - 1:
                        ins.then_inc(sem("h_mm"), 1)

            def second_product(n):
                e = n if n < E else 0
                pe.wait_ge(sem(f"wo_in{e}"), 16 if n < E else 32)
                pe.wait_ge(sem("gelu_done"), 2 * n + 2)
                if n >= 2:
                    pe.wait_ge(sem("ys_done"), n - 1)
                for c in range(2):
                    ins = product(bank[4 + n % 2][:, c * W:(c + 1) * W],
                                  [wo_of(e)[:, i, c * P:(c + 1) * P] for i in range(IT)],
                                  [hT[:, n % 2, i] for i in range(IT)])
                ins.then_inc(sem("window_mm"), 1)

            def turn_out(n):
                pe.wait_ge(sem("yTe_done"), n + 1)
                for c in range(2):
                    ins = pe.transpose(bank[4 + n % 2][:, C + c * P:C + (c + 1) * P], yT_e[:, n % 2, c], ident)
                ins.then_inc(sem("y_tr"), 1)

            def back(n):
                pe.wait_ge(sem("ys_done"), n + 1)
                if n == 0:
                    pe.wait_ge(sem("selT_done"), (NW + 1) // 2)
                for a in range(2):
                    ins = pe.matmul(bank[6][:, a * C:(a + 1) * C], selT[:, n, a * P:(a + 1) * P], ys[:, n % YS],
                                    start=n == 0 and a == 0, stop=n == NW - 1, skip_group_check=True)
                ins.then_inc(sem("back_mm"), 1)

            first_product(0)
            for n in range(NW):
                if n + 1 < NW:
                    first_product(n + 1)
                second_product(n)
                if n >= 1:
                    turn_out(n - 1)
                if n + 2 <= NW // 2:
                    turn_sel(n + 2)
                if n >= NW // 2:
                    for m in range(0 if n == NW // 2 else n - 1, n):
                        back(m)
            turn_out(NW - 1)
            back(NW - 1)


_OUTS = [((1, T, C), 'float32')]


def kernel(**inputs):
    import numpy as _np
    import concourse.bacc as _bacc
    from concourse import mybir as _mybir
    from concourse.bass_utils import run_bass_kernel_spmd as _run

    g = {k: _np.asarray(a) for k, a in inputs.items()}
    gb = g["L0_attn_gates_b"]
    vec = {"ln_l_g": g["L0_xattn_ln_l_g"], "ln_l_b": g["L0_xattn_ln_l_b"], "qn_g": g["L0_xattn_qn_g"],
           "kn_g": g["L0_xattn_kn_g"], "bo": g["L0_xattn_bo"], "dn_g": g["L0_attn_dn_g"], "dn_b": g["L0_attn_dn_b"],
           "gates_bk": gb[C:2 * C], "gates_bv": gb[2 * C:3 * C], "lr_b": g["L0_attn_lr_b"],
           "out_b": g["L0_attn_out_b"], "mn_g": g["L0_attn_mn_g"], "mn_b": g["L0_attn_mn_b"],
           "b2": g["L0_attn_b2"], "ffn_g": g["L0_ffn_ln_gamma"], "ffn_b": g["L0_ffn_ln_beta"]}
    r, c = _np.arange(P)[:, None], _np.arange(P)[None, :]
    consts = _np.zeros((P, NCONST), _np.float32)
    levels = _np.zeros((P, (NLEV + 1) * P), _np.float32)
    for n in range(NLEV):
        s = 1 << n
        below = (r // (2 * s) == c // (2 * s)) & (r // s % 2 == 1) & (c // s % 2 == 0)
        levels[:, (1 + n) * P:(2 + n) * P] = below.T
        if n == 0:
            levels[:, 0:P] = below
    consts[:, C_ID:C_ID + P] = r == c
    consts[:, C_TRI:C_TRI + P] = r < c
    consts[:, C_IOTA:] = _np.arange(SLOTS)
    arrays_in = {
        "x": g["x"], "ctx": g["ctx_768"], "ctxT": g["ctx_768"][0].T, "mask": g["mask_BxS2_bk0"],
        "wkvT": g["L0_xattn_Wkv"].T, "wqT": g["L0_xattn_Wq"].T, "wlkvT": g["L0_xattn_Wlkv"].T,
        "woT": g["L0_xattn_Wo"].T, "gates": g["L0_attn_gates_w"], "lrw": g["L0_attn_lr_w"].reshape(2, P).T,
        "outw": g["L0_attn_out_w"], "w1": g["L0_attn_w1"], "w2": g["L0_attn_w2"],
        "gateT": g["L0_ffn_gate_weight"].T, "wi": g["L0_ffn_wi"], "wo": g["L0_ffn_wo"],
        "rows": _np.concatenate([vec[k] for k in ROW]),
        "cols": _np.concatenate([gb[0:C].reshape(2, P), g["L0_attn_b1"].reshape(2, P)]).T,
        "cols_ctx": _np.concatenate([g["L0_xattn_ln_x_g"].reshape(2, CT), g["L0_xattn_ln_x_b"].reshape(2, CT)]).T,
        "consts": consts, "levels": levels, "key_ones": _np.ones((1, HEADS, NKEY), _np.float16),
    }
    nc = _bacc.Bacc("TRN2", target_bir_lowering=False, num_devices=1)
    arrays, args = {}, []
    for name, a in arrays_in.items():
        a = _np.ascontiguousarray(a)
        arrays[f"in_{name}_dram"] = a
        args.append(nc.dram_tensor(f"in_{name}_dram", a.shape, _mybir.dt.from_np(a.dtype), kind="ExternalInput").ap())
    for i, (shape, dtype) in enumerate(_OUTS):
        dt = _mybir.dt.from_np(_np.dtype(dtype))
        args.append(nc.dram_tensor(f"out_{i}_dram", shape, dt, kind="ExternalOutput").ap())
    perceiver_layer(nc, *args)
    r = _run(nc, [arrays], core_ids=[0])
    return r.results[0]["out_0_dram"]
```

```python
import math
from contextlib import ExitStack

import concourse.bass as bass
from concourse import mybir

F32 = mybir.dt.float32
F16 = mybir.dt.float16
I32 = mybir.dt.int32
U8 = mybir.dt.uint8
ALU = mybir.AluOpType
ACT = mybir.ActivationFunctionType
AX = mybir.AxisListType

P = 128
T = 256
C = 256
H2 = T // P
NCTX = 4096
DC = 192
CT = DC // 2
HEADS = 4
DH = 64
NKEY = NCTX + T
PAIR = 2 * P
NCP = NCTX // PAIR
NPAIR = NKEY // PAIR
KR = DH + 2
LN_EPS = 1e-5
R_LAT, R_DN, R_DN1, R_KEY, R_MN, R_FFN, R_FFN1 = range(7)
RMS_EPS = 1e-8
RANGE = 8.0
BIG = 30000.0
E = 8
I = 1024
IT = I // P
W = 128
NX = (T - 1) // W
NW = E + NX
SLOTS = NW * W
NRES = 3
YS = NW // 2
assert W == P and NX == 1
V1, VL = DH, DH + 1
VD = 2 * (DH + 1)
P_SLOTS = 4
P_SCALE_LOG = 11 * math.log(2.0)
LATE = 4
LAG = 3

ROW = {}
_at = 0
for _n, _w in (("ln_l_g", C), ("ln_l_b", C), ("qn_g", DH), ("kn_g", DH), ("bo", C), ("dn_g", C), ("dn_b", C),
               ("gates_bv", C), ("lr_b", 1), ("out_b", C), ("mn_g", C), ("mn_b", C), ("b2", C),
               ("ffn_g", C), ("ffn_b", C)):
    ROW[_n] = (_at, _at + _w)
    _at += _w
NROW = _at
NLEV = 7
C_ID = 0
C_TRI = C_ID + P
C_IOTA = C_TRI + P
NCONST = C_IOTA + SLOTS
XS_CUTS = [(at, min(512, SLOTS - at)) for at in range(0, SLOTS, 512)]


def perceiver_layer(nc, x, ctx, ctxT, mask, wkvT, wqT, wlkvT, woT, gates, lrw, outw, w1, w2, gateT, wi, wo,
                    rows, cols, cols_ctx, consts, levels, key_ones, out):
    with ExitStack() as stack:
        def sb(name, shape, dt=F32):
            return stack.enter_context(nc.sbuf_tensor(name, shape, dt))

        sems = {}

        def sem(name):
            if name not in sems:
                sems[name] = stack.enter_context(nc.semaphore(name))
            return sems[name]

        bank = [stack.enter_context(nc.psum_tensor(f"bank{i}", [P, 512], F32))[:] for i in range(8)]

        def region(tensor, at=0):
            pos = [at]

            def take(cols, dt=F32, parts=P):
                n = cols if dt in (F32, I32) else cols // 2
                a = tensor[0:parts, pos[0]:pos[0] + n]
                pos[0] += n
                assert pos[0] <= tensor.shape[1], (pos, tensor.shape)
                return a if dt == F32 else a.bitcast(dt)
            return take, pos

        def v(ap, spec, /, **dims):
            return ap.rearrange(spec, **dims)

        def two(a):
            return a.rearrange("p (a b) -> p a b", a=2)

        rowv = sb("rowv", [P, NROW])
        colv = sb("colv", [P, 6])
        cst = sb("cst", [P, NCONST])
        ident = cst[:, C_ID:C_ID + P]
        tri = cst[:, C_TRI:C_TRI + P]
        iota = cst[:, C_IOTA:C_IOTA + SLOTS]
        id16 = sb("id16", [P, P], F16)
        ones = sb("ones", [P, P])
        ones16 = sb("ones16", [P, P], F16)
        tri16 = sb("tri16", [P, P], F16)
        xbuf = sb("xbuf", [P, H2, C])
        var_eps = sb("var_eps", [P, 16])
        rstd = sb("rstd", [P, 16])
        mhalf = sb("mhalf", [P, 2])
        stats = sb("stats", [P, H2, 6])
        mv = sb("mv", [P, H2, 2])
        eps_c = sb("eps_c", [P, 1])
        gt_sb = sb("gt_sb", [P, 2, E])
        lrw_sb = sb("lrw_sb", [P, 2])
        small = sb("small", [P, 140])
        rt = sb("rt", [P, 232])
        wi_res = sb("wi_res", [P, NRES, H2, I])

        R = sb("R", [P, HEADS * NKEY + (E - NRES) * H2 * I])
        take, _ = region(R)
        key16 = v(take(HEADS * 2 * NKEY, F16), "p (h o k) -> p h o k", h=HEADS, o=2)
        keyA = key16[:, :, 0]
        keyB = key16[:, :, 1]
        val16 = v(take(2 * NPAIR * HEADS * VD, F16), "p (j h d) -> p j h d", h=HEADS, d=VD)
        per_head_room = v(R[:, 0:HEADS * NKEY], "p (h n) -> p h n", h=HEADS)

        def wo_of(e):
            return v(per_head_room[:, e // 2, (e % 2) * IT * C:(e % 2 + 1) * IT * C], "p (i c) -> p i c", i=IT)

        def level_pair(h):
            return per_head_room[:, h, 2 * IT * C:2 * IT * C + 2 * P]

        def level(n):
            return level_pair(n // 2)[:, (n % 2) * P:(n % 2 + 1) * P]

        lower1 = level(0)

        def upper(n):
            return level(n + 1)

        wi_late = v(R[:, HEADS * NKEY:], "p (e k n) -> p e k n", e=E - NRES, k=H2)

        def wi_of(e):
            return wi_res[:, e] if e < NRES else wi_late[:, e - NRES]

        S = sb("S", [P, 13184])
        take, pos = region(S)
        ctxn = v(take(2 * 2 * DC), "p (s t c) -> p s t c", s=2, t=2)
        ctxt = v(take(2 * 2 * PAIR, parts=CT), "p (s k n) -> p s k n", s=2, k=2)
        wc = two(take(2 * 512, parts=CT))
        wq = two(take(2 * C))
        wl = two(take(2 * 512))
        bw = take(512)
        KEY_STAGE = pos[0]
        kf = v(take(2 * 512), "p (s t n) -> p s t n", s=2, t=2)
        ksq = v(take(2 * 512), "p (s n) -> p s n", s=2)
        kh = v(take(2 * 512), "p (s t n) -> p s t n", s=2, t=2)
        k16 = v(take(2 * 2 * HEADS * P, F16), "p (s t h d) -> p s t h d", s=2, t=2, h=HEADS)
        qT_max = v(take(HEADS * T, F16), "p (h t) -> p h t", h=HEADS)
        qT_exp = v(take(HEADS * T, F16), "p (h t) -> p h t", h=HEADS)
        qT_hh = v(take(HEADS * T, F16), "p (h t) -> p h t", h=HEADS)
        q_exp = v(take(H2 * HEADS * KR, F16), "p (a h d) -> p a h d", a=H2, h=HEADS)
        mask8 = take(P // 4)[0:NCTX // P].bitcast(U8)
        mask16 = take(P, F16, parts=NKEY // P)
        pmax = v(take(H2 * NPAIR), "p (a n) -> p a n", a=H2)
        v32 = v(take(2 * 512), "p (s t n) -> p s t n", s=2, t=2)
        o_sb = two(take(H2 * C))
        oT = two(take(H2 * T))
        lnT = oT
        take_p, _ = region(S, KEY_STAGE)
        prob = v(take_p(P_SLOTS * 512), "p (s n) -> p s n", s=P_SLOTS)
        p_hi = v(take_p(P_SLOTS * 512, F16), "p (s n) -> p s n", s=P_SLOTS)
        p_lo = v(take_p(P_SLOTS * 512, F16), "p (s n) -> p s n", s=P_SLOTS)
        wo_at = two(S[:, 3584:3584 + 2 * C])
        take, _ = region(wi_res[:].rearrange("p e k n -> p (e k n)"))
        wc_raw = two(take(2 * 512, parts=CT))
        lat = two(take(H2 * C))
        q_max = v(take(H2 * HEADS * KR, F16), "p (a h d) -> p a h d", a=H2, h=HEADS)
        q_hh = v(take(H2 * HEADS * P, F16), "p (a h d) -> p a h d", a=H2, h=HEADS)
        qf = take(512)
        qn = take(512)
        qsq = take(512)
        gqk = take(DH)
        cmean = take(CT, parts=CT)
        bfree = two(take(2 * P, parts=CT))
        take, pos = region(S)
        gw = two(take(2 * 3 * C))
        ow = two(take(2 * C))
        w1_sb = two(take(2 * C))
        w2_sb = two(take(2 * C))
        DELTA_W = pos[0]
        assert DELTA_W <= 8448
        x1 = two(take(H2 * C))
        xx = two(take(H2 * C))
        nrm = two(take(H2 * C))
        nT = two(take(H2 * T))
        kT = two(take(H2 * T))
        qT = two(take(H2 * T))
        vd = two(take(H2 * C))
        vs = two(take(H2 * C))
        score = two(take(H2 * T))
        yT = two(take(H2 * T))
        u = two(take(H2 * C))
        xm = two(take(H2 * C))
        res2 = two(take(H2 * C))
        hm = two(take(H2 * T))
        gram = v(take(3 * P), "p (b n) -> p b n", b=3)
        bT = v(take((NLEV - 1) * 2 * P), "p (l b n) -> p l b n", l=NLEV - 1, b=2)
        X = two(take(2 * P))
        XT = two(take(2 * P))
        T1 = two(take(2 * P))
        lv = two(take(2 * P))
        x2 = xbuf
        take, _ = region(S)
        xn = two(take(H2 * C))
        tok = two(take(H2 * C))
        tokT = two(take(H2 * T))
        fin = two(take(H2 * C))
        x2xn = two(take(H2 * C))
        sel = two(take(H2 * SLOTS, F16))
        tok_hi = two(take(H2 * C, F16))
        tok_lo = two(take(H2 * C, F16))
        xs = two(take(H2 * SLOTS))
        selT = v(take(NW * T, F16), "p (g t) -> p g t", g=NW)
        hT = v(take(2 * IT * W), "p (s i w) -> p s i w", s=2, i=IT)
        ys_hi = v(take(YS * C, F16), "p (s c) -> p s c", s=YS)
        ys_lo = v(take(YS * C, F16), "p (s c) -> p s c", s=YS)

        colc = small[0:CT, 0:4]
        c_st = v(small[:, 8:32], "p (s t n) -> p s t n", s=2, t=2)
        c_mv = v(small[:, 32:40], "p (s t n) -> p s t n", s=2, t=2)
        sd = two(small[:, 40:44])
        rs = two(small[:, 44:48])
        ss = two(small[:, 48:64])
        ksd = two(small[:, 64:80])
        krm = small[:, 80:88]
        qss = small[:, 88:96]
        kr = two(small[:, 96:112])
        shift = small[:, 128:130]
        rden = small[:, 130:132]
        inv_len2 = small[:, 132:134]
        neg_len2 = small[:, 136:138]
        lr = small[:, 134:136]
        qsd = small[:, 112:120]
        qr = small[:, 120:128]

        def wi_sem(e):
            return sem(f"wi_in{(e + 1) // 2}")

        def wi_loaded(e):
            return 16 if e in (0, E - 1) else 32

        def row(name):
            return rowv[:, ROW[name][0]:ROW[name][1]]

        def row2(name):
            return row(name).unsqueeze(1).to_broadcast([P, 2, C])

        def per_head(a, n=2 * HEADS):
            return a.unsqueeze(2).to_broadcast([P, n, DH])

        def heads8(a):
            if len(a.shape) == 3:
                a = v(a, "p t n -> p (t n)")
            return v(a, "p (g d) -> p g d", g=2 * HEADS)

        rtake, _ = region(rt)
        lexp = two(rtake(2 * E))
        cand = two(rtake(2 * E))
        hot = two(rtake(2 * E, F16))
        prod = two(rtake(2 * E))
        over = rtake(E)
        xid = rtake(NX)
        exid = rtake(NX, I32)
        lmax, nlmax, lsum, wtop, top, rank, top_w, to_extra, in_own, in_extra, slot = (rtake(2) for _ in range(11))

        block = stack.enter_context(nc.Block())

        cn = v(ctx[0], "(g t p) c -> g p t c", t=2, p=P)
        cT = v(ctxT, "(k p) (g n) -> g p k n", k=2, g=NCP)

        @block.sync
        def _(sp):
            def load_ctx(g, s):
                sp.dma_start(ctxn[:, s], cn[bass.ds(g, 1)].rearrange("g p t c -> p (g t) c")
                             ).then_inc(sem(f"ctx_in{s}"), 16)
                sp.dma_start(ctxt[:, s], cT[bass.ds(g, 1)].rearrange("g p k n -> p (g k) n")
                             ).then_inc(sem(f"ctx_in{s}"), 16)

            def reload(g, s):
                sp.wait_ge(sem("ctx_stats"), g + 1)
                sp.wait_ge(sem("kv_mm"), g + 1)
                load_ctx(g + 2, s)

            def copy_high(g):
                sp.wait_ge(sem("keyB_done"), 16 * (g + 1))
                sp.wait_ge(sem("keyA_in"), 16 * (g + 1))
                sp.dma_start(keyA[0:DH, :, bass.ds(g * PAIR, PAIR)], keyB[0:DH, :, bass.ds(g * PAIR, PAIR)]
                             ).then_inc(sem("keyA_in"), 16)

            sp.dma_start(wc_raw, v(wkvT, "(k p) n -> p k n", k=2)).then_inc(sem("wc_in"), 16)
            sp.dma_start(colc, cols_ctx).then_inc(sem("wc_in"), 16)
            load_ctx(0, 0)
            load_ctx(1, 1)
            sp.dma_start(wq, v(wqT, "(k p) n -> p k n", k=2)).then_inc(sem("latent_weights_in"), 16)
            sp.dma_start(wl, v(wlkvT, "(k p) n -> p k n", k=2)).then_inc(sem("latent_weights_in"), 16)
            for g in range(4):
                reload(g, g % 2)
            with sp.Fori(2, NCP // 2 - 1) as it:
                for s in range(2):
                    reload(2 * it + s, s)
                    copy_high(2 * it + s - 4)
            for g in range(NCP - 6, NPAIR - LATE):
                copy_high(g)
            sp.wait_ge(sem("ctx_stats"), NCP)
            sp.wait_ge(sem("kv_mm"), NPAIR)
            sp.dma_start(gw, v(gates, "(k p) n -> p k n", p=P)).then_inc(sem("delta_weights_in"), 16)
            sp.dma_start(ow, v(outw, "(k p) n -> p k n", p=P)).then_inc(sem("delta_weights_in"), 16)
            sp.dma_start(w1_sb, v(w1, "(k p) n -> p k n", p=P)).then_inc(sem("delta_weights_in"), 16)
            sp.dma_start(w2_sb, v(w2, "(k p) n -> p k n", p=P)).then_inc(sem("delta_weights_in"), 16)
            sp.dma_start(wo_at, v(woT, "(k p) n -> p k n", k=2)).then_inc(sem("delta_weights_in"), 16)
            for e in range(NRES):
                sp.dma_start(wi_of(e), v(wi[e], "(k p) n -> p k n", p=P)).then_inc(wi_sem(e), 16)
            for h in range(HEADS):
                sp.wait_ge(sem("pv_done"), (h + 1) * NPAIR)
                sp.dma_start(level_pair(h), levels[:, 2 * h * P:2 * (h + 1) * P]).then_inc(sem("levels_in"), 16)
                for e in (2 * h, 2 * h + 1):
                    sp.dma_start(wo_of(e), v(wo[e], "(i p) c -> p i c", p=P)).then_inc(sem(f"wo_in{h}"), 16)
            for e in range(NRES, E):
                sp.dma_start(wi_of(e), v(wi[e], "(k p) n -> p k n", p=P)).then_inc(wi_sem(e), 16)
            sp.wait_ge(sem("extra_ids"), 1)
            for k in range(NX):
                ex = sp.value_load(exid[0:1, k:k + 1], min_val=0, max_val=E - 1)
                sp.wait_ge(sem("window_mm"), k + 1)
                sp.dma_start(wi_of(k), v(wi[bass.ds(ex, 1)], "e (k p) n -> p (e k) n", p=P)
                             ).then_inc(wi_sem(k), 16)
                sp.dma_start(wo_of(k), v(wo[bass.ds(ex, 1)], "e (i p) c -> p (e i) c", p=P)
                             ).then_inc(sem(f"wo_in{k}"), 16)
            for h in range(H2):
                sp.wait_ge(sem("y_out"), h + 1)
                sp.dma_start(v(out[0], "(h p) c -> p h c", p=P)[:, h], fin[:, h]).then_inc(sem("stored"), 16)
            sp.wait_ge(sem("stored"), 16 * H2)

        @block.gpsimd
        def _(pool):
            pool.memset(mhalf[:], -0.5)
            pool.memset(eps_c[:], LN_EPS)
            pool.memset(ones[:], 1.0)
            pool.memset(ones16[:], 1.0)
            pool.memset(cmean, 1.0 / DC)
            pool.memset(q_max[:, :, :, DH:DH + 1], 0.0)
            pool.memset(q_max[:, :, :, DH + 1:KR], BIG)
            pool.memset(q_exp[:, :, :, DH + 1:KR], BIG)
            pool.memset(mask16, 0.0)
            pool.memset(val16[:, :, :, V1:V1 + 1], 1.0).then_inc(sem("pool_consts"), 1)

            def power(job):
                pool.wait_ge(sem("var_ready"), job + 1)
                pool.tensor_tensor(rstd[:, 2 * job:2 * job + 2], var_eps[:, 2 * job:2 * job + 2], mhalf[:], ALU.pow
                                   ).then_inc(sem("rstd_ready"), 1)

            pool.wait_ge(sem("pool_consts"), 1)
            power(R_LAT)
            pool.memset(qT_max, 0.0)
            pool.memset(qT_exp, 0.0)
            pool.memset(per_head_room[:, :, 0:NKEY // 2], 0.0).then_inc(sem("rows_clear"), 1)

            pool.wait_ge(sem("lat_done"), H2)
            pool.wait_ge(sem("tables_in"), 80)
            pool.tensor_tensor(gqk, row("qn_g"), row("kn_g"), ALU.mult).then_inc(sem("pool_link"), 1)
            pool.wait_ge(sem("qr_ready"), 1)
            pool.tensor_tensor(heads8(qn), heads8(qf), per_head(qr), ALU.mult).then_inc(sem("pool_link"), 1)
            pool.wait_ge(sem("pool_link"), 2)
            pool.tensor_tensor(heads8(qn), heads8(qn), gqk.unsqueeze(1).to_broadcast([P, 2 * HEADS, DH]), ALU.mult
                               ).then_inc(sem("qn_ready"), 1)

            def low(g, s):
                pool.wait_ge(sem("hi_done"), g + 1)
                for t in range(2):
                    a = v(kh[:, s, t], "p (h d) -> p h d", h=HEADS)
                    ins = pool.tensor_tensor(k16[:, s, t, :, DH:2 * DH], a, k16[:, s, t, :, 0:DH], ALU.subtract)
                ins.then_inc(sem("lo_done"), 1)

            def scale_keys(g, s):
                pool.wait_ge(sem("kr_ready"), g + 1)
                pool.tensor_tensor(heads8(kh[:, s]), heads8(kf[:, s]), per_head(kr[:, s]), ALU.mult
                                   ).then_inc(sem("khat"), 1)

            def value_low(g, s):
                pool.wait_ge(sem("vhi_done"), g + 1)
                room = val16[:, bass.ds(2 * g, 2)]
                pool.tensor_tensor(room[:, :, :, VL:VL + DH], v(v32[:, s], "p t (h d) -> p t h d", h=HEADS),
                                   room[:, :, :, 0:DH], ALU.subtract).then_inc(sem("vlo_done"), 1)

            def pool_step(g, s):
                if not isinstance(g, int) or 1 <= g < NPAIR + 1:
                    value_low(g - 1, 1 - s)
                if not isinstance(g, int) or 2 <= g < NPAIR + 2:
                    low(g - 2, s)
                if not isinstance(g, int) or 1 <= g < NPAIR + 1:
                    scale_keys(g - 1, 1 - s)

            for g in range(7):
                pool_step(g, g % 2)
            with pool.Fori(0, 4) as it:
                for k in range(2):
                    pool_step(2 * it + 7 + k, (7 + k) % 2)
            pool_step(NCP - 1, 1)
            last = NPAIR - 1
            low(last - 2, 0)
            scale_keys(last - 1, 1)
            value_low(last - 1, 1)
            low(last - 1, 1)
            value_low(last, 0)

            pool.tensor_tensor(xbuf[:], xbuf[:], row2("bo"), ALU.add).then_inc(sem("xbo_done"), 1)

            def prob_low(n, s):
                pool.wait_ge(sem("exp_done"), n + 1)
                if not (isinstance(n, int) and n < P_SLOTS):
                    pool.wait_ge(sem("pv_done"), n - P_SLOTS + 1)
                pool.tensor_tensor(p_lo[:, s, 0:T], prob[:, s, 0:T], p_hi[:, s, 0:T], ALU.subtract
                                   ).then_inc(sem("plo0_done"), 1)

            for n in range(P_SLOTS):
                prob_low(n, n)
            with pool.Fori(1, HEADS * NPAIR // P_SLOTS) as it:
                for s in range(P_SLOTS):
                    prob_low(P_SLOTS * it + s, s)

            power(R_DN)
            power(R_DN1)
            pool.wait_ge(sem("xx_ready"), 2)
            pool.tensor_tensor(res2, xx, row2("out_b"), ALU.add).then_inc(sem("xxb"), 1)
            pool.wait_ge(sem("gram_sb"), 1)
            pool.wait_ge(sem("levels_in"), 16 * HEADS)
            for n in range(NLEV - 1):
                pool.tensor_tensor(bT[:, n], gram[:, 0:3:2, :], upper(n + 1).unsqueeze(1).to_broadcast([P, 2, P]),
                                   ALU.mult).then_inc(sem("bT_ready"), 1)
                if n == 0:
                    power(R_KEY)
            pool.tensor_tensor(x1, x1, row2("b2"), ALU.add).then_inc(sem("pool_link"), 1)
            pool.wait_ge(sem("xm_ready"), H2)
            power(R_MN)
            pool.wait_ge(sem("pool_link"), 3)
            pool.tensor_tensor(x1, x1, xm, ALU.add).then_inc(sem("res_ready"), 1)
            power(R_FFN)
            power(R_FFN1)
            pool.wait_ge(sem("tok_hi_done"), 1)
            pool.tensor_tensor(tok_lo, tok, tok_hi, ALU.subtract).then_inc(sem("tok_lo_done"), 1)
            pool.wait_ge(sem("xn_ready"), 2)
            pool.tensor_tensor(x2xn, x2[:], xn, ALU.add).then_inc(sem("x2xn_ready"), 1)

        @block.scalar
        def _(act):
            early = ROW["bo"][0]
            act.dma_start(xbuf[:], v(x[0], "(h p) c -> p h c", p=P)).then_inc(sem("x_in"), 16)
            act.dma_start(rowv[:, 0:early], rows[0:early].partition_broadcast(P)).then_inc(sem("rows0_in"), 16)
            act.dma_start(cst[:, 0:C_TRI], consts[:, 0:C_TRI]).then_inc(sem("ident_in"), 16)
            act.dma_start(mask8, v(mask, "o (p n) -> (o p) n", n=P)).then_inc(sem("mask_in"), 16)
            act.dma_start(rowv[:, early:], rows[early:].partition_broadcast(P)).then_inc(sem("tables_in"), 16)
            act.dma_start(cst[:, C_TRI:], consts[:, C_TRI:]).then_inc(sem("tables_in"), 16)
            act.dma_start(colv[:], cols).then_inc(sem("tables_in"), 16)
            act.dma_start(gt_sb[:], v(gateT, "(k p) n -> p k n", p=P)).then_inc(sem("tables_in"), 16)
            act.dma_start(lrw_sb[:], lrw).then_inc(sem("tables_in"), 16)
            nc.scalar.preload_act_table(ACT.Sqrt)
            act.wait_ge(sem("ident_in"), 16)
            act.activation(id16[:], ident, ACT.Copy).then_inc(sem("id16_done"), 1)

            def evac(dst, src, need, n, done):
                act.wait_ge(sem(need), n)
                act.activation(dst, src, ACT.Copy).then_inc(sem(done), 1)


            def values(g, s):
                act.wait_ge(sem("kv_mm"), g + 1)
                act.wait_ge(sem("rs_ready"), g + 1)
                if not isinstance(g, int) or g >= 2:
                    act.wait_ge(sem("vlo_done"), g - 1)
                for t in range(2):
                    ins = act.activation(v32[:, s, t], bank[2 + s][:, t * C:(t + 1) * C], ACT.Copy,
                                         scale=rs[:, s, t:t + 1])
                ins.then_inc(sem("v_done"), 1)

            def value_high(g, s):
                if isinstance(g, int) and g == NPAIR - 1:
                    act.wait_ge(sem("vl_done"), 2)
                else:
                    act.wait_ge(sem("v_done"), g + 1)
                act.activation(val16[:, bass.ds(2 * g, 2), :, 0:DH], v(v32[:, s], "p t (h d) -> p t h d", h=HEADS),
                               ACT.Copy).then_inc(sem("vhi_done"), 1)

            def deviation(g, s):
                act.wait_ge(sem("ctx_stats"), g + 1)
                act.activation(sd[:, s], c_mv[:, s, :, 1], ACT.Sqrt, bias=eps_c[:]).then_inc(sem("sd_ready"), 1)

            def high(g, s):
                if isinstance(g, int) and g == NPAIR - 1:
                    act.wait_ge(sem("last_khat"), 1)
                else:
                    act.wait_ge(sem("khat"), g + 1)
                if not isinstance(g, int) or g >= 2:
                    act.wait_ge(sem("key_tr"), g - 1)
                for t in range(2):
                    ins = act.activation(k16[:, s, t, :, 0:DH], v(kh[:, s, t], "p (h d) -> p h d", h=HEADS), ACT.Copy)
                ins.then_inc(sem("hi_done"), 1)

            def square(g, s):
                act.wait_ge(sem("kraw"), g + 1)
                if not isinstance(g, int) or g >= 2:
                    act.wait_ge(sem("ss_ready"), g - 1)
                act.activation(ksq[:, s], v(kf[:, s], "p t n -> p (t n)"), ACT.Square).then_inc(sem("sq_ready"), 1)

            def key_norm(g, s):
                act.wait_ge(sem("ss_ready"), g + 1)
                act.activation(ksd[:, s], ss[:, s], ACT.Sqrt, scale=1.0 / (DH * RANGE * RANGE)
                               ).then_inc(sem("ksd_ready"), 1)

            def store_keys(g, s):
                act.wait_ge(sem("key_tr"), g + 1)
                act.activation(keyB[:, :, bass.ds(g * PAIR, PAIR)],
                               v(bank[4 + s].bitcast(F16), "p (h k) -> p h k", h=HEADS), ACT.Copy
                               ).then_inc(sem("keyB_done"), 16)

            def act_step(g, s):
                def has(p, n):
                    return not isinstance(p, int) or 0 <= p < n
                if has(g, NCP):
                    values(g, s)
                if has(g - 2, NPAIR):
                    high(g - 2, s)
                if has(g, NPAIR):
                    square(g, s)
                if has(g + 1, NCP):
                    deviation(g + 1, 1 - s)
                if has(g - 1, NPAIR):
                    key_norm(g - 1, 1 - s)
                if has(g - 4, NPAIR):
                    store_keys(g - 4, s)
                if has(g, NPAIR):
                    value_high(g, s)

            deviation(0, 0)
            evac(bw, bank[6][:, 0:512], "bw_mm", 1, "bw_done")
            evac(v(lnT, "p a b -> p (a b)"), bank[5], "lnT_mm", 1, "lnT_done")
            for g in range(7):
                act_step(g, g % 2)
                if g == 0:
                    act.wait_ge(sem("q_raw_mm"), 2)
                    act.activation(qsq, bank[4], ACT.Square).then_inc(sem("q_sq"), 1)
                    act.activation(qf, bank[4], ACT.Copy)
                    act.wait_ge(sem("q_ss"), 1)
                    act.activation(qsd, qss, ACT.Sqrt, scale=1.0 / DH).then_inc(sem("q_sd"), 1)
                if g == 1:
                    act.wait_ge(sem("rows_clear"), 1)
                    act.dma_start(keyA[DH:DH + 1], key_ones).then_inc(sem("keyA_in"), 16)
                    act.wait_ge(sem("mask16_done"), 1)
                    for h in range(HEADS):
                        act.dma_start(keyA[DH + 1:KR, h, :], mask16).then_inc(sem("mrow_in"), 16)
            with act.Fori(0, 4) as it:
                for k in range(2):
                    act_step(2 * it + 7 + k, (7 + k) % 2)
            act_step(NCP - 1, 1)
            last = NPAIR - 1
            high(last - 2, 0)
            key_norm(last - 1, 1)
            store_keys(last - 4, 0)
            square(last, 0)
            key_norm(last, 0)
            high(last - 1, 1)
            store_keys(last - 3, 1)
            high(last, 0)
            store_keys(last - 2, 0)
            value_high(last, 0)
            store_keys(last - 1, 1)
            store_keys(last, 0)

            nc.scalar.preload_act_table(ACT.Exp)

            def exp_group(n, s):
                act.wait_ge(sem("s_done"), n + 1)
                if not (isinstance(n, int) and n < P_SLOTS):
                    act.wait_ge(sem("pv_done"), n - P_SLOTS + 1)
                for dst in (p_hi, prob):
                    ins = act.activation(dst[:, s], bank[s % 2], ACT.Exp, scale=1.0 / (RANGE * RANGE))
                ins.then_inc(sem("exp_done"), 1)

            for n in range(P_SLOTS):
                exp_group(n, n)
            with act.Fori(1, HEADS * NPAIR // P_SLOTS) as it:
                for s in range(P_SLOTS):
                    exp_group(P_SLOTS * it + s, s)

            evac(oT[:, 0], bank[6][:, 0:T], "oT_mm", 1, "oT0_done")
            evac(nT[:, 0], bank[2][:, 0:T], "nT_mm", 1, "nT0_done")
            act.wait_ge(sem("tables_in"), 80)
            act.activation(tri16[:], tri, ACT.Copy).then_inc(sem("tri16_done"), 1)
            act.wait_ge(sem("kT_mm"), 1)
            act.activation(kT[:, 0], bank[4][:, 0:T], ACT.Identity, bias=colv[:, 4:5]).then_inc(sem("kT0_done"), 1)
            evac(gram[:, 2], bank[1][:, 0:P], "gram_mm", 2, "gram11_sb")
            act.wait_ge(sem("diag00"), 1)
            act.activation(v(gram[:, 0:2], "p b n -> p (b n)"), bank[0][:, 0:T], ACT.Copy).then_inc(sem("gram_sb"), 1)
            for a in range(2):
                act.wait_ge(sem("q_mm"), a + 1)
                act.activation(qT[:, a], bank[6 + a][:, 0:T], ACT.Identity, bias=colv[:, a:a + 1]
                               ).then_inc(sem("qT_done"), 1)
            act.wait_ge(sem("rstd_ready"), R_KEY + 1)
            for a in range(2):
                act.wait_ge(sem("vd_ready"), a + 1)
                act.activation(vs[:, a], vd[:, a], ACT.Copy, scale=rstd[:, 2 * R_KEY + a:2 * R_KEY + a + 1]
                               ).then_inc(sem("vs_ready"), 1)
            act.wait_ge(sem("lr_ready"), 1)
            for a in range(2):
                act.wait_ge(sem("score_mm"), a + 1)
                act.activation(score[:, a], bank[3 - a][:, 0:T], ACT.Copy, scale=lr[:, a:a + 1]
                               ).then_inc(sem("score_done"), 1)
            evac(yT[:, 0], bank[6][:, 0:T], "yT_mm", 1, "yT0_done")
            evac(nT[:, 0], bank[2][:, 0:T], "nT_mm", 2, "nT0_done")
            act.wait_ge(sem("hm_mm"), 1)
            act.activation(hm[:, 0], bank[4][:, 0:T], ACT.Relu, bias=colv[:, 2:3]).then_inc(sem("hm0_done"), 1)
            evac(tokT[:, 0], bank[0][:, 0:T], "nT_mm", 3, "nT0_done")
            evac(tok_hi, tok, "tok_done", 2, "tok_hi_done")
            act.wait_ge(sem("logits_used"), 1)
            for a in range(2):
                act.activation(lexp[:, a], bank[2][:, a * E:(a + 1) * E], ACT.Exp, bias=nlmax[:, a:a + 1],
                               accum_out=lsum[:, a:a + 1]).then_inc(sem("lsum_ready"), 1)
            nc.scalar.preload_act_table(ACT.Gelu)
            for m, (at, n) in enumerate(XS_CUTS):
                act.wait_ge(sem("xs_mm"), 2 * m + 2)
                act.activation(xs[:, 1, at:at + n], bank[2 * m + 1][:, 0:n], ACT.Copy).then_inc(sem("xs1_done"), 1)
            def window_high(n):
                act.wait_ge(sem("window_mm"), n + 1)
                if n >= YS:
                    act.wait_ge(sem("back_mm"), n - YS + 1)
                act.activation(ys_hi[:, n % YS], bank[4 + n % 2][:, 0:C], ACT.Copy).then_inc(sem("ys_hi_done"), 1)

            for n in range(NW):
                for j in range(2):
                    act.wait_ge(sem("h_mm"), 2 * n + j + 1)
                    if n >= 2:
                        act.wait_ge(sem("window_mm"), n - 1)
                    act.activation(v(hT[:, n % 2, j * (IT // 2):(j + 1) * (IT // 2)], "p i w -> p (i w)"),
                                   bank[2 * (n % 2) + j], ACT.Gelu).then_inc(sem("gelu_done"), 1)
                if n:
                    window_high(n - 1)
            window_high(NW - 1)

        @block.vector
        def _(dve):
            done = {}

            def done_count(name):
                done[name] = done.get(name, 0) + 1

            def link(ins, name="dve_link"):
                done_count(name)
                ins.then_inc(sem(name), 1)
                dve.wait_ge(sem(name), done[name])

            def norm(src, dst, job, gamma, beta, done, twice, once=None, once_done=None, need=None):
                for a in range(2):
                    if need is not None:
                        need(a)
                    ins = dve.bn_stats(stats[:, a], src[:, a])
                link(ins)
                for a in range(2):
                    ins = dve.bn_aggr(mv[:, a], stats[:, a])
                link(ins)
                jobs = ((1.0 + LN_EPS, LN_EPS * LN_EPS), (1.0, LN_EPS)) if once is not None else (
                    ((1.0 + LN_EPS, LN_EPS * LN_EPS),) if twice else ((1.0, LN_EPS),))
                for k, (factor, plus) in enumerate(jobs):
                    dve.tensor_scalar(var_eps[:, 2 * (job + k):2 * (job + k) + 2], mv[:, :, 1], factor, plus,
                                      ALU.mult, ALU.add).then_inc(sem("var_ready"), 1)
                    done_count("var_ready")
                for a in range(2):
                    ins = dve.scalar_tensor_tensor(dst[:, a], src[:, a], mv[:, a, 0:1], row(gamma),
                                                   ALU.subtract, ALU.mult)
                link(ins)
                dve.wait_ge(sem("rstd_ready"), job + 1)
                for a in range(2):
                    ins = dve.scalar_tensor_tensor(dst[:, a], dst[:, a], rstd[:, 2 * job + a:2 * job + a + 1],
                                                   row(beta), ALU.mult, ALU.add).then_inc(sem(done), 1)
                if once is not None:
                    dve.wait_ge(sem("rstd_ready"), job + 2)
                    for a in range(2):
                        dve.tensor_scalar(once[:, a], src[:, a], mv[:, a, 0:1],
                                          rstd[:, 2 * job + 2 + a:2 * job + 3 + a],
                                          ALU.subtract, ALU.mult).then_inc(sem(once_done), 1)

            dve.wait_ge(sem("pool_consts"), 1)
            dve.wait_ge(sem("wc_in"), 32)
            for k in range(2):
                ins = dve.tensor_scalar(wc[:, k], wc_raw[:, k], colc[:, k:k + 1], None, ALU.mult)
            link(ins, "wg_done")
            for k in range(2):
                ins = dve.tensor_scalar(bfree[:, k], ones[0:CT], colc[:, 2 + k:3 + k], None, ALU.mult)
            link(ins, "bfree_done")
            dve.wait_ge(sem("x_in"), 16)
            dve.wait_ge(sem("rows0_in"), 16)
            norm(xbuf, lat, R_LAT, "ln_l_g", "ln_l_b", "lat_done", twice=True)
            dve.wait_ge(sem("cmean_mm"), 1)
            for k in range(2):
                ins = dve.tensor_tensor(wc[:, k], wc[:, k], bank[7][0:CT, 0:512], ALU.subtract)
            link(ins, "wprep_done")

            def q_norms():
                dve.wait_ge(sem("q_sq"), 1)
                dve.tensor_reduce(qss, heads8(qsq), AX.X, ALU.add).then_inc(sem("q_ss"), 1)
                dve.wait_ge(sem("q_sd"), 1)
                link(dve.tensor_scalar(qsd, qsd, RMS_EPS, None, ALU.max))
                dve.reciprocal(qr, qsd).then_inc(sem("qr_ready"), 1)

            def q_split():
                dve.wait_ge(sem("qn_ready"), 1)
                for a in range(2):
                    exact = v(qn[:, a * C:(a + 1) * C], "p (h d) -> p h d", h=HEADS)
                    link(dve.tensor_copy(q_max[:, a, :, 0:DH], exact))
                    for c in range(2):
                        dve.tensor_copy(q_hh[:, a, :, c * DH:(c + 1) * DH], q_max[:, a, :, 0:DH])
                    link(dve.tensor_tensor(q_exp[:, a, :, 0:DH], exact, q_max[:, a, :, 0:DH], ALU.subtract), "q_split")

            def q_store():
                dve.wait_ge(sem("qT_mm"), 1)
                dve.wait_ge(sem("rows_clear"), 1)
                link(dve.tensor_copy(v(qT_max[0:KR], "p h t -> p (h t)"), bank[6].bitcast(F16)[0:KR, :]))
                link(dve.tensor_copy(v(qT_hh, "p h t -> p (h t)"), bank[7].bitcast(F16)), "qT_ready")

            def ctx_stats(g, s):
                dve.wait_ge(sem(f"ctx_in{s}"), 16 * (g - s) + 32)
                for t in range(2):
                    ins = dve.bn_stats(c_st[:, s, t], ctxn[:, s, t])
                ins.then_inc(sem("ctx_bn"), 1)

            def ctx_aggr(g, s):
                for t in range(2):
                    ins = dve.bn_aggr(c_mv[:, s, t], c_st[:, s, t])
                ins.then_inc(sem("ctx_stats"), 1)

            def ctx_rstd(g, s):
                dve.wait_ge(sem("sd_ready"), g + 1)
                if not (isinstance(g, int) and g < 2):
                    dve.wait_ge(sem("v_done"), g - 1)
                dve.reciprocal(rs[:, s], sd[:, s]).then_inc(sem("rs_ready"), 1)

            def raw_keys(g, s):
                dve.wait_ge(sem("kv_mm"), g + 1)
                dve.wait_ge(sem("rs_ready"), g + 1)
                if not (isinstance(g, int) and g < 2):
                    dve.wait_ge(sem("khat"), g - 1)
                    dve.wait_ge(sem("sq_ready"), g - 1)
                for t in range(2):
                    ins = dve.scalar_tensor_tensor(kf[:, s, t], bank[s][:, t * C:(t + 1) * C], rs[:, s, t:t + 1],
                                                   bw[:, 0:C], ALU.mult, ALU.add)
                ins.then_inc(sem("kraw"), 1)

            def latent_keys(g, s):
                dve.wait_ge(sem("kv_mm"), g + 1)
                dve.wait_ge(sem("khat"), g - 1)
                dve.wait_ge(sem("sq_ready"), g - 1)
                dve.tensor_copy(v(kf[:, s], "p t n -> p (t n)"), bank[s]).then_inc(sem("kraw"), 1)

            def latent_values(g, s):
                dve.wait_ge(sem("vlo_done"), g - 1)
                for t in range(2):
                    dve.tensor_tensor(v32[:, s, t], bank[2 + s][:, t * C:(t + 1) * C], bw[:, C:2 * C], ALU.subtract
                                      ).then_inc(sem("vl_done"), 1)

            def sum_squares(g, s):
                dve.wait_ge(sem("sq_ready"), g + 1)
                dve.tensor_reduce(ss[:, s], heads8(ksq[:, s]), AX.X, ALU.add).then_inc(sem("ss_ready"), 1)

            def key_scale(g, s):
                dve.wait_ge(sem("ksd_ready"), g + 1)
                dve.tensor_scalar(krm, ksd[:, s], RMS_EPS / RANGE, None, ALU.max).then_inc(sem("krm_done"), 1)
                dve.wait_ge(sem("krm_done"), g + 1)
                dve.reciprocal(kr[:, s], krm).then_inc(sem("kr_ready"), 1)

            def group_max(n, i, banks, s):
                dve.wait_ge(sem("x_done"), n + 1)
                dve.tensor_reduce(pmax[:, :, bass.ds(i, 1)], v(bank[banks + s], "p (a k) -> p a k", a=2), AX.X, ALU.max
                                  ).then_inc(sem("max_done"), 1)

            def dve_step(g, s):
                def has(p, n):
                    return not isinstance(p, int) or 0 <= p < n
                if has(g, NCP):
                    raw_keys(g, s)
                if has(g + 1, NCP):
                    ctx_stats(g + 1, 1 - s)
                    dve.wait_ge(sem("ctx_bn"), g + 2)
                if has(g - 1, NPAIR):
                    sum_squares(g - 1, 1 - s)
                if has(g + 1, NCP):
                    ctx_aggr(g + 1, 1 - s)
                if has(g - 1, NPAIR):
                    key_scale(g - 1, 1 - s)
                if has(g + 1, NCP):
                    ctx_rstd(g + 1, 1 - s)
                if has(g - 6, NPAIR):
                    group_max(g - 6, g - 6, 6, s)

            ctx_stats(0, 0)
            dve.wait_ge(sem("ctx_bn"), 1)
            ctx_aggr(0, 0)
            ctx_rstd(0, 0)
            dve.wait_ge(sem("bw_done"), 1)
            for g in range(7):
                dve_step(g, g % 2)
                if g == 0:
                    q_norms()
                    dve.wait_ge(sem("mask_in"), 16)
                    link(dve.tensor_scalar(mask16[0:NCTX // P], mask8, BIG, -BIG, ALU.mult, ALU.add), "mask16_done")
                if g == 1:
                    q_split()
                if g == 4:
                    q_store()
            with dve.Fori(0, 4) as it:
                for k in range(2):
                    dve_step(2 * it + 7 + k, (7 + k) % 2)
            dve_step(NCP - 1, 1)

            def last_scaled(g, s):
                dve.wait_ge(sem("kr_ready"), g + 1)
                dve.wait_ge(sem("lo_done"), g - 1)
                dve.tensor_tensor(heads8(kh[:, s]), heads8(kf[:, s]), per_head(kr[:, s]), ALU.mult
                                  ).then_inc(sem("last_khat"), 1)

            def last_low(g, s):
                dve.wait_ge(sem("hi_done"), g + 1)
                for t in range(2):
                    a = v(kh[:, s, t], "p (h d) -> p h d", h=HEADS)
                    ins = dve.tensor_tensor(k16[:, s, t, :, DH:2 * DH], a, k16[:, s, t, :, 0:DH], ALU.subtract)
                ins.then_inc(sem("last_lo"), 1)

            def late_copy(g):
                dve.wait_ge(sem("keyB_done"), 16 * (g + 1))
                dve.tensor_copy(keyA[0:DH, :, g * PAIR:(g + 1) * PAIR], keyB[0:DH, :, g * PAIR:(g + 1) * PAIR]
                                ).then_inc(sem("keyA_late"), 1)

            def first_max(g):
                group_max(g, g, 6, g % 2)

            last = NPAIR - 1
            sum_squares(last - 1, 1)
            latent_keys(last, 0)
            key_scale(last - 1, 1)
            first_max(last - 6)
            sum_squares(last, 0)
            key_scale(last, 0)
            last_scaled(last, 0)
            latent_values(last, 0)
            first_max(last - 5)
            late_copy(last - 3)
            last_low(last, 0)
            late_copy(last - 2)
            first_max(last - 4)
            late_copy(last - 1)
            first_max(last - 3)
            first_max(last - 2)
            late_copy(last)
            first_max(last - 1)
            first_max(last)

            def head_shift(h):
                dve.wait_ge(sem("max_done"), NPAIR * (h + 1))
                link(dve.tensor_reduce(shift, pmax, AX.X, ALU.max))
                link(dve.tensor_scalar(q_exp[:, :, h, DH], shift, -1.0, P_SCALE_LOG * RANGE * RANGE,
                                       ALU.mult, ALU.add), "shift_done")

            def head_queries(h):
                dve.wait_ge(sem("qe_mm"), h + 1)
                link(dve.tensor_copy(qT_exp[0:KR, h], bank[6].bitcast(F16)[0:KR, 0:T]), "qe_done")

            def prob_low(n, s):
                dve.wait_ge(sem("exp_done"), n + 1)
                if not (isinstance(n, int) and n < P_SLOTS):
                    dve.wait_ge(sem("pv_done"), n - P_SLOTS + 1)
                dve.tensor_tensor(p_lo[:, s, T:2 * T], prob[:, s, T:2 * T], p_hi[:, s, T:2 * T], ALU.subtract
                                  ).then_inc(sem("plo1_done"), 1)

            def head_output(h):
                dve.wait_ge(sem("pv_done"), NPAIR * (h + 1))
                acc = v(bank[4 + h % 2][:, 0:2 * VD], "p (a d) -> p a d", a=2)
                both_parts = two(v32[:, 0, 0, 0:2 * DH])
                dve.tensor_copy(both_parts, acc[:, :, VL:VL + DH])
                link(dve.reciprocal(rden, acc[:, :, V1]))
                link(dve.tensor_tensor(both_parts, acc[:, :, 0:DH], both_parts, ALU.add))
                for a in range(2):
                    link(dve.scalar_tensor_tensor(o_sb[:, a, h * DH:(h + 1) * DH], both_parts[:, a], rden[:, a:a + 1],
                                                  bw[:, C + h * DH:C + (h + 1) * DH], ALU.mult, ALU.add), "o_done")

            head_shift(0)
            head_queries(0)
            for h in range(HEADS):
                def head_group(i, k):
                    n = h * NPAIR + i
                    if h + 1 < HEADS:
                        group_max(n + NPAIR + 1, i + 1, 2, (h + k) % 2)
                    prob_low(n, (h + k) % P_SLOTS)

                if h + 1 < HEADS:
                    group_max(h * NPAIR + NPAIR, 0, 2, (h + 1) % 2)
                for i in range(P_SLOTS):
                    head_group(i, i)
                    if h and i == 2:
                        head_output(h - 1)
                with dve.Fori(1, NPAIR // P_SLOTS - 1) as it:
                    for k in range(P_SLOTS):
                        head_group(P_SLOTS * it + k, k)
                for k in range(P_SLOTS - 1):
                    head_group(NPAIR - 1 - P_SLOTS + k, k)
                if h + 1 < HEADS:
                    group_max(h * NPAIR + 2 * NPAIR - 1, NPAIR - 1, 2, (h + 1) % 2)
                    head_shift(h + 1)
                prob_low(h * NPAIR + NPAIR - 2, (h + NPAIR - 2) % P_SLOTS)
                if h + 1 < HEADS:
                    head_queries(h + 1)
                prob_low(h * NPAIR + NPAIR - 1, (h + NPAIR - 1) % P_SLOTS)
            head_output(HEADS - 1)

            def evac(dst, src, need, n, name):
                dve.wait_ge(sem(need), n)
                dve.tensor_copy(dst, src).then_inc(sem(name), 1)

            evac(oT[:, 1], bank[7][:, 0:T], "oT_mm", 1, "oT1_done")
            dve.wait_ge(sem("xbo_done"), 1)
            dve.wait_ge(sem("tables_in"), 80)

            def attended(a):
                dve.wait_ge(sem("att_mm"), a + 1)
                link(dve.tensor_tensor(x1[:, a], bank[a][:, 0:C], xbuf[:, a], ALU.add))

            norm(x1, nrm, R_DN, "dn_g", "dn_b", "nrm_done", twice=True, once=xx, once_done="xx_ready", need=attended)
            evac(nT[:, 1], bank[3][:, 0:T], "nT_mm", 1, "nT1_done")
            dve.wait_ge(sem("kT_mm"), 2)
            dve.tensor_scalar(kT[:, 1], bank[5][:, 0:T], colv[:, 5:6], None, ALU.add).then_inc(sem("kT1_done"), 1)
            dve.wait_ge(sem("gram_mm"), 1)
            dve.tensor_tensor(lv[:, 0], bank[0][:, 0:P], ident, ALU.mult).then_inc(sem("diag00"), 1)
            dve.wait_ge(sem("gram11_sb"), 1)
            dve.wait_ge(sem("diag00"), 1)
            link(dve.tensor_tensor(lv[:, 1], bank[1][:, 0:P], ident, ALU.mult))
            link(dve.tensor_reduce(var_eps[:, 2 * R_KEY:2 * R_KEY + 2], lv, AX.X, ALU.add), "var_ready")
            link(dve.reciprocal(inv_len2, var_eps[:, 2 * R_KEY:2 * R_KEY + 2]))
            dve.wait_ge(sem("levels_in"), 16 * HEADS)
            dve.wait_ge(sem("gram_sb"), 1)
            for b in range(2):
                dve.scalar_tensor_tensor(T1[:, b], gram[:, 2 * b], inv_len2[:, b:b + 1], lower1,
                                               ALU.mult, ALU.mult).then_inc(sem("t1_done"), 1)
            dve.wait_ge(sem("t1_done"), 2)
            for b in range(2):
                dve.tensor_tensor(X[:, b], ident, T1[:, b], ALU.subtract).then_inc(sem("x_next"), 1)
            dve.tensor_scalar(neg_len2, inv_len2, -1.0, None, ALU.mult).then_inc(sem("neg_done"), 1)
            for b in range(2):
                dve.wait_ge(sem("xtt_mm"), b + 1)
                dve.tensor_tensor(XT[:, b], ident, bank[6 + b][:, 0:P], ALU.subtract
                                  ).then_inc(sem("xt_next"), 1)

            def values_in(a):
                dve.wait_ge(sem("v_mm"), a + 1)
                dve.tensor_tensor(vd[:, a], bank[2 + a][:, 0:C], row("gates_bv"), ALU.add
                                  ).then_inc(sem("vd_ready"), 1)

            for n in range(NLEV - 1):
                for b in range(2):
                    dve.wait_ge(sem("t1_mm"), 2 * n + b + 1)
                    dve.tensor_scalar(T1[:, b], bank[b][:, 0:P], inv_len2[:, b:b + 1], None, ALU.mult
                                      ).then_inc(sem("t1_done"), 1)
                if n < NLEV - 2:
                    for b in range(2):
                        dve.wait_ge(sem("xx_mm"), 2 * n + b + 1)
                        dve.tensor_tensor(X[:, b], X[:, b], bank[4 + b][:, 0:P], ALU.subtract
                                          ).then_inc(sem("x_next"), 1)
                for b in range(2):
                    dve.wait_ge(sem("xtt_mm"), 2 * n + b + 3)
                    dve.tensor_tensor(XT[:, b], XT[:, b], bank[6 + b][:, 0:P], ALU.subtract
                                      ).then_inc(sem("xt_next"), 1)
                if n == 0:
                    values_in(0)
                if n == 1:
                    values_in(1)
                if n == 2:
                    dve.wait_ge(sem("lr_mm"), 1)
                    dve.tensor_tensor(lr, bank[2][:, C:C + 2], row("lr_b").to_broadcast([P, 2]), ALU.add
                                      ).then_inc(sem("lr_ready"), 1)
            evac(u[:, 0], bank[4][:, 0:C], "u1_mm", 1, "u_done")
            dve.wait_ge(sem("vs_ready"), 2)
            dve.wait_ge(sem("neg_done"), 1)
            dve.wait_ge(sem("u01_mm"), 1)
            dve.scalar_tensor_tensor(vs[:, 1], bank[5][:, 0:C], neg_len2[:, 1:2], vs[:, 1], ALU.mult, ALU.add
                                     ).then_inc(sem("vs_ready"), 1)
            evac(u[:, 1], bank[0][:, 0:C], "u2_mm", 1, "u_done")
            evac(yT[:, 1], bank[7][:, 0:T], "yT_mm", 1, "yT1_done")
            dve.wait_ge(sem("xxb"), 1)

            def delta_out(a):
                dve.wait_ge(sem("delta_mm"), a + 1)
                link(dve.tensor_tensor(xm[:, a], bank[a][:, 0:C], res2[:, a], ALU.add), "xm_ready")

            norm(xm, nrm, R_MN, "mn_g", "mn_b", "nrm_done", twice=False, need=delta_out)
            evac(nT[:, 1], bank[3][:, 0:T], "nT_mm", 2, "nT1_done")
            dve.wait_ge(sem("hm_mm"), 2)
            dve.tensor_scalar(hm[:, 1], bank[5][:, 0:T], colv[:, 3:4], 0.0, ALU.add, ALU.max
                              ).then_inc(sem("hm1_done"), 1)
            dve.wait_ge(sem("res_ready"), 1)

            def mlp_out(a):
                dve.wait_ge(sem("mlp_mm"), a + 1)
                link(dve.tensor_tensor(x2[:, a], bank[6 + a][:, 0:C], x1[:, a], ALU.add))

            norm(x2, tok, R_FFN, "ffn_g", "ffn_b", "tok_done", twice=True, once=xn, once_done="xn_ready", need=mlp_out)
            evac(tokT[:, 1], bank[1][:, 0:T], "nT_mm", 3, "nT1_done")
            dve.wait_ge(sem("logit_mm"), 2)
            logits = two(bank[2][:, 0:2 * E])
            iota_e = iota[:, 0:E]

            def each(m, n=E):
                return m.unsqueeze(2).to_broadcast([P, 2, n])

            iota_2e = iota_e.unsqueeze(1).to_broadcast([P, 2, E])
            link(dve.tensor_reduce(lmax, logits, AX.X, ALU.max))
            dve.tensor_scalar(nlmax, lmax, -1.0, None, ALU.mult)
            link(dve.tensor_tensor(cand, logits, each(lmax), ALU.is_lt), "logits_used")
            link(dve.scalar_tensor_tensor(cand, cand, 100.0, iota_2e, ALU.mult, ALU.add))
            link(dve.tensor_reduce(top, cand, AX.X, ALU.min))
            link(dve.tensor_tensor(hot, iota_2e, each(top), ALU.is_equal), "hot_done")
            dve.tensor_scalar(top_w, top, float(W), None, ALU.mult)
            dve.tensor_scalar(to_extra, top, -float(W), float((E - 1) * W), ALU.mult, ALU.add)
            dve.wait_ge(sem("lsum_ready"), 2)
            link(dve.reciprocal(wtop, lsum))
            dve.wait_ge(sem("rank_mm"), 1)
            link(dve.tensor_tensor(prod, two(bank[6][:, 0:2 * E]), hot, ALU.mult))
            link(dve.tensor_reduce(rank, prod, AX.X, ALU.add))
            dve.tensor_tensor(in_own, rank, top_w, ALU.add)
            link(dve.scalar_tensor_tensor(in_extra, rank, float(W), to_extra, ALU.is_ge, ALU.mult))
            link(dve.tensor_tensor(slot, in_own, in_extra, ALU.add))
            for at, n in XS_CUTS:
                for a in range(2):
                    dve.tensor_scalar(sel[:, a, at:at + n], iota[:, at:at + n], slot[:, a:a + 1], None, ALU.is_equal
                                      ).then_inc(sem("sel_done"), 1)
            link(dve.scalar_tensor_tensor(over, bank[6][:, 2 * E:3 * E], float(W), iota_e, ALU.is_gt, ALU.mult))
            link(dve.tensor_reduce(xid, over, AX.X, ALU.add))
            link(dve.tensor_copy(exid, xid), "extra_ids")
            for m, (at, n) in enumerate(XS_CUTS):
                dve.wait_ge(sem("xs_mm"), 2 * m + 1)
                link(dve.tensor_copy(xs[:, 0, at:at + n], bank[2 * m][:, 0:n]), "xs0_done")

            def store_selT(q):
                n = min(2, NW - 2 * q)
                dve.wait_ge(sem("selT_mm"), q + 1)
                link(dve.tensor_copy(v(selT[:, 2 * q:2 * q + n], "p g t -> p (g t)"),
                                     bank[6 + q % 2].bitcast(F16)[:, 0:n * T]),
                     "selT_done")

            store_selT(0)
            for n in range(NW):
                if 1 <= n <= NW // 2:
                    store_selT(n)
                dve.wait_ge(sem("ys_hi_done"), n + 1)
                if n >= YS:
                    dve.wait_ge(sem("back_mm"), n - YS + 1)
                dve.tensor_tensor(ys_lo[:, n % YS], bank[4 + n % 2][:, 0:C], ys_hi[:, n % YS], ALU.subtract
                                  ).then_inc(sem("ys_done"), 1)
            dve.wait_ge(sem("x2xn_ready"), 1)
            dve.wait_ge(sem("back_mm"), NW)
            for a in range(2):
                dve.scalar_tensor_tensor(fin[:, a], bank[6][:, a * C:(a + 1) * C], wtop[:, a:a + 1], x2xn[:, a],
                                         ALU.mult, ALU.add).then_inc(sem("y_out"), 1)

        @block.tensor
        def _(pe):
            def part(dst, a, n):
                return dst[a][:, 0:n] if isinstance(dst, tuple) else dst[:, a * n:(a + 1) * n]

            def turn(dst, src, need, n, done):
                for a in range(2):
                    pe.wait_ge(sem(need), n + a + 1)
                    for c in range(2):
                        ins = pe.transpose(part(dst, c, T)[:, a * P:(a + 1) * P], src[:, a, c * P:(c + 1) * P], ident)
                ins.then_inc(sem(done), 1)

            def moved(name, n):
                pe.wait_ge(sem(name.replace("*", "0")), n)
                pe.wait_ge(sem(name.replace("*", "1")), n)

            def product(dst, lhsT, rhs):
                n = len(lhsT)
                for k in range(n):
                    ins = pe.matmul(dst, lhsT[k], rhs[k], start=k == 0, stop=k == n - 1)
                return ins

            def keep_clock(n, spare):
                for _ in range(n):
                    pe.matmul(spare[:, 0:2 * P], id16[:], ones[:].bitcast(F16), start=True, stop=True)

            def by_token(dst, src, w, done, halves=(0, 1)):
                n = w.shape[2]
                for a in halves:
                    ins = product(part(dst, a, n), [src[:, k, a * P:(a + 1) * P] for k in range(2)],
                                  [w[:, k] for k in range(2)])
                    ins.then_inc(sem(done), 1)

            def by_channel(dst, src, w, done, halves=(0, 1)):
                for a in halves:
                    ins = product(part(dst, a, T), [w[:, k, a * P:(a + 1) * P] for k in range(2)],
                                  [src[:, k] for k in range(2)])
                    ins.then_inc(sem(done), 1)

            pe.wait_ge(sem("wg_done"), 1)
            product(bank[7][0:CT], [cmean] * 2, [wc[:, k] for k in range(2)]).then_inc(sem("cmean_mm"), 1)
            pe.wait_ge(sem("bfree_done"), 1)
            product(bank[6], [bfree[:, k] for k in range(2)], [wc_raw[:, k] for k in range(2)]
                    ).then_inc(sem("bw_mm"), 1)

            def latent_queries():
                pe.wait_ge(sem("ident_in"), 16)
                turn(bank[5], lat, "lat_done", 0, "lnT_mm")
                pe.wait_ge(sem("lnT_done"), 1)
                pe.wait_ge(sem("latent_weights_in"), 32)
                by_token(bank[4], lnT, wq, "q_raw_mm")

            def turn_q():
                pe.wait_ge(sem("q_split"), 2)
                pe.wait_ge(sem("bw_done"), 1)
                pe.wait_ge(sem("id16_done"), 1)
                for src, dst, n in ((q_max, bank[6], KR), (q_hh, bank[7], P)):
                    for h in range(HEADS):
                        for a in range(2):
                            ins = pe.transpose(dst.bitcast(F16)[0:n, h * T + a * P:h * T + (a + 1) * P],
                                               src[:, a, h, :], id16[:])
                ins.then_inc(sem("qT_mm"), 1)

            def keys_values(g, s):
                if isinstance(g, int) and g == NPAIR - 1:
                    pe.wait_ge(sem("latent_weights_in"), 32)
                    src, w = lnT, wl
                else:
                    pe.wait_ge(sem(f"ctx_in{s}"), 16 * (g - s) + 32)
                    src, w = ctxt[:, s], wc
                if not (isinstance(g, int) and g < 2):
                    pe.wait_ge(sem("kraw"), g - 1)
                    pe.wait_ge(sem("v_done"), g - 1)
                for t in range(2):
                    mine = [src[:, k, t * P:(t + 1) * P] for k in range(2)]
                    product(bank[s][:, t * C:(t + 1) * C], mine, [w[:, k, 0:C] for k in range(2)])
                    ins = product(bank[2 + s][:, t * C:(t + 1) * C], mine, [w[:, k, C:2 * C] for k in range(2)])
                ins.then_inc(sem("kv_mm"), 1)

            def turn_keys(g, s):
                if isinstance(g, int) and g == NPAIR - 1:
                    pe.wait_ge(sem("last_lo"), 1)
                else:
                    pe.wait_ge(sem("lo_done"), g + 1)
                if not (isinstance(g, int) and g < 2):
                    pe.wait_ge(sem("keyB_done"), 16 * (g - 1))
                for h in range(HEADS):
                    for t in range(2):
                        ins = pe.transpose(bank[4 + s].bitcast(F16)[:, h * PAIR + t * P:h * PAIR + (t + 1) * P],
                                           k16[:, s, t, h, :], id16[:])
                ins.then_inc(sem("key_tr"), 1)

            def max_scores(h, i, n, banks, s):
                if not (isinstance(n, int) and n < 2):
                    pe.wait_ge(sem("max_done"), n - 1)
                for a in range(2):
                    ins = pe.matmul(bank[banks + s][:, a * T:(a + 1) * T], qT_max[:, h, a * P:(a + 1) * P],
                                    keyA[:, h, bass.ds(i * PAIR, PAIR)], start=True, stop=True)
                ins.then_inc(sem("x_done"), 1)

            def first_scores(g, s):
                if isinstance(g, int) and g >= NPAIR - LATE:
                    pe.wait_ge(sem("keyA_late"), g - (NPAIR - LATE) + 1)
                else:
                    pe.wait_ge(sem("keyA_in"), 16 * g + 32)
                max_scores(0, g, g, 6, s)

            def pe_step(g, s):
                def has(p, n):
                    return not isinstance(p, int) or 0 <= p < n
                if has(g, NPAIR):
                    keys_values(g, s)
                if has(g - 3, NPAIR):
                    turn_keys(g - 3, 1 - s)
                if has(g - 6, NPAIR):
                    first_scores(g - 6, s)

            pe.wait_ge(sem("wprep_done"), 1)
            for g in range(7):
                pe_step(g, g % 2)
                if g == 0:
                    latent_queries()
                if g == 3:
                    turn_q()
                if g == 5:
                    pe.wait_ge(sem("qT_ready"), 1)
                    pe.wait_ge(sem("mrow_in"), 16 * HEADS)
            with pe.Fori(0, 4) as it:
                for k in range(2):
                    pe_step(2 * it + 7 + k, (7 + k) % 2)
            pe_step(NCP - 1, 1)
            last = NPAIR - 1
            keys_values(last, 0)
            for g in range(last - 3, last + 1):
                turn_keys(g, g % 2)
                first_scores(g - 3, (g - 3) % 2)
            for g in range(last - 2, last + 1):
                first_scores(g, g % 2)

            def scores(h, i, n, s):
                if not (isinstance(n, int) and n < 2):
                    pe.wait_ge(sem("exp_done"), n - 1)
                for t in range(2):
                    at = bass.ds(i * PAIR + t * P, P)
                    pe.matmul(bank[s][:, t * T:(t + 1) * T], keyA[:, h, at], qT_exp[:, h], start=True, stop=False)
                    ins = pe.matmul(bank[s][:, t * T:(t + 1) * T], keyB[:, h, at], qT_hh[:, h],
                                    start=False, stop=True)
                ins.then_inc(sem("s_done"), 1)

            def weighted_values(h, i, n, s, first=False, last=False):
                for t in range(2):
                    pe.wait_ge(sem(f"plo{t}_done"), n + 1)
                    values = val16[:, 2 * i + t, h]
                    for a in range(2):
                        at = slice(t * T + a * P, t * T + (a + 1) * P)
                        pe.matmul(bank[4 + h % 2][:, a * VD:a * VD + VL + DH], p_hi[:, s, at], values[:, 0:VL + DH],
                                  start=first and t == 0 and a == 0, stop=last and t == 1, skip_group_check=True)
                        ins = pe.matmul(bank[4 + h % 2][:, a * VD:a * VD + VL], p_lo[:, s, at], values[:, 0:VL],
                                        start=False, stop=last and t == 1, skip_group_check=True)
                ins.then_inc(sem("pv_done"), 1)

            def head_tail(h, groups):
                for i in groups:
                    weighted_values(h, i, h * NPAIR + i, (h + i) % P_SLOTS, last=i == NPAIR - 1)

            def turn_queries(h):
                pe.wait_ge(sem("shift_done"), h + 1)
                for a in range(2):
                    ins = pe.transpose(bank[6].bitcast(F16)[0:KR, a * P:(a + 1) * P], q_exp[:, a, h, :], id16[:])
                ins.then_inc(sem("qe_mm"), 1)

            pe.wait_ge(sem("vlo_done"), NPAIR)
            turn_queries(0)
            for h in range(HEADS):
                base = h * NPAIR
                if h + 1 < HEADS:
                    max_scores(h + 1, 0, base + NPAIR, 2, (base + 1) % 2)
                pe.wait_ge(sem("qe_done"), h + 1)

                def group(i):
                    n = base + i
                    scores(h, i, n, n % 2)
                    ahead = h + 1 < HEADS and i + 1 < NPAIR
                    early = i >= NPAIR - 3
                    if ahead and early:
                        max_scores(h + 1, i + 1, n + NPAIR + 1, 2, n % 2)
                    if i >= LAG:
                        if i == LAG and h >= 2:
                            pe.wait_ge(sem("o_done"), 2 * (h - 1))
                        weighted_values(h, i - LAG, n - LAG, (n - LAG) % P_SLOTS, first=i == LAG)
                    if ahead and not early:
                        max_scores(h + 1, i + 1, n + NPAIR + 1, 2, n % 2)

                for i in range(NPAIR):
                    group(i)
                    if h and i == 0:
                        head_tail(h - 1, [NPAIR - 1])
                if h + 1 < HEADS:
                    turn_queries(h + 1)
                head_tail(h, range(NPAIR - LAG, NPAIR - 1))
            head_tail(HEADS - 1, [NPAIR - 1])

            turn((bank[6], bank[7]), o_sb, "o_done", 2 * HEADS - 2, "oT_mm")
            moved("oT*_done", 1)
            pe.wait_ge(sem("delta_weights_in"), 80)
            by_token((bank[0], bank[1]), oT, wo_at, "att_mm")

            keep_clock(22, bank[4])
            turn((bank[2], bank[3]), nrm, "nrm_done", 0, "nT_mm")
            moved("nT*_done", 1)
            by_channel((bank[4], bank[5]), nT, gw[:, :, C:2 * C], "kT_mm")
            by_channel((bank[6], bank[7]), nT, gw[:, :, 0:C], "q_mm", (0,))
            moved("kT*_done", 1)
            product(bank[0][:, 0:T], [kT[:, k, 0:P] for k in range(2)], [kT[:, k] for k in range(2)]
                    ).then_inc(sem("gram_mm"), 1)
            product(bank[1][:, 0:P], [kT[:, k, P:T] for k in range(2)], [kT[:, k, P:T] for k in range(2)]
                    ).then_inc(sem("gram_mm"), 1)
            by_channel((bank[6], bank[7]), nT, gw[:, :, 0:C], "q_mm", (1,))
            by_token((bank[2], bank[3]), nT, gw[:, :, 2 * C:3 * C], "v_mm", (0,))
            for b in range(2):
                pe.wait_ge(sem("t1_done"), b + 1)
                pe.wait_ge(sem("qT_done"), b + 1)
                pe.transpose(bank[6 + b][:, 0:P], T1[:, b], ident).then_inc(sem("xtt_mm"), 1)

            def between(n):
                if n == 0:
                    by_token((bank[2], bank[3]), nT, gw[:, :, 2 * C:3 * C], "v_mm", (1,))
                if n == 1:
                    pe.wait_ge(sem("tables_in"), 80)
                    pe.wait_ge(sem("vd_ready"), 1)
                    for a in range(2):
                        ins = product(bank[2][:, C + a:C + a + 1], [nT[:, k, a * P:(a + 1) * P] for k in range(2)],
                                      [lrw_sb[:, k:k + 1] for k in range(2)])
                    ins.then_inc(sem("lr_mm"), 1)
                if n in (2, 3):
                    pe.wait_ge(sem("vd_ready"), 2) if n == 2 else pe.wait_ge(sem("lr_ready"), 1)
                    by_channel((bank[3], bank[2]), qT, kT, "score_mm", (n - 2,))

            for n in range(NLEV - 1):
                pe.wait_ge(sem("bT_ready"), n + 1)
                for b in range(2):
                    pe.wait_ge(sem("x_next"), 2 * n + b + 1)
                    pe.matmul(bank[b][:, 0:P], bT[:, n, b], X[:, b], start=True, stop=True
                              ).then_inc(sem("t1_mm"), 1)
                between(n)
                for b in range(2):
                    pe.wait_ge(sem("t1_done"), 2 * n + b + 3)
                    pe.wait_ge(sem("xt_next"), 2 * n + b + 1)
                    if n < NLEV - 2:
                        pe.matmul(bank[4 + b][:, 0:P], XT[:, b], T1[:, b], start=True, stop=True
                                  ).then_inc(sem("xx_mm"), 1)
                for b in range(2):
                    pe.matmul(bank[6 + b][:, 0:P], T1[:, b], XT[:, b], start=True, stop=True
                              ).then_inc(sem("xtt_mm"), 1)
            pe.wait_ge(sem("xt_next"), 2 * NLEV - 1)
            pe.wait_ge(sem("vs_ready"), 2)
            pe.matmul(bank[4][:, 0:C], XT[:, 0], vs[:, 0], start=True, stop=True).then_inc(sem("u1_mm"), 1)
            pe.wait_ge(sem("u_done"), 1)
            pe.matmul(bank[5][:, 0:C], gram[:, 1], u[:, 0], start=True, stop=True).then_inc(sem("u01_mm"), 1)
            pe.wait_ge(sem("score_done"), 2)
            pe.wait_ge(sem("xt_next"), 2 * NLEV)
            for a in range(2):
                pe.matmul(bank[6 + a][:, 0:T], u[:, 0, a * P:(a + 1) * P], score[:, 0], start=True, stop=False,
                          skip_group_check=True)
            pe.wait_ge(sem("vs_ready"), 3)
            pe.matmul(bank[0][:, 0:C], XT[:, 1], vs[:, 1], start=True, stop=True).then_inc(sem("u2_mm"), 1)
            pe.wait_ge(sem("u_done"), 2)
            for a in range(2):
                ins = pe.matmul(bank[6 + a][:, 0:T], u[:, 1, a * P:(a + 1) * P], score[:, 1],
                                start=False, stop=True, skip_group_check=True)
            ins.then_inc(sem("yT_mm"), 1)
            moved("yT*_done", 1)
            by_token((bank[0], bank[1]), yT, ow, "delta_mm")
            keep_clock(22, bank[4])
            turn((bank[2], bank[3]), nrm, "nrm_done", 2, "nT_mm")
            moved("nT*_done", 2)
            by_channel((bank[4], bank[5]), nT, w1_sb, "hm_mm")
            moved("hm*_done", 1)
            by_token((bank[6], bank[7]), hm, w2_sb, "mlp_mm")

            keep_clock(22, bank[2])
            turn((bank[0], bank[1]), tok, "tok_done", 0, "nT_mm")
            moved("nT*_done", 3)
            by_token(bank[2], tokT, gt_sb[:], "logit_mm")
            keep_clock(10, bank[3])
            pe.wait_ge(sem("hot_done"), 1)
            pe.wait_ge(sem("tri16_done"), 1)
            product(bank[6][:, 0:E], [tri16[:]], [hot[:, 0]])
            product(bank[6][:, E:2 * E], [ones16[:], tri16[:]], [hot[:, 0], hot[:, 1]])
            product(bank[6][:, 2 * E:3 * E], [ones16[:], ones16[:]], [hot[:, 0], hot[:, 1]]).then_inc(sem("rank_mm"), 1)
            keep_clock(16, bank[3])
            pe.wait_ge(sem("tok_lo_done"), 1)
            for m, (at, n) in enumerate(XS_CUTS):
                pe.wait_ge(sem("sel_done"), 2 * m + 2)
                for c in range(2):
                    product(bank[2 * m + c][:, 0:n],
                            [part[:, a, c * P:(c + 1) * P] for part in (tok_hi, tok_lo) for a in range(2)],
                            [sel[:, a, at:at + n] for a in range(2)] * 2).then_inc(sem("xs_mm"), 1)

            def turn_sel(q):
                n = min(2, NW - 2 * q)
                if q >= 2:
                    pe.wait_ge(sem("selT_done"), q - 1)
                for j in range(n):
                    for a in range(2):
                        ins = pe.transpose(bank[6 + q % 2].bitcast(F16)[:, j * T + a * P:j * T + (a + 1) * P],
                                           sel[:, a, (2 * q + j) * P:(2 * q + j + 1) * P], id16[:])
                ins.then_inc(sem("selT_mm"), 1)

            pe.wait_ge(sem("extra_ids"), 1)
            turn_sel(0)
            turn_sel(1)

            def first_product(n):
                e = n if n < E else 0
                pe.wait_ge(wi_sem(e), wi_loaded(e) if n < E else 32)
                if n == 0:
                    pe.wait_ge(sem("xs0_done"), len(XS_CUTS))
                    pe.wait_ge(sem("xs1_done"), len(XS_CUTS))
                if n >= 2:
                    pe.wait_ge(sem("gelu_done"), 2 * (n - 1))
                for i in range(IT):
                    b = bank[2 * (n % 2) + i // (IT // 2)]
                    at = i % (IT // 2) * W
                    ins = product(b[:, at:at + W], [wi_of(e)[:, k, i * P:(i + 1) * P] for k in range(2)],
                                  [xs[:, k, n * W:(n + 1) * W] for k in range(2)])
                    if i % (IT // 2) == IT // 2 - 1:
                        ins.then_inc(sem("h_mm"), 1)

            def second_product(n):
                e = n if n < E else 0
                pe.wait_ge(sem(f"wo_in{e // 2}"), 32 if n < E else 48)
                pe.wait_ge(sem("gelu_done"), 2 * n + 2)
                if n >= 2:
                    pe.wait_ge(sem("ys_done"), n - 1)
                product(bank[4 + n % 2][:, 0:C], [hT[:, n % 2, i] for i in range(IT)],
                        [wo_of(e)[:, i] for i in range(IT)]).then_inc(sem("window_mm"), 1)

            def back(n):
                pe.wait_ge(sem("ys_done"), n + 1)
                if n == 0:
                    pe.wait_ge(sem("selT_done"), (NW + 1) // 2)
                for a in range(2):
                    for ys in (ys_hi, ys_lo):
                        ins = pe.matmul(bank[6][:, a * C:(a + 1) * C], selT[:, n, a * P:(a + 1) * P], ys[:, n % YS],
                                        start=n == 0 and a == 0 and ys is ys_hi, stop=n == NW - 1 and ys is ys_lo,
                                        skip_group_check=True)
                ins.then_inc(sem("back_mm"), 1)

            first_product(0)
            for n in range(NW):
                if n + 1 < NW:
                    first_product(n + 1)
                second_product(n)
                if n + 2 <= NW // 2:
                    turn_sel(n + 2)
                if n >= NW // 2:
                    for m in range(0 if n == NW // 2 else n - 1, n):
                        back(m)
            back(NW - 1)


_OUTS = [((1, T, C), 'float32')]


def kernel(**inputs):
    import numpy as _np
    import concourse.bacc as _bacc
    from concourse import mybir as _mybir
    from concourse.bass_utils import run_bass_kernel_spmd as _run

    g = {k: _np.asarray(a) for k, a in inputs.items()}
    gb = g["L0_attn_gates_b"]
    vec = {"ln_l_g": g["L0_xattn_ln_l_g"], "ln_l_b": g["L0_xattn_ln_l_b"], "qn_g": g["L0_xattn_qn_g"],
           "kn_g": g["L0_xattn_kn_g"], "bo": g["L0_xattn_bo"], "dn_g": g["L0_attn_dn_g"], "dn_b": g["L0_attn_dn_b"],
           "gates_bv": gb[2 * C:3 * C], "lr_b": g["L0_attn_lr_b"],
           "out_b": g["L0_attn_out_b"], "mn_g": g["L0_attn_mn_g"], "mn_b": g["L0_attn_mn_b"],
           "b2": g["L0_attn_b2"], "ffn_g": g["L0_ffn_ln_gamma"], "ffn_b": g["L0_ffn_ln_beta"]}
    r, c = _np.arange(P)[:, None], _np.arange(P)[None, :]
    consts = _np.zeros((P, NCONST), _np.float32)
    levels = _np.zeros((P, (NLEV + 1) * P), _np.float32)
    for n in range(NLEV):
        s = 1 << n
        below = (r // (2 * s) == c // (2 * s)) & (r // s % 2 == 1) & (c // s % 2 == 0)
        levels[:, (1 + n) * P:(2 + n) * P] = below.T
        if n == 0:
            levels[:, 0:P] = below
    consts[:, C_ID:C_ID + P] = r == c
    consts[:, C_TRI:C_TRI + P] = r < c
    consts[:, C_IOTA:] = _np.arange(SLOTS)
    arrays_in = {
        "x": g["x"], "ctx": g["ctx_768"], "ctxT": g["ctx_768"][0].T, "mask": g["mask_BxS2_bk0"],
        "wkvT": g["L0_xattn_Wkv"].T, "wqT": g["L0_xattn_Wq"].T, "wlkvT": g["L0_xattn_Wlkv"].T,
        "woT": g["L0_xattn_Wo"].T, "gates": g["L0_attn_gates_w"], "lrw": g["L0_attn_lr_w"].reshape(2, P).T,
        "outw": g["L0_attn_out_w"], "w1": g["L0_attn_w1"], "w2": g["L0_attn_w2"],
        "gateT": g["L0_ffn_gate_weight"].T, "wi": g["L0_ffn_wi"], "wo": g["L0_ffn_wo"],
        "rows": _np.concatenate([vec[k] for k in ROW]),
        "cols": _np.concatenate([gb[0:C].reshape(2, P), g["L0_attn_b1"].reshape(2, P), gb[C:2 * C].reshape(2, P)]).T,
        "cols_ctx": _np.concatenate([g["L0_xattn_ln_x_g"].reshape(2, CT), g["L0_xattn_ln_x_b"].reshape(2, CT)]).T,
        "consts": consts, "levels": levels, "key_ones": _np.ones((1, HEADS, NKEY), _np.float16),
    }
    nc = _bacc.Bacc("TRN2", target_bir_lowering=False, num_devices=1)
    arrays, args = {}, []
    for name, a in arrays_in.items():
        a = _np.ascontiguousarray(a)
        arrays[f"in_{name}_dram"] = a
        args.append(nc.dram_tensor(f"in_{name}_dram", a.shape, _mybir.dt.from_np(a.dtype), kind="ExternalInput").ap())
    for i, (shape, dtype) in enumerate(_OUTS):
        dt = _mybir.dt.from_np(_np.dtype(dtype))
        args.append(nc.dram_tensor(f"out_{i}_dram", shape, dt, kind="ExternalOutput").ap())
    perceiver_layer(nc, *args)
    r = _run(nc, [arrays], core_ids=[0])
    return r.results[0]["out_0_dram"]
```
